# Optimizing a Trainium2 kernel written in Bass

```python
import numpy as np
import jax
import jax.numpy as jnp

def _softmax(x, axis=-1):
    return jax.nn.softmax(x, axis=axis)

def _gelu(x):
    return jax.nn.gelu(x, approximate=True)

def _silu(x):
    return jax.nn.silu(x)

def _sigmoid(x):
    return jax.nn.sigmoid(x)

def _layernorm(x, axis=-1, eps=1e-05):
    m = jnp.mean(x, axis=axis, keepdims=True)
    v = jnp.var(x, axis=axis, keepdims=True)
    return (x - m) / jnp.sqrt(v + eps)

def _scatter_add(tgt, idx, src, axis=0):
    return tgt.at[idx].add(src)

def _segment_sum(src, seg, n):
    return jax.ops.segment_sum(src, seg, n)
kernel_name = 'mk_gnn_resnorm_d4_gnn_r32_0c809e'

def setup_inputs(seed: int=0):
    np.random.seed(seed)
    _w = jnp.asarray

    def _rec_inputs():
        import jax
        import jax.numpy as jnp
        _gk = jax.random.key(seed)
        x = -0.000202 + 1 * jax.random.normal(jax.random.fold_in(_gk, 1), (50000, 128), jnp.float32)
        src = jax.random.randint(jax.random.fold_in(_gk, 2), (25000,), 0, 50000, jnp.int32)
        dst = jnp.minimum((50000 * jax.random.uniform(jax.random.fold_in(_gk, 3), (25000,)) ** 2.0).astype(jnp.int32), 49999)
        _o = jnp.argsort(dst, stable=True)
        src = src[_o]
        dst = dst[_o]
        edge_attr_3 = -0.000451519 + 1.00018 * jax.random.normal(jax.random.fold_in(_gk, 12), (25000, 3), jnp.float32)
        edge_attr_64 = 0.000167468 + 1.0002 * jax.random.normal(jax.random.fold_in(_gk, 13), (25000, 64), jnp.float32)
        edge_weight = jax.random.uniform(jax.random.fold_in(_gk, 15), (25000,), jnp.float32, 0.0, 0.999998)
        return (x, src, dst, edge_attr_3, edge_attr_64, edge_weight)
    x, src, dst, edge_attr_3, edge_attr_64, edge_weight = _rec_inputs()

    def _L0_gnn_setup():
        import jax, jax.numpy as jnp
        import numpy as np
        N_NODES = 50000
        N_EDGES = 25000
        D_IN = 128
        D_OUT = 128
        LN_EPS = 1e-05
        key = jax.random.key(seed)
        k1, k2, k3, k4, k5 = jax.random.split(key, 5)
        feature = jax.random.normal(k1, (N_NODES, D_IN), dtype=jnp.float32)
        src = jax.random.randint(k2, (N_EDGES,), 0, N_NODES, dtype=jnp.int32)
        dst = jax.random.randint(k3, (N_EDGES,), 0, N_NODES, dtype=jnp.int32)
        W = jax.random.normal(k4, (D_OUT, D_IN), dtype=jnp.float32) * (1.0 / np.sqrt(D_IN))
        b = jax.random.normal(k5, (D_OUT,), dtype=jnp.float32) * 0.01
        gamma = jnp.ones((D_OUT,), dtype=jnp.float32)
        beta = jnp.zeros((D_OUT,), dtype=jnp.float32)
        return {'feature': feature, 'src': src, 'dst': dst, 'W': W, 'b': b, 'gamma': gamma, 'beta': beta}
    _L0_gnn_all = _L0_gnn_setup()
    _L0_gnn_in = {k: v for k, v in _L0_gnn_all.items() if k in ('W', 'b', 'gamma', 'beta')}
    del _L0_gnn_all

    def _L1_gnn_setup():
        import jax, jax.numpy as jnp
        import numpy as np
        N = 50000
        E = 25000
        MUL = 32
        NB = 8
        R_MAX = 1.0
        AVG = 16.0
        SQ3 = 3.0 ** 0.5

        def _radial_embedding(r):
            x = jnp.clip(r / R_MAX, 0.0, 1.0)
            centers = jnp.arange(NB, dtype=jnp.float32) / (NB - 1)
            sigma = 1.0 / (NB - 1)
            emb = jnp.exp(-0.5 * ((x[:, None] - centers[None, :]) / sigma) ** 2)
            emb = emb * NB ** 0.5 * (r <= R_MAX).astype(jnp.float32)[:, None]
            return emb
        key = jax.random.key(seed)
        k = jax.random.split(key, 12)
        inp = {'node_feats': jax.random.normal(k[0], (N, 4 * MUL), dtype=jnp.float32), 'edge_vec': jax.random.normal(k[1], (E, 3), dtype=jnp.float32), 'edge_length': jax.random.uniform(k[2], (E,), dtype=jnp.float32), 'senders': jax.random.randint(k[3], (E,), 0, N, dtype=jnp.int32), 'receivers': jax.random.randint(k[4], (E,), 0, N, dtype=jnp.int32), 'num_nodes': N, 'W_up0': jax.random.normal(k[5], (MUL, MUL), dtype=jnp.float32), 'W_up1': jax.random.normal(k[6], (MUL, MUL), dtype=jnp.float32), 'mlp_w0': jax.random.normal(k[7], (NB, 64), dtype=jnp.float32) / NB ** 0.5, 'mlp_b0': jnp.zeros((64,), dtype=jnp.float32), 'mlp_w1': jax.random.normal(k[8], (64, 64), dtype=jnp.float32) / 8.0, 'mlp_b1': jnp.zeros((64,), dtype=jnp.float32), 'mlp_w2': jax.random.normal(k[9], (64, 4 * MUL), dtype=jnp.float32) / 8.0, 'mlp_b2': jnp.zeros((4 * MUL,), dtype=jnp.float32), 'W_out0': jax.random.normal(k[10], (2 * MUL, MUL), dtype=jnp.float32), 'W_out1': jax.random.normal(k[11], (2 * MUL, MUL), dtype=jnp.float32)}
        return inp
    _L1_gnn_all = _L1_gnn_setup()
    _L1_gnn_in = {k: v for k, v in _L1_gnn_all.items() if k in ('W_up0', 'W_up1', 'mlp_w0', 'mlp_b0', 'mlp_w1', 'mlp_b1', 'mlp_w2', 'mlp_b2', 'W_out0', 'W_out1')}
    del _L1_gnn_all

    def _L2_gnn_setup():
        import jax, jax.numpy as jnp
        import numpy as np
        N_NODES = 50000
        N_EDGES = 18750
        D = 128
        LN_EPS = 1e-05

        def _layer_norm(f, gamma, beta):
            mu = jnp.mean(f, axis=-1, keepdims=True)
            var = jnp.mean(jnp.square(f - mu), axis=-1, keepdims=True)
            return (f - mu) * jax.lax.rsqrt(var + LN_EPS) * gamma + beta
        key = jax.random.key(seed)
        k1, k2, k3, k4 = jax.random.split(key, 4)
        x = jax.random.normal(k1, (N_NODES, D), dtype=jnp.float32)
        edge_index = jax.random.randint(k2, (2, N_EDGES), 0, N_NODES, dtype=jnp.int64)
        scale = 1.0 / np.sqrt(D)
        W_l = jax.random.normal(k3, (D, D), dtype=jnp.float32) * scale
        W_r = jax.random.normal(k4, (D, D), dtype=jnp.float32) * scale
        b_l = jnp.zeros((D,), dtype=jnp.float32)
        gamma = jnp.ones((D,), dtype=jnp.float32)
        beta = jnp.zeros((D,), dtype=jnp.float32)
        return {'x': x, 'edge_index': edge_index, 'W_l': W_l, 'b_l': b_l, 'W_r': W_r, 'gamma': gamma, 'beta': beta}
    _L2_gnn_all = _L2_gnn_setup()
    _L2_gnn_in = {k: v for k, v in _L2_gnn_all.items() if k in ('W_l', 'b_l', 'W_r', 'gamma', 'beta')}
    del _L2_gnn_all

    def _L3_gnn_setup():
        import jax, jax.numpy as jnp
        import numpy as np
        N = 1250
        E = 20000
        ND = 128
        ED = 64
        LN_EPS = 1e-05
        key = jax.random.key(seed)
        ks = jax.random.split(key, 16)
        s = lambda k, shape, fan_in: jax.random.normal(k, shape, dtype=jnp.float32) * (1.0 / np.sqrt(fan_in))
        return {'node_features': jax.random.normal(ks[0], (N, ND), dtype=jnp.float32), 'edge_indices': jax.random.randint(ks[1], (2, E), 0, N, dtype=jnp.int32), 'edge_features': jax.random.normal(ks[2], (E, ED), dtype=jnp.float32), 'W1': s(ks[3], (2 * ND + ED, ND), 2 * ND + ED), 'b1': jnp.zeros((ND,), jnp.float32), 'ln_g': jnp.ones((ND,), jnp.float32), 'ln_b': jnp.zeros((ND,), jnp.float32), 'W2': s(ks[4], (ND, ND), ND), 'b2': jnp.zeros((ND,), jnp.float32), 'gate_w': s(ks[5], (ED, 1), ED), 'gate_b': jnp.zeros((1,), jnp.float32), 'W_ih': s(ks[6], (3 * ND, ND), ND), 'b_ih': jnp.zeros((3 * ND,), jnp.float32), 'W_hh': s(ks[7], (3 * ND, ND), ND), 'b_hh': jnp.zeros((3 * ND,), jnp.float32)}
    _L3_gnn_all = _L3_gnn_setup()
    _L3_gnn_in = {k: v for k, v in _L3_gnn_all.items() if k in ('W1', 'b1', 'ln_g', 'ln_b', 'W2', 'b2', 'gate_w', 'gate_b', 'W_ih', 'b_ih', 'W_hh', 'b_hh')}
    del _L3_gnn_all
    return {'x': x, 'src': src, 'dst': dst, 'edge_attr_3': edge_attr_3, 'edge_attr_64': edge_attr_64, 'edge_weight': edge_weight, 'L0_gnn_W': _L0_gnn_in['W'], 'L0_gnn_b': _L0_gnn_in['b'], 'L0_gnn_gamma': _L0_gnn_in['gamma'], 'L0_gnn_beta': _L0_gnn_in['beta'], 'L1_gnn_W_up0': _L1_gnn_in['W_up0'], 'L1_gnn_W_up1': _L1_gnn_in['W_up1'], 'L1_gnn_mlp_w0': _L1_gnn_in['mlp_w0'], 'L1_gnn_mlp_b0': _L1_gnn_in['mlp_b0'], 'L1_gnn_mlp_w1': _L1_gnn_in['mlp_w1'], 'L1_gnn_mlp_b1': _L1_gnn_in['mlp_b1'], 'L1_gnn_mlp_w2': _L1_gnn_in['mlp_w2'], 'L1_gnn_mlp_b2': _L1_gnn_in['mlp_b2'], 'L1_gnn_W_out0': _L1_gnn_in['W_out0'], 'L1_gnn_W_out1': _L1_gnn_in['W_out1'], 'L2_gnn_W_l': _L2_gnn_in['W_l'], 'L2_gnn_b_l': _L2_gnn_in['b_l'], 'L2_gnn_W_r': _L2_gnn_in['W_r'], 'L2_gnn_gamma': _L2_gnn_in['gamma'], 'L2_gnn_beta': _L2_gnn_in['beta'], 'L3_gnn_W1': _L3_gnn_in['W1'], 'L3_gnn_b1': _L3_gnn_in['b1'], 'L3_gnn_ln_g': _L3_gnn_in['ln_g'], 'L3_gnn_ln_b': _L3_gnn_in['ln_b'], 'L3_gnn_W2': _L3_gnn_in['W2'], 'L3_gnn_b2': _L3_gnn_in['b2'], 'L3_gnn_gate_w': _L3_gnn_in['gate_w'], 'L3_gnn_gate_b': _L3_gnn_in['gate_b'], 'L3_gnn_W_ih': _L3_gnn_in['W_ih'], 'L3_gnn_b_ih': _L3_gnn_in['b_ih'], 'L3_gnn_W_hh': _L3_gnn_in['W_hh'], 'L3_gnn_b_hh': _L3_gnn_in['b_hh']}

def reference(x, src, dst, edge_attr_3, edge_attr_64, edge_weight, L0_gnn_W, L0_gnn_b, L0_gnn_gamma, L0_gnn_beta, L1_gnn_W_up0, L1_gnn_W_up1, L1_gnn_mlp_w0, L1_gnn_mlp_b0, L1_gnn_mlp_w1, L1_gnn_mlp_b1, L1_gnn_mlp_w2, L1_gnn_mlp_b2, L1_gnn_W_out0, L1_gnn_W_out1, L2_gnn_W_l, L2_gnn_b_l, L2_gnn_W_r, L2_gnn_gamma, L2_gnn_beta, L3_gnn_W1, L3_gnn_b1, L3_gnn_ln_g, L3_gnn_ln_b, L3_gnn_W2, L3_gnn_b2, L3_gnn_gate_w, L3_gnn_gate_b, L3_gnn_W_ih, L3_gnn_b_ih, L3_gnn_W_hh, L3_gnn_b_hh):
    import jax
    import jax.numpy as jnp

    def _L0_gnn_ref(feature, src, dst, W, b, gamma, beta):
        import jax, jax.numpy as jnp
        import numpy as np
        N_NODES = 50000
        N_EDGES = 25000
        D_IN = 128
        D_OUT = 128
        LN_EPS = 1e-05
        n_nodes = feature.shape[0]
        agg_h = jax.ops.segment_sum(feature[src], dst, num_segments=n_nodes)
        h = jnp.einsum('nd,od->no', agg_h, W) + b
        mu = jnp.mean(h, axis=-1, keepdims=True)
        var = jnp.mean(jnp.square(h - mu), axis=-1, keepdims=True)
        h = (h - mu) * jax.lax.rsqrt(var + LN_EPS)
        return h * gamma + beta

    def _L1_gnn_ref(node_feats, edge_vec, edge_length, senders, receivers, num_nodes, W_up0, W_up1, mlp_w0, mlp_b0, mlp_w1, mlp_b1, mlp_w2, mlp_b2, W_out0, W_out1):
        import jax, jax.numpy as jnp
        import numpy as np
        N = 50000
        E = 25000
        MUL = 32
        NB = 8
        R_MAX = 1.0
        AVG = 16.0
        SQ3 = 3.0 ** 0.5

        def _radial_embedding(r):
            x = jnp.clip(r / R_MAX, 0.0, 1.0)
            centers = jnp.arange(NB, dtype=jnp.float32) / (NB - 1)
            sigma = 1.0 / (NB - 1)
            emb = jnp.exp(-0.5 * ((x[:, None] - centers[None, :]) / sigma) ** 2)
            emb = emb * NB ** 0.5 * (r <= R_MAX).astype(jnp.float32)[:, None]
            return emb
        f32 = jnp.float32
        rhat = edge_vec / (jnp.linalg.norm(edge_vec, axis=-1, keepdims=True) + 1e-12)
        Y1 = SQ3 * rhat
        emb = _radial_embedding(edge_length)
        h = jax.nn.silu(emb @ mlp_w0 + mlp_b0)
        h = jax.nn.silu(h @ mlp_w1 + mlp_b1)
        w = (h @ mlp_w2 + mlp_b2).reshape(-1, 4, MUL)
        s = node_feats[:, :MUL]
        v = node_feats[:, MUL:].reshape(-1, MUL, 3)
        xs = s @ W_up0 / f32(MUL) ** 0.5
        xv = jnp.einsum('nmc,mk->nkc', v, W_up1) / f32(MUL) ** 0.5
        ss = xs[senders]
        vv = xv[senders]
        m0 = w[:, 0] * ss
        m1 = w[:, 1][:, :, None] * ss[:, :, None] * Y1[:, None, :]
        m2 = w[:, 2][:, :, None] * vv
        m3 = w[:, 3] * (jnp.einsum('emc,ec->em', vv, Y1) / SQ3)
        mid_s = jnp.concatenate([m0, m3], axis=1)
        mid_v = jnp.concatenate([m1, m2], axis=1)
        msg_s = jax.ops.segment_sum(mid_s, receivers, num_segments=num_nodes)
        msg_v = jax.ops.segment_sum(mid_v, receivers, num_segments=num_nodes)
        out_s = msg_s @ W_out0 / f32(2 * MUL) ** 0.5
        out_v = jnp.einsum('nmc,mk->nkc', msg_v, W_out1) / f32(2 * MUL) ** 0.5
        out = jnp.concatenate([out_s, out_v.reshape(-1, 3 * MUL)], axis=1)
        return out / max(AVG, 1e-08)

    def _L2_gnn_ref(x, edge_index, W_l, b_l, W_r, gamma, beta):
        import jax, jax.numpy as jnp
        import numpy as np
        N_NODES = 50000
        N_EDGES = 18750
        D = 128
        LN_EPS = 1e-05

        def _layer_norm(f, gamma, beta):
            mu = jnp.mean(f, axis=-1, keepdims=True)
            var = jnp.mean(jnp.square(f - mu), axis=-1, keepdims=True)
            return (f - mu) * jax.lax.rsqrt(var + LN_EPS) * gamma + beta
        n = x.shape[0]
        src, dst = (edge_index[0], edge_index[1])
        agg = jax.ops.segment_sum(x[src], dst, num_segments=n)
        cnt = jax.ops.segment_sum(jnp.ones_like(src, dtype=x.dtype), dst, num_segments=n)
        mean = agg / jnp.maximum(cnt, 1.0)[:, None]
        f = mean @ W_l + b_l + x @ W_r
        f = jax.nn.gelu(f, approximate=False)
        f = _layer_norm(f, gamma, beta)
        return f + x

    def _L3_gnn_ref(node_features, edge_indices, edge_features, W1, b1, ln_g, ln_b, W2, b2, gate_w, gate_b, W_ih, b_ih, W_hh, b_hh):
        import jax, jax.numpy as jnp
        import numpy as np
        N = 1250
        E = 20000
        ND = 128
        ED = 64
        LN_EPS = 1e-05
        src, dst = (edge_indices[0], edge_indices[1])
        edge_inputs = jnp.concatenate([node_features[src], node_features[dst], edge_features], axis=1)
        h = edge_inputs @ W1 + b1
        mu = jnp.mean(h, axis=-1, keepdims=True)
        var = jnp.var(h, axis=-1, keepdims=True)
        h = (h - mu) * jax.lax.rsqrt(var + LN_EPS) * ln_g + ln_b
        h = jax.nn.relu(h)
        messages = h @ W2 + b2
        gate = jax.nn.sigmoid(edge_features @ gate_w + gate_b)
        messages = messages * gate
        agg = jax.ops.segment_sum(messages, dst, num_segments=node_features.shape[0])
        gi = agg @ W_ih.T + b_ih
        gh = node_features @ W_hh.T + b_hh
        i_r, i_z, i_n = jnp.split(gi, 3, axis=1)
        h_r, h_z, h_n = jnp.split(gh, 3, axis=1)
        r = jax.nn.sigmoid(i_r + h_r)
        z = jax.nn.sigmoid(i_z + h_z)
        n = jnp.tanh(i_n + r * h_n)
        return (1.0 - z) * n + z * node_features
    edge_index = jnp.stack([src, dst])
    x = _layernorm(x + _L0_gnn_ref(x, src, dst, L0_gnn_W, L0_gnn_b, L0_gnn_gamma, L0_gnn_beta), axis=-1)
    x = _layernorm(x + _L1_gnn_ref(x, edge_attr_3, edge_weight, src, dst, 50000, L1_gnn_W_up0, L1_gnn_W_up1, L1_gnn_mlp_w0, L1_gnn_mlp_b0, L1_gnn_mlp_w1, L1_gnn_mlp_b1, L1_gnn_mlp_w2, L1_gnn_mlp_b2, L1_gnn_W_out0, L1_gnn_W_out1), axis=-1)
    x = _layernorm(x + _L2_gnn_ref(x, edge_index, L2_gnn_W_l, L2_gnn_b_l, L2_gnn_W_r, L2_gnn_gamma, L2_gnn_beta), axis=-1)
    x = _layernorm(x + _L3_gnn_ref(x, edge_index, edge_attr_64, L3_gnn_W1, L3_gnn_b1, L3_gnn_ln_g, L3_gnn_ln_b, L3_gnn_W2, L3_gnn_b2, L3_gnn_gate_w, L3_gnn_gate_b, L3_gnn_W_ih, L3_gnn_b_ih, L3_gnn_W_hh, L3_gnn_b_hh), axis=-1)
    return x

_drawn_inputs = setup_inputs


def setup_inputs(seed=0):
    import zlib

    import numpy as np

    out = dict(_drawn_inputs(seed))
    spreads = {'L0_gnn_gamma': (1.0, 0.2),
     'L0_gnn_beta': (0.0, 0.1),
     'L1_gnn_mlp_b0': (0.0, 0.8),
     'L1_gnn_mlp_b1': (0.0, 0.8),
     'L1_gnn_mlp_b2': (0.0, 0.8),
     'L2_gnn_b_l': (0.0, 0.1),
     'L2_gnn_gamma': (1.0, 0.2),
     'L2_gnn_beta': (0.0, 0.1),
     'L3_gnn_b1': (0.0, 0.8),
     'L3_gnn_ln_g': (1.0, 0.6),
     'L3_gnn_ln_b': (0.0, 0.8),
     'L3_gnn_b2': (0.0, 0.58),
     'L3_gnn_b_ih': (0.0, 0.1),
     'L3_gnn_b_hh': (0.0, 0.377)}
    factors = {'edge_attr_3': 4.91,
     'edge_weight': 4.729,
     'L1_gnn_W_up0': 4.85,
     'L1_gnn_W_up1': 4.021,
     'L1_gnn_mlp_w0': 3.675,
     'L1_gnn_mlp_w1': 3.165,
     'L1_gnn_mlp_w2': 3.039,
     'L1_gnn_W_out0': 6.547,
     'L1_gnn_W_out1': 3.584}
    for name, (base, spread) in spreads.items():
        noise = np.random.default_rng([zlib.crc32(name.encode()), seed]).standard_normal(out[name].shape)
        drawn = base * np.exp(spread * noise) if base else spread * noise
        out[name] = jnp.asarray(drawn.astype(out[name].dtype))
    for name, factor in factors.items():
        out[name] = (out[name] * factor).astype(out[name].dtype)
    return out
```

```python
from contextlib import ExitStack

import concourse.bass as bass
from concourse import mybir

F32 = mybir.dt.float32
I32 = mybir.dt.int32
U32 = mybir.dt.uint32
ALU = mybir.AluOpType
ACT = mybir.ActivationFunctionType

P = 128
D = 128
G = 4
GP = G * P
U = 2
N_NODES = 50000
N_EDGES = 25000
NODE_GROUPS = -(-N_NODES // (GP * U)) * U
EDGE_GROUPS = -(-N_EDGES // (GP * U)) * U
NODES_PAD = NODE_GROUPS * GP
EDGES_PAD = EDGE_GROUPS * GP
MUL = 32
NB = 8
H1 = 64
ED = 64
R_MAX = 1.0
SIGMA = 1.0 / (NB - 1)
LN_EPS = 1e-5
SKIP = 1 << 20
LAST_ROW = NODES_PAD - 1
BN = 6
SCALED = 19
SUMS = (G, 2 * G, G, G)


class Signal:

    def __init__(self, sem, base):
        self.sem, self.base = sem, base

    def __call__(self, n):
        return self.sem, self.base + n


def build(nc, A, O):
    with ExitStack() as ctx:
        def sb(name, shape, dt=F32):
            return ctx.enter_context(nc.sbuf_tensor(name, shape, dt))

        pool_of_sems = {}

        def signal(name, total):
            sem, base = pool_of_sems.get(name) or (ctx.enter_context(nc.semaphore(name)), 0)
            pool_of_sems[name] = (sem, base + total)
            return Signal(sem, base)

        def signals(names, total):
            return {n.partition("*")[0]: signal(n.partition("*")[0], total * int(n.partition("*")[2] or 1))
                    for n in names.split()}

        def signals_by_buffer(names, total):
            return {n.partition("*")[0]: [signal(n.partition("*")[0] + str(u), total * int(n.partition("*")[2] or 1))
                                          for u in range(U)] for n in names.split()}

        def table(name, shape):
            return nc.dram_tensor(name, shape, F32, kind="Internal").ap()

        def pair(name, shape, dt=F32):
            return [sb(f"{name}{u}", shape, dt) for u in range(U)]

        x1_table, x2_table, x3_table = (table(f"x{k}_table", (NODES_PAD, D)) for k in (1, 2, 3))
        x1_slots, x2_slots = (table(f"x{k}_slots", (EDGE_GROUPS, P, G * D)) for k in (1, 2))
        radial_w = table("radial_w", (EDGE_GROUPS, P, G * D))
        gate_sums = table("gate_sums", (1, EDGES_PAD))
        x0_table, out = A["x"], O

        def node_rows(t, g):
            return t.rearrange("(g p j) d -> g p (j d)", p=P, j=G)[g]

        ident = sb("ident", [P, P])
        neg_half = sb("neg_half", [P, 8])
        rows = {}
        for name in ("b0", "gamma0", "beta0", "bl", "gamma2", "beta2", "ln_g3", "ln_b3"):
            rows[name] = sb(f"row_{name}", [P, D])
        half_beta2 = sb("half_beta2", [P, D])
        empty0 = sb("empty0", [P, D])
        w0t = sb("w0t", [D, D])
        wup = sb("wup", [D, D])
        wo = [sb(f"wo{h}", [P, D]) for h in range(2)]
        wl = sb("wl", [D, D])
        wr = sb("wr", [D, D])
        w1a = sb("w1a", [D, D])
        w1b = sb("w1b", [D, D])
        w1c = sb("w1c", [ED + 1, D])
        w2 = sb("w2", [D, D])
        b2row = sb("b2row", [1, D])
        wih = sb("wih", [D, 3 * D])
        whh = sb("whh", [D, 3 * D])
        bih = sb("bih", [D, 3])
        bhh = sb("bhh", [D, 3])
        brz = sb("brz", [D, 3])
        m0 = sb("m0", [NB, H1])
        m1 = sb("m1", [H1, H1])
        m2 = sb("m2", [H1 + 1, D])
        mb0 = sb("mb0", [H1, 1])
        mb1 = sb("mb1", [H1, 1])
        mb0h = sb("mb0h", [H1, 1])
        mb1h = sb("mb1h", [H1, 1])
        neg_centers = sb("neg_centers", [NB, 1])
        gate_w = sb("gate_w", [ED, 1])
        gate_b = sb("gate_b", [P, 1])
        gate_bh = sb("gate_bh", [P, 1])
        NT = EDGE_GROUPS * G
        rhat = sb("rhat", [P, NT, 3])
        count_inv = sb("count_inv", [P, NT])
        gates = sb("gates", [P, NT])
        empty_st = sb("empty_st", [P, BN])
        empty_mv = sb("empty_mv", [P, 2])
        empty_v = sb("empty_v", [P, 1])
        empty_r = sb("empty_r", [P, 1])
        always = sb("always", [P, 1])
        half = sb("half", [P, NT])
        sq_vec = sb("sq_vec", [P, NT, 3])
        norm = sb("norm", [P, NT])
        ones_row = sb("ones_row", [1, GP])

        bA = pair("bA", [P, G, D])
        bB = pair("bB", [P, G, D])
        bC = pair("bC", [P, G, D])
        bD = pair("bD", [P, G, D])
        bE = pair("bE", [P, G, D])
        bF = pair("bF", [P, G, D])
        bS = pair("bS", [P, G, D])
        bG = pair("bG", [P, G, D])
        bO = pair("bO", [P, G, D])
        bA2 = pair("bA2", [P, G, D])
        bE2 = pair("bE2", [P, G, D])
        xt = pair("xt", [P, G, D])
        xt3 = pair("xt3", [P, G, D])
        gr = pair("gr", [P, G, D])
        gn = pair("gn", [P, G, D])
        vr = pair("vr", [P, G, 3, MUL])
        rh = pair("rh", [P, G, 3])
        cinv = pair("cinv", [P, G])
        cnt_max = pair("cnt_max", [P, G])
        gate_t = pair("gate_t", [P, G])
        gate_row_t = pair("gate_row_t", [1, GP])
        sq_row = pair("sq_row", [NB, GP])
        exp_row = pair("exp_row", [NB, GP])
        emb_row = pair("emb_row", [NB, GP])
        hid_t = pair("hid_t", [H1, GP])
        hid_x = pair("hid_x", [H1, GP])
        hid0 = pair("hid0", [H1, GP])
        hid1 = pair("hid1", [H1 + 1, GP])
        mid = pair("mid", [P, G, 2 * D])
        sums = [pair(f"sums{h}_", [P, G, D]) for h in range(2)]
        carry_in = pair("carry_in", [P, D])
        stats = pair("stats", [P, G, BN])
        mv = pair("mv", [P, G, 2])
        vv = pair("vv", [P, 2, G])
        rstd = pair("rstd", [P, 2, G])
        idx = pair("idx", [P, 3 * G], I32)
        scat = pair("scat", [P, G], U32)
        is_mid = pair("is_mid", [P, G])
        dst_row = pair("dst_row", [P, GP + 1], I32)
        dst_col = pair("dst_col", [P, G])
        dst_before = pair("dst_before", [P, G])
        attr = pair("attr", [ED + 1, GP])
        r_row = pair("r_row", [NB, GP])
        e_row = pair("e_row", [NB, GP])
        mask_row = pair("mask_row", [NB, GP])
        same_row = pair("same_row", [1, GP])
        cnt_row = pair("cnt_row", [1, GP])
        gate_row = pair("gate_row", [1, GP])
        gsum_row = pair("gsum_row", [1, GP])
        rq = pair("rq", [P, G, MUL])

        ps = [[ctx.enter_context(nc.psum_tensor(f"ps{u}{k}", [P, G, D], F32)) for k in range(4)]
              for u in range(U)]


        CONST_TILES = [(t, A[n]) for t, n in (
            (w0t, "w0t"), (wup, "wup"), (wl, "wl"), (wr, "wr"), (w1c, "w1c"), (w2, "w2"), (b2row, "b2row"),
            (wih, "wih"), (whh, "whh"), (bih, "bih"), (bhh, "bhh"), (m0, "m0"), (m1, "m1"), (m2, "m2"),
            (mb0, "mb0"), (mb1, "mb1"), (gate_w, "gate_w"))]
        CONST_TILES += [(w1a, A["w1ab"][0:D, :]), (w1b, A["w1ab"][D:2 * D, :]), (wo[0], A["wo"][0:P, :]),
                        (wo[1], A["wo"][P:2 * P, :]), (gate_b, A["gate_b"].broadcast_to((P, 1)))]
        CONST_LOADS = len(rows) + len(CONST_TILES) + 1

        def flat(t):
            return t[:, :, :].rearrange("p j d -> p (j d)")

        def over_tiles(row):
            return row[:, :].unsqueeze(1).broadcast_to((P, G, D))

        def edges_of(g):
            return bass.ds(g * GP, GP)

        def tiles_of(g):
            return bass.ds(g * G, G)

        def tile_edges(j):
            return slice(j * P, (j + 1) * P)

        def reuse(eng, sem, g, each=1, stand=False):
            if isinstance(g, int) and g < U:
                return
            if stand:
                apart(eng, *sem(each * (g - (U - 1))))
            else:
                eng.wait_ge(*sem(each * (g - (U - 1))))

        def turns(eng, body, groups):
            body(0)
            with eng.Fori(1, groups // U) as turn:
                body(turn)

        def turns_ahead(eng, ahead, body, groups, before=lambda turn: None):
            ahead(0)
            before(0)
            ahead(1)
            body(0)
            with eng.Fori(1, groups // U - 1) as turn:
                before(turn)
                ahead(turn + 1)
                body(turn)
            before(groups // U - 1)
            body(groups // U - 1)

        def both(turn):
            return [(turn * U + u, u) for u in range(U)]

        A_TURNS = EDGE_GROUPS // U
        N_TURNS = NODE_GROUPS // U

        su = signals("go loaded consts ident scaled e_stats e_mv e_add e_rstd e_norm e_gamma empty sq ssum root "
                                       "root_eps rinv rhat", 0)
        E, N, T, NT_ = EDGE_GROUPS, NODE_GROUPS, A_TURNS, N_TURNS
        pa = signals("clipped squared exped masked emb h0_mm h0_tanh h0_lin h0 h1_mm h1_tanh h1_lin h1 w_mm "
                                       "w_copied logit_mm gate_tanh grow_tanh gate grow same cnt cnt_mm cnt_max cnt_inv gsum", E)
        pad = signals_by_buffer("r_in*16 attr_in*16 dst_in*16 w_st*16 gs_st*16", T)
        nd = signals("y0 st1 mv1 var1 rs1 x1 x2 tr xt f_mm f gelu st2 mv2 var2 rs2 fg xb y st3 mv3 var3 rs3 x3 "
                                       "tr3 xt3 r_mm z_mm n_mm r_tanh z_tanh hn rh n ya yb yt tr4 st4 mv4 var4 rs4 x", N)
        ndd = signals_by_buffer("x_in*16 x1_st*16 x2_st*16 x3_st*16 x_st*16", NT_)
        seg = [signals(f"dcol dbefore mid scat S agg carry*{SUMS[k]} sums*{SUMS[k]}", E) for k in range(4)]
        segd = [signals_by_buffer(f"idx_in*16 dst_in*16 src_in*{16 * G} scattered*{16 * G}", T) for k in range(4)]
        s0 = signals("h_mm f st1 mv1 var1 rs1 fg xb y st2 mv2 var2 rs2 x", E)
        s0d = signals_by_buffer(f"xd_in*{16 * G} x_st*16", T)
        s1 = signals("tr xt up rh m0b m1 vr vr01 vr012 m3 m2 h_mm y st1 mv1 var1 rs1 x", E)
        s1d = signals_by_buffer("w_in*16 x_in*16 x_st*16", T)
        s2 = signals("tr xt l_mm r_mm rb f gelu cinv st1 mv1 var1 rs1 fg xb y st2 mv2 var2 rs2 x", E)
        s2d = signals_by_buffer("x_in*16", T)
        s3 = signals("trs tr xt xt3 h_mm st1 mv1 var1 rs1 fg y relu gcol a2_mm a2 r_mm z_mm in_mm n_mm "
                                       "r_tanh z_tanh hn rh ni n ya yb yt tr4 st2 mv2 var2 rs2 x", E)
        s3d = signals_by_buffer(f"xd_in*{16 * G} attr_in*16 gs_in*16", T)

        def apart(eng, sem, value):
            value = value if isinstance(value, int) else eng.to_reg(value)
            eng.wait_ge(*su["go"](1))
            eng.wait_ge(sem, value)

        def all_of(eng, sem_pair, value):
            for q in sem_pair:
                eng.wait_ge(*q(value))

        def edge_phase_done(eng):
            all_of(eng, pad["w_st"], 16 * A_TURNS)
            all_of(eng, pad["gs_st"], 16 * A_TURNS)
            eng.wait_ge(*pa["gate"](EDGE_GROUPS))
            eng.wait_ge(*pa["cnt_inv"](EDGE_GROUPS))

        def node_phase_done(eng):
            for q in (ndd["x1_st"], ndd["x2_st"], ndd["x3_st"], ndd["x_st"]):
                all_of(eng, q, 16 * N_TURNS)

        def slots_done(eng, k):
            all_of(eng, segd[k]["scattered"], 16 * G * A_TURNS)
            if k == 0:
                all_of(eng, s0d["x_st"], 16 * A_TURNS)
            if k == 1:
                all_of(eng, s1d["x_st"], 16 * A_TURNS)

        block = ctx.enter_context(nc.Block())

        @block.sync
        def _(sp):
            for name in rows:
                sp.dma_start(rows[name][:, :], A[name].broadcast_to((P, D))).then_inc(su["loaded"].sem, 16)
            for t, source in CONST_TILES:
                sp.dma_start(t[:, :], source).then_inc(su["loaded"].sem, 16)
            sp.dma_start(rhat[:, :, :].rearrange("p t c -> p (t c)"), A["edge_vec"]).then_inc(su["loaded"].sem, 16)

            def edge_load(turn):
                for g, u in both(turn):
                    reuse(sp, pa["clipped"], g)
                    reuse(sp, pa["masked"], g)
                    sp.dma_start(r_row[u][:, :], A["edge_r"][:, edges_of(g)].broadcast_to((NB, GP))).then_inc(pad["r_in"][u].sem, 16)
                    reuse(sp, pa["logit_mm"], g)
                    sp.dma_start(attr[u][0:ED, :], A["attr_t"][0:ED, edges_of(g)]).then_inc(pad["attr_in"][u].sem, 16)
                    reuse(sp, pa["same"], g)
                    sp.dma_start(dst_row[u][0:1, :], A["dst_line"][:, bass.ds(g * GP, GP + 1)]).then_inc(pad["dst_in"][u].sem, 16)

            def edge_store(turn):
                for g, u in both(turn):
                    sp.wait_ge(*pa["w_copied"](g + 1))
                    sp.dma_start(radial_w[g], flat(bA[u])).then_inc(pad["w_st"][u].sem, 16)
                    sp.wait_ge(*pa["gsum"](g + 1))
                    sp.dma_start(gate_sums[:, edges_of(g)], gsum_row[u][0:1, :]).then_inc(pad["gs_st"][u].sem, 16)

            turns_ahead(sp, edge_load, edge_store, EDGE_GROUPS)
            edge_phase_done(sp)

            def node_load(turn):
                for g, u in both(turn):
                    reuse(sp, nd["y0"], g)
                    sp.dma_start(flat(bA[u]), node_rows(x0_table, g)).then_inc(ndd["x_in"][u].sem, 16)

            def node_store(turn):
                for g, u in both(turn):
                    sp.wait_ge(*nd["x1"](g + 1))
                    sp.dma_start(node_rows(x1_table, g), flat(bC[u])).then_inc(ndd["x1_st"][u].sem, 16)
                    sp.wait_ge(*nd["x2"](g + 1))
                    sp.dma_start(node_rows(x2_table, g), flat(bD[u])).then_inc(ndd["x2_st"][u].sem, 16)
                for g, u in both(turn):
                    sp.wait_ge(*nd["x3"](g + 1))
                    sp.dma_start(node_rows(x3_table, g), flat(bF[u])).then_inc(ndd["x3_st"][u].sem, 16)
                for g, u in both(turn):
                    sp.wait_ge(*nd["x"](g + 1))
                    sp.dma_start(node_rows(out, g), flat(bO[u])).then_inc(ndd["x_st"][u].sem, 16)

            turns_ahead(sp, node_load, node_store, NODE_GROUPS)
            node_phase_done(sp)

            def slot_load(k, turn):
                s, d = seg[k], segd[k]
                for g, u in both(turn):
                    reuse(sp, s["scat"], g, stand=True)
                    if not (isinstance(turn, int) and turn == 0):
                        apart(sp, *d["src_in"][u](16 * G * turn))
                        if k in (0, 3):
                            sp.wait_ge(*(s0d if k == 0 else s3d)["xd_in"][u](16 * G * turn))
                    sp.dma_start(idx[u][:, :], A["edge_idx"][g]).then_inc(d["idx_in"][u].sem, 16)
                for g, u in both(turn):
                    reuse(sp, s["sums"], g, SUMS[k], stand=True)
                    sp.dma_start(dst_row[u][:, :], A["dst_line"][:, bass.ds(g * GP, GP + 1)]
                                 .broadcast_to((P, GP + 1))).then_inc(d["dst_in"][u].sem, 16)

            def s0_store(turn):
                for g, u in both(turn):
                    sp.wait_ge(*s0["x"](g + 1))
                    sp.dma_start(x1_slots[g], flat(bF[u])).then_inc(s0d["x_st"][u].sem, 16)

            turns_ahead(sp, lambda turn: slot_load(0, turn), s0_store, EDGE_GROUPS)
            slots_done(sp, 0)

            def s1_load(turn):
                slot_load(1, turn)
                for g, u in both(turn):
                    reuse(sp, s1["m2"], g)
                    sp.dma_start(flat(bB[u]), radial_w[g]).then_inc(s1d["w_in"][u].sem, 16)
                    reuse(sp, s1["y"], g)
                    sp.dma_start(flat(bC[u]), x1_slots[g]).then_inc(s1d["x_in"][u].sem, 16)

            def s1_store(turn):
                for g, u in both(turn):
                    sp.wait_ge(*s1["x"](g + 1))
                    sp.dma_start(x2_slots[g], flat(bF[u])).then_inc(s1d["x_st"][u].sem, 16)

            turns_ahead(sp, s1_load, s1_store, EDGE_GROUPS)
            slots_done(sp, 1)

            def s2_load(turn):
                slot_load(2, turn)
                for g, u in both(turn):
                    reuse(sp, s2["tr"], g)
                    reuse(sp, s2["xb"], g)
                    sp.dma_start(flat(bC[u]), x2_slots[g]).then_inc(s2d["x_in"][u].sem, 16)

            turns(sp, s2_load, EDGE_GROUPS)
            slots_done(sp, 2)

            def s3_load(turn):
                slot_load(3, turn)
                for g, u in both(turn):
                    reuse(sp, s3["h_mm"], g)
                    sp.dma_start(attr[u][:, :], A["attr_t"][:, edges_of(g)]).then_inc(s3d["attr_in"][u].sem, 16)
                    reuse(sp, s3["a2_mm"], g)
                    sp.dma_start(gsum_row[u][0:1, :], gate_sums[:, edges_of(g)]).then_inc(s3d["gs_in"][u].sem, 16)

            turns(sp, s3_load, EDGE_GROUPS)
            slots_done(sp, 3)

        @block.gpsimd
        def _(pool):
            pool.memset(always[:, :], 0.0).then_inc(su["go"].sem, 1)
            pool.memset(neg_half[:, :], -0.5).then_inc(su["consts"].sem, 1)
            pool.memset(half[:, :], 0.5).then_inc(su["consts"].sem, 1)
            pool.memset(ident[:, :], 0.0).then_inc(su["ident"].sem, 1)
            pool.wait_ge(*su["ident"](1))
            pool.affine_select(out=ident[:, :], in_=ident[:, :], compare_op=ALU.not_equal, fill=1.0, base=0,
                               pattern=[[-1, P]], channel_multiplier=1).then_inc(su["ident"].sem, 1)
            pool.iota(neg_centers[:, :], pattern=[[0, 1]], base=0, channel_multiplier=-1,
                      allow_small_or_imprecise_dtypes=True).then_inc(su["consts"].sem, 1)
            pool.wait_ge(*su["consts"](2))
            pool.wait_ge(*su["e_add"](1))
            pool.tensor_tensor(empty_r[:, :], empty_v[:, :], neg_half[:, 0:1], ALU.pow).then_inc(su["e_rstd"].sem, 1)
            pool.wait_ge(*su["ssum"](1))
            pool.tensor_tensor(norm[:, :], norm[:, :], half[:, :], ALU.pow).then_inc(su["root"].sem, 1)

            def rsqrt(turn, mv_ready, var_ready, rs_ready, mult, add):
                for g, u in both(turn):
                    apart(pool, *mv_ready(g + 1))
                    pool.tensor_scalar(vv[u][:, 0, :], mv[u][:, :, 1], mult, add, ALU.mult, ALU.add).then_inc(var_ready.sem, 1)
                    pool.wait_ge(*var_ready(g + 1))
                    pool.tensor_tensor(rstd[u][:, 0, :], vv[u][:, 0, :], neg_half[:, 0:G], ALU.pow).then_inc(rs_ready.sem, 1)

            pool.wait_ge(*su["empty"](1))
            edge_phase_done(pool)

            def node(turn):
                for g, u in both(turn):
                    pool.wait_ge(*ndd["x_in"][u](16 * (turn + 1)))
                    reuse(pool, nd["x2"], g)
                    pool.tensor_tensor(bB[u][:, :, :], bA[u][:, :, :], over_tiles(empty0), ALU.add).then_inc(nd["y0"].sem, 1)
                for g, u in both(turn):
                    apart(pool, *nd["mv1"](g + 1))
                    pool.tensor_scalar(vv[u][:, 0, :], mv[u][:, :, 1], 1.0, LN_EPS, ALU.mult, ALU.add)
                    pool.tensor_scalar(vv[u][:, 1, :], mv[u][:, :, 1], 1.0 + LN_EPS, LN_EPS * LN_EPS,
                                       ALU.mult, ALU.add).then_inc(nd["var1"].sem, 1)
                    pool.wait_ge(*nd["var1"](g + 1))
                    pool.tensor_tensor(rstd[u][:, :, :], vv[u][:, :, :],
                                       neg_half[:, :].rearrange("p (a b) -> p a b", a=2), ALU.pow).then_inc(nd["rs1"].sem, 1)
                for g, u in both(turn):
                    pool.wait_ge(*nd["x2"](g + 1))
                    reuse(pool, nd["y"], g)
                    pool.tensor_tensor(bE[u][:, :, :], bD[u][:, :, :], over_tiles(half_beta2), ALU.add).then_inc(nd["xb"].sem, 1)
                rsqrt(turn, nd["mv2"], nd["var2"], nd["rs2"], 4.0, 4.0 * LN_EPS)
                rsqrt(turn, nd["mv3"], nd["var3"], nd["rs3"], 1.0, LN_EPS / 4.0)
                rsqrt(turn, nd["mv4"], nd["var4"], nd["rs4"], 1.0, LN_EPS * 4.0)

            turns(pool, node, NODE_GROUPS)
            node_phase_done(pool)

            def gather(table_, buf, col, done, u):
                for j in range(G):
                    pool.indirect_dma_start(
                        out=buf[u][:, j, :], out_offset=None, in_=table_,
                        in_offset=bass.IndirectOffsetOnAxis(ap=idx[u][:, col + j:col + j + 1].bitcast(U32), axis=0),
                    ).then_inc(done[u].sem, 16)

            def scatter(k, turn, table_, x_ready):
                for g, u in both(turn):
                    apart(pool, *x_ready(g + 1))
                    for j in range(G):
                        pool.indirect_dma_start(
                            out=table_, out_offset=bass.IndirectOffsetOnAxis(ap=scat[u][:, j:j + 1], axis=0),
                            in_=bF[u][:, j, :], in_offset=None, bounds_check=LAST_ROW, oob_is_err=False,
                        ).then_inc(segd[k]["scattered"][u].sem, 16)

            def s0_gather(turn):
                for g, u in both(turn):
                    apart(pool, *segd[0]["idx_in"][u](16 * (turn + 1)))
                    reuse(pool, seg[0]["agg"], g, stand=True)
                    gather(x0_table, bA, 0, segd[0]["src_in"], u)
                    reuse(pool, s0["xb"], g, stand=True)
                    gather(x0_table, bC, G, s0d["xd_in"], u)

            def s0_residual(turn):
                for g, u in both(turn):
                    pool.wait_ge(*s0d["xd_in"][u](16 * G * (turn + 1)))
                    reuse(pool, s0["y"], g)
                    pool.tensor_tensor(bD[u][:, :, :], bC[u][:, :, :], over_tiles(rows["beta0"]), ALU.add).then_inc(s0["xb"].sem, 1)

            def s0_rest(turn):
                rsqrt(turn, s0["mv1"], s0["var1"], s0["rs1"], 1.0, LN_EPS)
                rsqrt(turn, s0["mv2"], s0["var2"], s0["rs2"], 1.0, LN_EPS)
                scatter(0, turn, x1_table, s0["x"])

            turns_ahead(pool, s0_gather, s0_rest, EDGE_GROUPS, s0_residual)
            slots_done(pool, 0)

            def s1_gather(turn):
                for g, u in both(turn):
                    apart(pool, *segd[1]["idx_in"][u](16 * (turn + 1)))
                    reuse(pool, s1["tr"], g, stand=True)
                    gather(x1_table, bA, 0, segd[1]["src_in"], u)

            def s1_rest(turn):
                rsqrt(turn, s1["mv1"], s1["var1"], s1["rs1"], 1.0, LN_EPS)
                scatter(1, turn, x2_table, s1["x"])

            turns_ahead(pool, s1_gather, s1_rest, EDGE_GROUPS)
            slots_done(pool, 1)

            def s2_gather(turn):
                for g, u in both(turn):
                    apart(pool, *segd[2]["idx_in"][u](16 * (turn + 1)))
                    reuse(pool, seg[2]["agg"], g, stand=True)
                    gather(x2_table, bA, 0, segd[2]["src_in"], u)

            def s2_rest(turn):
                for g, u in both(turn):
                    pool.wait_ge(*s2d["x_in"][u](16 * (turn + 1)))
                    reuse(pool, s2["y"], g)
                    pool.tensor_tensor(bD[u][:, :, :], bC[u][:, :, :], over_tiles(half_beta2), ALU.add).then_inc(s2["xb"].sem, 1)
                rsqrt(turn, s2["mv1"], s2["var1"], s2["rs1"], 4.0, 4.0 * LN_EPS)
                rsqrt(turn, s2["mv2"], s2["var2"], s2["rs2"], 1.0, LN_EPS / 4.0)
                scatter(2, turn, x3_table, s2["x"])

            turns_ahead(pool, s2_gather, s2_rest, EDGE_GROUPS)
            slots_done(pool, 2)

            def s3_gather(turn):
                for g, u in both(turn):
                    apart(pool, *segd[3]["idx_in"][u](16 * (turn + 1)))
                    reuse(pool, s3["trs"], g, stand=True)
                    gather(x3_table, bA, 0, segd[3]["src_in"], u)
                    reuse(pool, s3["tr"], g, stand=True)
                    gather(x3_table, bC, G, s3d["xd_in"], u)

            def s3_rest(turn):
                rsqrt(turn, s3["mv1"], s3["var1"], s3["rs1"], 1.0, LN_EPS)
                rsqrt(turn, s3["mv2"], s3["var2"], s3["rs2"], 1.0, 4.0 * LN_EPS)
                scatter(3, turn, out, s3["x"])

            turns_ahead(pool, s3_gather, s3_rest, EDGE_GROUPS)
            slots_done(pool, 3)

        @block.scalar
        def _(act):
            act.wait_ge(*su["loaded"](16 * CONST_LOADS))
            act.wait_ge(*su["consts"](3))
            act.wait_ge(*su["scaled"](SCALED))

            def edge(turn):
                for g, u in both(turn):
                    act.wait_ge(*pa["clipped"](g + 1))
                    reuse(act, pa["exped"], g)
                    act.activation(sq_row[u][:, :], e_row[u][:, :], ACT.Square, bias=neg_centers[:, 0:1],
                                   scale=1.0 / SIGMA).then_inc(pa["squared"].sem, 1)
                for g, u in both(turn):
                    act.wait_ge(*pa["squared"](g + 1))
                    reuse(act, pa["emb"], g)
                    act.activation(exp_row[u][:, :], sq_row[u][:, :], ACT.Exp, scale=-0.5).then_inc(pa["exped"].sem, 1)
                for g, u in both(turn):
                    act.wait_ge(*pa["h0_mm"](g + 1))
                    reuse(act, pa["h1"], g)
                    h = flat(ps[u][0])[0:H1, :]
                    act.activation(hid_t[u][:, :], h, ACT.Tanh, bias=mb0h[:, 0:1], scale=0.5).then_inc(pa["h0_tanh"].sem, 1)
                    act.activation(hid_x[u][:, :], h, ACT.Identity, bias=mb0[:, 0:1]).then_inc(pa["h0_lin"].sem, 1)
                for g, u in both(turn):
                    act.wait_ge(*pa["h1_mm"](g + 1))
                    h = flat(ps[u][0])[0:H1, :]
                    act.activation(hid_t[u][:, :], h, ACT.Tanh, bias=mb1h[:, 0:1], scale=0.5).then_inc(pa["h1_tanh"].sem, 1)
                    act.activation(hid_x[u][:, :], h, ACT.Identity, bias=mb1[:, 0:1]).then_inc(pa["h1_lin"].sem, 1)
                for g, u in both(turn):
                    act.wait_ge(*pa["logit_mm"](g + 1))
                    reuse(act, pa["gate"], g)
                    reuse(act, pa["grow"], g)
                    act.activation(gate_t[u][:, :], flat(ps[u][3])[:, 0:G], ACT.Tanh, bias=gate_bh[:, 0:1],
                                   scale=0.5).then_inc(pa["gate_tanh"].sem, 1)
                    act.activation(gate_row_t[u][:, :], flat(ps[u][1])[0:1, :], ACT.Tanh, bias=gate_bh[0:1, 0:1],
                                   scale=0.5).then_inc(pa["grow_tanh"].sem, 1)
                for g, u in both(turn):
                    act.wait_ge(*pa["w_mm"](g + 1))
                    if not (isinstance(turn, int) and turn == 0):
                        act.wait_ge(*pad["w_st"][u](16 * turn))
                    act.copy(flat(bA[u]), flat(ps[u][2])).then_inc(pa["w_copied"].sem, 1)

            turns(act, edge, EDGE_GROUPS)
            edge_phase_done(act)

            def node(turn):
                for g, u in both(turn):
                    act.wait_ge(*nd["tr"](g + 1))
                    reuse(act, nd["f_mm"], g)
                    act.copy(flat(xt[u]), flat(ps[u][0])).then_inc(nd["xt"].sem, 1)
                for g, u in both(turn):
                    act.wait_ge(*nd["f"](g + 1))
                    act.activation(flat(ps[u][1]), flat(ps[u][1]), ACT.Gelu).then_inc(nd["gelu"].sem, 1)
                for g, u in both(turn):
                    act.wait_ge(*nd["tr3"](g + 1))
                    reuse(act, nd["ya"], g)
                    act.copy(flat(xt3[u]), flat(ps[u][0])).then_inc(nd["xt3"].sem, 1)
                for g, u in both(turn):
                    act.wait_ge(*nd["r_mm"](g + 1))
                    reuse(act, nd["rh"], g)
                    act.activation(flat(gr[u]), flat(ps[u][1]), ACT.Tanh, bias=brz[:, 0:1], scale=0.5).then_inc(nd["r_tanh"].sem, 1)
                    act.wait_ge(*nd["n_mm"](g + 1))
                    act.activation(flat(ps[u][3]), flat(ps[u][3]), ACT.Identity, bias=bhh[:, 2:3]).then_inc(nd["hn"].sem, 1)
                    act.wait_ge(*nd["z_mm"](g + 1))
                    act.activation(flat(ps[u][2]), flat(ps[u][2]), ACT.Tanh, bias=brz[:, 1:2], scale=0.5).then_inc(nd["z_tanh"].sem, 1)
                for g, u in both(turn):
                    act.wait_ge(*nd["rh"](g + 1))
                    reuse(act, nd["yb"], g)
                    act.activation(flat(gn[u]), flat(ps[u][3]), ACT.Tanh, bias=bih[:, 2:3], scale=0.5).then_inc(nd["n"].sem, 1)

            turns(act, node, NODE_GROUPS)
            node_phase_done(act)

            slots_done(act, 0)

            def s1_turn(turn):
                for g, u in both(turn):
                    act.wait_ge(*s1["tr"](g + 1))
                    reuse(act, s1["up"], g)
                    act.copy(flat(xt[u]), flat(ps[u][0])).then_inc(s1["xt"].sem, 1)

            turns(act, s1_turn, EDGE_GROUPS)
            slots_done(act, 1)

            def s2_turn(turn):
                for g, u in both(turn):
                    act.wait_ge(*s2["tr"](g + 1))
                    reuse(act, s2["r_mm"], g)
                    act.copy(flat(xt[u]), flat(ps[u][0])).then_inc(s2["xt"].sem, 1)
                for g, u in both(turn):
                    act.wait_ge(*s2["f"](g + 1))
                    act.activation(flat(ps[u][2]), flat(ps[u][2]), ACT.Gelu).then_inc(s2["gelu"].sem, 1)

            turns(act, s2_turn, EDGE_GROUPS)
            slots_done(act, 2)

            def s3_turn(turn):
                for g, u in both(turn):
                    act.wait_ge(*s3["trs"](g + 1))
                    reuse(act, s3["h_mm"], g)
                    act.copy(flat(xt[u]), flat(ps[u][0])).then_inc(s3["xt"].sem, 1)
                    act.wait_ge(*s3["tr"](g + 1))
                    reuse(act, s3["ya"], g)
                    act.copy(flat(xt3[u]), flat(ps[u][1])).then_inc(s3["xt3"].sem, 1)
                for g, u in both(turn):
                    act.wait_ge(*s3["y"](g + 1))
                    act.activation(flat(bE[u]), flat(bE[u]), ACT.Relu).then_inc(s3["relu"].sem, 1)
                for g, u in both(turn):
                    act.wait_ge(*s3["a2_mm"](g + 1))
                    reuse(act, s3["in_mm"], g)
                    act.copy(flat(bB[u]), flat(ps[u][3])).then_inc(s3["a2"].sem, 1)
                for g, u in both(turn):
                    act.wait_ge(*s3["r_mm"](g + 1))
                    reuse(act, s3["rh"], g)
                    act.activation(flat(gr[u]), flat(ps[u][1]), ACT.Tanh, bias=brz[:, 0:1], scale=0.5).then_inc(s3["r_tanh"].sem, 1)
                    act.wait_ge(*s3["n_mm"](g + 1))
                    act.activation(flat(ps[u][0]), flat(ps[u][0]), ACT.Identity, bias=bhh[:, 2:3]).then_inc(s3["hn"].sem, 1)
                    act.wait_ge(*s3["z_mm"](g + 1))
                    act.activation(flat(ps[u][2]), flat(ps[u][2]), ACT.Tanh, bias=brz[:, 1:2], scale=0.5).then_inc(s3["z_tanh"].sem, 1)
                for g, u in both(turn):
                    act.wait_ge(*s3["ni"](g + 1))
                    reuse(act, s3["yb"], g)
                    act.activation(flat(gn[u]), flat(ps[u][3]), ACT.Tanh, bias=bih[:, 2:3]).then_inc(s3["n"].sem, 1)

            turns(act, s3_turn, EDGE_GROUPS)
            slots_done(act, 3)

        @block.tensor
        def _(pe):
            pe.wait_ge(*su["loaded"](16 * CONST_LOADS))
            pe.wait_ge(*su["ident"](2))
            pe.wait_ge(*su["scaled"](SCALED))

            def transposes(target, source):
                for j in range(G):
                    last = pe.transpose(target[:, j, :], source[:, j, :], ident[:, :])
                return last

            def rows_by(target, source_t, weights, start=True, stop=True):
                for j in range(G):
                    last = pe.matmul(target[:, j, :], source_t[:, j, :], weights, start=start, stop=stop)
                return last

            def edge(turn):
                for g, u in both(turn):
                    pe.wait_ge(*pa["emb"](g + 1))
                    reuse(pe, pa["h1_lin"], g)
                    pe.matmul(flat(ps[u][0])[0:H1, :], m0[:, :], emb_row[u][:, :], start=True, stop=True).then_inc(pa["h0_mm"].sem, 1)
                for g, u in both(turn):
                    apart(pe, *pa["h0"](g + 1))
                    pe.matmul(flat(ps[u][0])[0:H1, :], m1[:, :], hid0[u][:, :], start=True, stop=True).then_inc(pa["h1_mm"].sem, 1)
                for g, u in both(turn):
                    pe.wait_ge(*pad["attr_in"][u](16 * (turn + 1)))
                    reuse(pe, pa["gate_tanh"], g)
                    reuse(pe, pa["cnt_max"], g)
                    reuse(pe, pa["grow_tanh"], g)
                    for j in range(G):
                        pe.matmul(flat(ps[u][3])[:, j:j + 1], attr[u][0:ED, tile_edges(j)], gate_w[:, :], start=True, stop=True)
                    pe.matmul(flat(ps[u][1])[0:1, :], gate_w[:, :], attr[u][0:ED, :], start=True, stop=True).then_inc(pa["logit_mm"].sem, 1)
                for g, u in both(turn):
                    pe.wait_ge(*pa["cnt"](g + 1))
                    pe.wait_ge(*pa["gate_tanh"](g + 1))
                    for j in range(G):
                        last = pe.matmul(flat(ps[u][3])[:, G + j:G + j + 1], cnt_row[u][0:1, tile_edges(j)],
                                         ones_row[0:1, 0:1], start=True, stop=True)
                    last.then_inc(pa["cnt_mm"].sem, 1)
                for g, u in both(turn):
                    pe.wait_ge(*pa["h1"](g + 1))
                    reuse(pe, pa["w_copied"], g)
                    for j in range(G):
                        last = pe.matmul(ps[u][2][:, j, :], hid1[u][:, tile_edges(j)], m2[:, :], start=True, stop=True)
                    last.then_inc(pa["w_mm"].sem, 1)

            turns(pe, edge, EDGE_GROUPS)
            edge_phase_done(pe)

            def node(turn):
                for g, u in both(turn):
                    pe.wait_ge(*nd["x2"](g + 1))
                    reuse(pe, nd["x"], g)
                    transposes(ps[u][0], bD[u]).then_inc(nd["tr"].sem, 1)
                for g, u in both(turn):
                    pe.wait_ge(*nd["xt"](g + 1))
                    rows_by(ps[u][1], xt[u], wr[:, :]).then_inc(nd["f_mm"].sem, 1)
                for g, u in both(turn):
                    pe.wait_ge(*nd["x3"](g + 1))
                    transposes(ps[u][0], bF[u]).then_inc(nd["tr3"].sem, 1)
                for g, u in both(turn):
                    pe.wait_ge(*nd["xt3"](g + 1))
                    pe.matmul(flat(ps[u][1]), whh[:, 0:D], flat(xt3[u]), start=True, stop=True).then_inc(nd["r_mm"].sem, 1)
                    pe.matmul(flat(ps[u][3]), whh[:, 2 * D:3 * D], flat(xt3[u]), start=True, stop=True).then_inc(nd["n_mm"].sem, 1)
                    pe.matmul(flat(ps[u][2]), whh[:, D:2 * D], flat(xt3[u]), start=True, stop=True).then_inc(nd["z_mm"].sem, 1)
                for g, u in both(turn):
                    pe.wait_ge(*nd["yt"](g + 1))
                    transposes(ps[u][0], bE2[u]).then_inc(nd["tr4"].sem, 1)

            turns(pe, node, NODE_GROUPS)
            node_phase_done(pe)

            def sum_runs(k, turn, messages, banks, ready, each=1):
                for g, u in both(turn):
                    pe.wait_ge(*seg[k]["S"](g + 1))
                    if isinstance(ready, list):
                        pe.wait_ge(*ready[u](16 * G * (turn + 1)))
                    else:
                        pe.wait_ge(*ready(g + 1))
                    reuse(pe, seg[k]["sums"], g, SUMS[k])
                    for h, bank in enumerate(banks):
                        for j in range(G):
                            last = pe.matmul(ps[u][bank][:, j, :], messages[u][:, j, h * D:(h + 1) * D], bS[u][:, j, :],
                                             start=True, stop=True)
                    last.then_inc(seg[k]["agg"].sem, 1)

            def s0_turn(turn):
                sum_runs(0, turn, bA, [0], segd[0]["src_in"])
                for g, u in both(turn):
                    pe.wait_ge(*seg[0]["sums"](SUMS[0] * (g + 1)))
                    reuse(pe, s0["y"], g)
                    rows_by(ps[u][1], sums[0][u], w0t[:, :]).then_inc(s0["h_mm"].sem, 1)

            turns(pe, s0_turn, EDGE_GROUPS)
            slots_done(pe, 0)

            def s1_turn(turn):
                for g, u in both(turn):
                    pe.wait_ge(*segd[1]["src_in"][u](16 * G * (turn + 1)))
                    reuse(pe, s1["y"], g)
                    transposes(ps[u][0], bA[u]).then_inc(s1["tr"].sem, 1)
                for g, u in both(turn):
                    pe.wait_ge(*s1["xt"](g + 1))
                    reuse(pe, s1["m2"], g)
                    rows_by(ps[u][1], xt[u], wup[:, :]).then_inc(s1["up"].sem, 1)
                sum_runs(1, turn, mid, [2, 3], s1["m2"])
                for g, u in both(turn):
                    pe.wait_ge(*seg[1]["sums"](SUMS[1] * (g + 1)))
                    for j in range(G):
                        pe.matmul(ps[u][0][:, j, :], sums[0][u][:, j, :], wo[0][:, :], start=True, stop=False)
                        last = pe.matmul(ps[u][0][:, j, :], sums[1][u][:, j, :], wo[1][:, :], start=False, stop=True)
                    last.then_inc(s1["h_mm"].sem, 1)

            turns(pe, s1_turn, EDGE_GROUPS)
            slots_done(pe, 1)

            def s2_turn(turn):
                for g, u in both(turn):
                    pe.wait_ge(*s2d["x_in"][u](16 * (turn + 1)))
                    reuse(pe, s2["xt"], g)
                    transposes(ps[u][0], bC[u]).then_inc(s2["tr"].sem, 1)
                for g, u in both(turn):
                    pe.wait_ge(*s2["xt"](g + 1))
                    reuse(pe, s2["rb"], g)
                    rows_by(ps[u][3], xt[u], wr[:, :]).then_inc(s2["r_mm"].sem, 1)
                sum_runs(2, turn, bA, [1], segd[2]["src_in"])
                for g, u in both(turn):
                    pe.wait_ge(*seg[2]["sums"](SUMS[2] * (g + 1)))
                    reuse(pe, s2["y"], g)
                    rows_by(ps[u][2], sums[0][u], wl[:, :]).then_inc(s2["l_mm"].sem, 1)

            turns(pe, s2_turn, EDGE_GROUPS)
            slots_done(pe, 2)

            def s3_turn(turn):
                for g, u in both(turn):
                    pe.wait_ge(*segd[3]["src_in"][u](16 * G * (turn + 1)))
                    reuse(pe, s3["rh"], g)
                    transposes(ps[u][0], bA[u]).then_inc(s3["trs"].sem, 1)
                    pe.wait_ge(*s3d["xd_in"][u](16 * G * (turn + 1)))
                    reuse(pe, s3["x"], g)
                    transposes(ps[u][1], bC[u]).then_inc(s3["tr"].sem, 1)
                for g, u in both(turn):
                    pe.wait_ge(*s3["xt"](g + 1))
                    pe.wait_ge(*s3["xt3"](g + 1))
                    pe.wait_ge(*s3d["attr_in"][u](16 * (turn + 1)))
                    reuse(pe, s3["ya"], g)
                    for j in range(G):
                        pe.matmul(ps[u][2][:, j, :], xt[u][:, j, :], w1a[:, :], start=True, stop=False)
                        pe.matmul(ps[u][2][:, j, :], xt3[u][:, j, :], w1b[:, :], start=False, stop=False)
                        last = pe.matmul(ps[u][2][:, j, :], attr[u][:, tile_edges(j)], w1c[:, :], start=False, stop=True)
                    last.then_inc(s3["h_mm"].sem, 1)
                sum_runs(3, turn, bE, [3], s3["relu"])
                for g, u in both(turn):
                    pe.wait_ge(*seg[3]["sums"](SUMS[3] * (g + 1)))
                    pe.wait_ge(*s3d["gs_in"][u](16 * (turn + 1)))
                    pe.matmul(flat(ps[u][3]), w2[:, :], flat(sums[0][u]), start=True, stop=False)
                    pe.matmul(flat(ps[u][3]), b2row[:, :], gsum_row[u][:, :], start=False, stop=True).then_inc(s3["a2_mm"].sem, 1)
                for g, u in both(turn):
                    pe.wait_ge(*s3["a2"](g + 1))
                    x, a = flat(xt3[u]), flat(bB[u])
                    pe.matmul(flat(ps[u][1]), wih[:, 0:D], a, start=True, stop=False)
                    pe.matmul(flat(ps[u][1]), whh[:, 0:D], x, start=False, stop=True).then_inc(s3["r_mm"].sem, 1)
                    pe.matmul(flat(ps[u][0]), whh[:, 2 * D:3 * D], x, start=True, stop=True).then_inc(s3["n_mm"].sem, 1)
                    pe.matmul(flat(ps[u][2]), wih[:, D:2 * D], a, start=True, stop=False)
                    pe.matmul(flat(ps[u][2]), whh[:, D:2 * D], x, start=False, stop=True).then_inc(s3["z_mm"].sem, 1)
                    pe.matmul(flat(ps[u][3]), wih[:, 2 * D:3 * D], a, start=True, stop=True).then_inc(s3["in_mm"].sem, 1)
                for g, u in both(turn):
                    pe.wait_ge(*s3["yt"](g + 1))
                    transposes(ps[u][1], bE2[u]).then_inc(s3["tr4"].sem, 1)

            turns(pe, s3_turn, EDGE_GROUPS)
            slots_done(pe, 3)

        @block.vector
        def _(dve):
            dve.wait_ge(*su["loaded"](16 * CONST_LOADS))
            done = [0]

            def scaled(ins):
                done[0] += 1
                ins.then_inc(su["scaled"].sem, 1)

            s_up, s_out, s3_ = MUL ** -0.5, (2 * MUL) ** -0.5 / 16.0, 3.0 ** 0.5
            scaled(dve.tensor_scalar(wup[:, :], wup[:, :], s_up, None, ALU.mult))
            scaled(dve.tensor_scalar(wo[0][0:64, :], wo[0][0:64, :], s_out, None, ALU.mult))
            scaled(dve.tensor_scalar(wo[0][64:128, :], wo[0][64:128, :], s_out * s3_, None, ALU.mult))
            scaled(dve.tensor_scalar(wo[1][0:32, :], wo[1][0:32, :], s_out * s3_, None, ALU.mult))
            scaled(dve.tensor_scalar(wo[1][32:64, :], wo[1][32:64, :], s_out, None, ALU.mult))
            scaled(dve.tensor_scalar(wo[1][64:128, :], wo[1][64:128, :], s_out, None, ALU.mult))
            scaled(dve.tensor_scalar(m1[:, :], m1[:, :], 0.5, None, ALU.mult))
            scaled(dve.tensor_scalar(m2[0:H1, :], m2[0:H1, :], 0.5, None, ALU.mult))
            scaled(dve.tensor_scalar(mb0h[:, :], mb0[:, :], 0.5, None, ALU.mult))
            scaled(dve.tensor_scalar(mb1h[:, :], mb1[:, :], 0.5, None, ALU.mult))
            scaled(dve.tensor_scalar(gate_bh[:, :], gate_b[:, :], 0.5, None, ALU.mult))
            scaled(dve.tensor_scalar(half_beta2[:, :], rows["beta2"][:, :], 0.5, None, ALU.mult))
            scaled(dve.tensor_tensor(brz[:, :], bih[:, :], bhh[:, :], ALU.add))
            scaled(dve.memset(ones_row[:, :], 1.0))
            scaled(dve.memset(sums[0][1][:, :, :], 0.0))
            scaled(dve.memset(sums[1][1][:, :, :], 0.0))
            for u in range(U):
                scaled(dve.memset(hid1[u][H1:H1 + 1, :], 1.0))
            dve.wait_ge(*su["scaled"](done[0]))
            scaled(dve.tensor_scalar(brz[:, :], brz[:, :], 0.5, None, ALU.mult))
            assert done[0] == SCALED

            dve.bn_stats(empty_st[:, :], rows["b0"][:, :]).then_inc(su["e_stats"].sem, 1)
            dve.wait_ge(*su["e_stats"](1))
            dve.bn_aggr(empty_mv[:, :], empty_st[:, :]).then_inc(su["e_mv"].sem, 1)
            dve.wait_ge(*su["e_mv"](1))
            dve.tensor_scalar(empty_v[:, :], empty_mv[:, 1:2], LN_EPS, None, ALU.add).then_inc(su["e_add"].sem, 1)
            dve.wait_ge(*su["e_rstd"](1))
            dve.tensor_scalar(empty0[:, :], rows["b0"][:, :], empty_mv[:, 0:1], empty_r[:, 0:1],
                              ALU.subtract, ALU.mult).then_inc(su["e_norm"].sem, 1)
            dve.wait_ge(*su["e_norm"](1))
            dve.tensor_tensor(empty0[:, :], empty0[:, :], rows["gamma0"][:, :], ALU.mult).then_inc(su["e_gamma"].sem, 1)
            dve.wait_ge(*su["e_gamma"](1))
            dve.tensor_tensor(empty0[:, :], empty0[:, :], rows["beta0"][:, :], ALU.add).then_inc(su["empty"].sem, 1)

            dve.tensor_tensor(sq_vec[:, :, :], rhat[:, :, :], rhat[:, :, :], ALU.mult).then_inc(su["sq"].sem, 1)
            dve.wait_ge(*su["sq"](1))
            dve.tensor_reduce(norm[:, :], sq_vec[:, :, :], mybir.AxisListType.X, ALU.add).then_inc(su["ssum"].sem, 1)
            dve.wait_ge(*su["root"](1))
            dve.tensor_scalar(norm[:, :], norm[:, :], 1e-12, None, ALU.add).then_inc(su["root_eps"].sem, 1)
            dve.wait_ge(*su["root_eps"](1))
            dve.reciprocal(norm[:, :], norm[:, :]).then_inc(su["rinv"].sem, 1)
            dve.wait_ge(*su["rinv"](1))
            dve.tensor_tensor(rhat[:, :, :], rhat[:, :, :], norm[:, :].unsqueeze(2).broadcast_to((P, NT, 3)),
                              ALU.mult).then_inc(su["rhat"].sem, 1)

            def edge(turn):
                for g, u in both(turn):
                    dve.wait_ge(*pad["r_in"][u](16 * (turn + 1)))
                    reuse(dve, pa["squared"], g)
                    dve.tensor_scalar(e_row[u][:, :], r_row[u][:, :], 0.0, 1.0, ALU.max, ALU.min).then_inc(pa["clipped"].sem, 1)
                    dve.tensor_scalar(mask_row[u][:, :], r_row[u][:, :], R_MAX, NB ** 0.5, ALU.is_le, ALU.mult).then_inc(pa["masked"].sem, 1)
                for g, u in both(turn):
                    dve.wait_ge(*pad["dst_in"][u](16 * (turn + 1)))
                    dve.tensor_tensor(same_row[u][:, :], dst_row[u][0:1, 1:GP + 1], dst_row[u][0:1, 0:GP],
                                      ALU.is_equal).then_inc(pa["same"].sem, 1)
                    dve.wait_ge(*pa["same"](g + 1))
                    reuse(dve, pa["cnt_mm"], g)
                    first = isinstance(g, int) and g == 0
                    if not first:
                        dve.wait_ge(*pa["cnt"](g))
                    dve.tensor_tensor_scan(cnt_row[u][:, :], same_row[u][:, :], ones_row[:, :],
                                           0.0 if first else cnt_row[1 - u][:, GP - 1:GP], ALU.mult, ALU.add).then_inc(pa["cnt"].sem, 1)
                for g, u in both(turn):
                    dve.wait_ge(*pa["exped"](g + 1))
                    dve.wait_ge(*pa["masked"](g + 1))
                    reuse(dve, pa["h0_mm"], g)
                    dve.tensor_tensor(emb_row[u][:, :], exp_row[u][:, :], mask_row[u][:, :], ALU.mult).then_inc(pa["emb"].sem, 1)
                for g, u in both(turn):
                    dve.wait_ge(*pa["h0_tanh"](g + 1))
                    dve.wait_ge(*pa["h0_lin"](g + 1))
                    reuse(dve, pa["h1_mm"], g)
                    dve.scalar_tensor_tensor(hid0[u][:, :], hid_t[u][:, :], 1.0, hid_x[u][:, :], ALU.add, ALU.mult).then_inc(pa["h0"].sem, 1)
                for g, u in both(turn):
                    dve.wait_ge(*pa["h1_tanh"](g + 1))
                    dve.wait_ge(*pa["h1_lin"](g + 1))
                    reuse(dve, pa["w_mm"], g)
                    dve.scalar_tensor_tensor(hid1[u][0:H1, :], hid_t[u][:, :], 1.0, hid_x[u][:, :], ALU.add, ALU.mult).then_inc(pa["h1"].sem, 1)
                for g, u in both(turn):
                    dve.wait_ge(*pa["gate_tanh"](g + 1))
                    dve.tensor_scalar(gates[:, tiles_of(g)], gate_t[u][:, :], 0.5, 0.5, ALU.mult, ALU.add).then_inc(pa["gate"].sem, 1)
                    dve.wait_ge(*pa["grow_tanh"](g + 1))
                    dve.tensor_scalar(gate_row[u][:, :], gate_row_t[u][:, :], 0.5, 0.5, ALU.mult, ALU.add).then_inc(pa["grow"].sem, 1)
                    dve.wait_ge(*pa["grow"](g + 1))
                    if not (isinstance(turn, int) and turn == 0):
                        dve.wait_ge(*pad["gs_st"][u](16 * turn))
                    first = isinstance(g, int) and g == 0
                    if not first:
                        dve.wait_ge(*pa["gsum"](g))
                    dve.tensor_tensor_scan(gsum_row[u][:, :], same_row[u][:, :], gate_row[u][:, :],
                                           0.0 if first else gsum_row[1 - u][:, GP - 1:GP], ALU.mult, ALU.add).then_inc(pa["gsum"].sem, 1)
                for g, u in both(turn):
                    dve.wait_ge(*pa["cnt_mm"](g + 1))
                    dve.tensor_scalar(cnt_max[u][:, :], flat(ps[u][3])[:, G:2 * G], 1.0, None, ALU.max).then_inc(pa["cnt_max"].sem, 1)
                    dve.wait_ge(*pa["cnt_max"](g + 1))
                    dve.reciprocal(count_inv[:, tiles_of(g)], cnt_max[u][:, :]).then_inc(pa["cnt_inv"].sem, 1)

            turns(dve, edge, EDGE_GROUPS)
            edge_phase_done(dve)

            def moments(turn, source, ready, st_ready, mv_ready):
                for g, u in both(turn):
                    dve.wait_ge(*ready(g + 1))
                    for j in range(G):
                        last = dve.bn_stats(stats[u][:, j, :], source[u][:, j, :])
                    last.then_inc(st_ready.sem, 1)
                for g, u in both(turn):
                    apart(dve, *st_ready(g + 1))
                    for j in range(G):
                        last = dve.bn_aggr(mv[u][:, j, :], stats[u][:, j, :])
                    last.then_inc(mv_ready.sem, 1)

            def normalize(u, target, source, which=0):
                for j in range(G):
                    last = dve.tensor_scalar(target[:, j, :], source[:, j, :], mv[u][:, j, 0:1], rstd[u][:, which, j:j + 1],
                                             ALU.subtract, ALU.mult)
                return last

            def scale_row(u, target, source, row):
                for j in range(G):
                    last = dve.scalar_tensor_tensor(target[:, j, :], source[:, j, :], mv[u][:, j, 0:1], row[:, :],
                                                    ALU.subtract, ALU.mult)
                return last

            def scale_add(u, target, source, other):
                for j in range(G):
                    last = dve.scalar_tensor_tensor(target[:, j, :], source[:, j, :], rstd[u][:, 0, j:j + 1], other(j),
                                                    ALU.mult, ALU.add)
                return last

            bank = lambda k: [ps[u][k] for u in range(U)]

            def node(turn):
                moments(turn, bB, nd["y0"], nd["st1"], nd["mv1"])
                later = not (isinstance(turn, int) and turn == 0)
                for g, u in both(turn):
                    dve.wait_ge(*nd["rs1"](g + 1))
                    if later:
                        dve.wait_ge(*ndd["x1_st"][u](16 * turn))
                        dve.wait_ge(*ndd["x2_st"][u](16 * turn))
                    normalize(u, bC[u], bB[u], 0).then_inc(nd["x1"].sem, 1)
                    reuse(dve, nd["tr"], g)
                    reuse(dve, nd["xb"], g)
                    normalize(u, bD[u], bB[u], 1).then_inc(nd["x2"].sem, 1)
                for g, u in both(turn):
                    dve.wait_ge(*nd["f_mm"](g + 1))
                    dve.tensor_tensor(ps[u][1][:, :, :], ps[u][1][:, :, :], over_tiles(rows["bl"]), ALU.add).then_inc(nd["f"].sem, 1)
                moments(turn, bank(1), nd["gelu"], nd["st2"], nd["mv2"])
                for g, u in both(turn):
                    dve.wait_ge(*nd["mv2"](g + 1))
                    scale_row(u, ps[u][1], ps[u][1], rows["gamma2"]).then_inc(nd["fg"].sem, 1)
                for g, u in both(turn):
                    dve.wait_ge(*nd["rs2"](g + 1))
                    dve.wait_ge(*nd["fg"](g + 1))
                    dve.wait_ge(*nd["xb"](g + 1))
                    scale_add(u, bA2[u], ps[u][1], lambda j: bE[u][:, j, :]).then_inc(nd["y"].sem, 1)
                moments(turn, bA2, nd["y"], nd["st3"], nd["mv3"])
                for g, u in both(turn):
                    dve.wait_ge(*nd["rs3"](g + 1))
                    if later:
                        dve.wait_ge(*ndd["x3_st"][u](16 * turn))
                        reuse(dve, nd["tr3"], g)
                    normalize(u, bF[u], bA2[u]).then_inc(nd["x3"].sem, 1)
                for g, u in both(turn):
                    dve.wait_ge(*nd["r_tanh"](g + 1))
                    dve.wait_ge(*nd["hn"](g + 1))
                    dve.scalar_tensor_tensor(flat(ps[u][3]), flat(gr[u]), 1.0, flat(ps[u][3]), ALU.add, ALU.mult).then_inc(nd["rh"].sem, 1)
                for g, u in both(turn):
                    dve.wait_ge(*nd["z_tanh"](g + 1))
                    dve.wait_ge(*nd["xt3"](g + 1))
                    dve.scalar_tensor_tensor(flat(bG[u]), flat(ps[u][2]), 3.0, flat(xt3[u]), ALU.add, ALU.mult).then_inc(nd["ya"].sem, 1)
                for g, u in both(turn):
                    dve.wait_ge(*nd["n"](g + 1))
                    dve.scalar_tensor_tensor(flat(ps[u][2]), flat(ps[u][2]), -1.0, flat(gn[u]), ALU.add, ALU.mult).then_inc(nd["yb"].sem, 1)
                for g, u in both(turn):
                    dve.wait_ge(*nd["ya"](g + 1))
                    dve.wait_ge(*nd["yb"](g + 1))
                    reuse(dve, nd["tr4"], g)
                    dve.tensor_tensor(flat(bE2[u]), flat(bG[u]), flat(ps[u][2]), ALU.subtract).then_inc(nd["yt"].sem, 1)
                moments(turn, bank(0), nd["tr4"], nd["st4"], nd["mv4"])
                for g, u in both(turn):
                    dve.wait_ge(*nd["rs4"](g + 1))
                    if later:
                        dve.wait_ge(*ndd["x_st"][u](16 * turn))
                    normalize(u, bO[u], ps[u][0]).then_inc(nd["x"].sem, 1)

            turns(dve, node, NODE_GROUPS)
            node_phase_done(dve)

            def selections(k, turn, gated=False):
                s, d = seg[k], segd[k]
                for g, u in both(turn):
                    dve.wait_ge(*d["idx_in"][u](16 * (turn + 1)))
                    dve.tensor_copy(dst_col[u][:, :], idx[u][:, G:2 * G]).then_inc(s["dcol"].sem, 1)
                    dve.tensor_tensor(is_mid[u][:, :], idx[u][:, G:2 * G], idx[u][:, 2 * G:3 * G], ALU.is_equal).then_inc(s["mid"].sem, 1)
                    dve.wait_ge(*d["dst_in"][u](16 * (turn + 1)))
                    dve.tensor_copy(dst_before[u][:, :], dst_row[u][:, 0:GP:P]).then_inc(s["dbefore"].sem, 1)
                    if gated:
                        dve.tensor_copy(gate_t[u][:, :], gates[:, tiles_of(g)]).then_inc(s3["gcol"].sem, 1)
                for g, u in both(turn):
                    dve.wait_ge(*s["mid"](g + 1))
                    if not (isinstance(turn, int) and turn == 0):
                        dve.wait_ge(*d["scattered"][u](16 * G * turn))
                    dve.scalar_tensor_tensor(scat[u][:, :], is_mid[u][:, :], float(SKIP), idx[u][:, G:2 * G],
                                             ALU.mult, ALU.add).then_inc(s["scat"].sem, 1)
                    dve.wait_ge(*s["dcol"](g + 1))
                    if gated:
                        dve.wait_ge(*s3["gcol"](g + 1))
                    reuse(dve, s["agg"], g)
                    for j in range(G):
                        last = dve.tensor_scalar(bS[u][:, j, :], dst_row[u][:, 1 + j * P:1 + (j + 1) * P], dst_col[u][:, j:j + 1],
                                                 gate_t[u][:, j:j + 1] if gated else None,
                                                 ALU.is_equal, *([ALU.mult] if gated else []))
                    last.then_inc(s["S"].sem, 1)

            def carry(k, turn, banks, used):
                s = seg[k]
                n = len(banks)
                for g, u in both(turn):
                    dve.wait_ge(*s["agg"](g + 1))
                    dve.wait_ge(*s["dbefore"](g + 1))
                    reuse(dve, used, g)
                    for j in range(G):
                        for h, b in enumerate(banks):
                            if isinstance(g, int) and g == 0 and j == 0:
                                pass
                            else:
                                dve.wait_ge(*s["sums"](n * (G * g + j - 1) + h + 1))
                            before = sums[h][u][:, j - 1, P - 1:P] if j else sums[h][1 - u][:, G - 1, P - 1:P]
                            dve.tensor_scalar(carry_in[h][:, :], dst_row[u][:, 1 + j * P:1 + (j + 1) * P],
                                              dst_before[u][:, j:j + 1], before, ALU.is_equal, ALU.mult).then_inc(s["carry"].sem, 1)
                            dve.wait_ge(*s["carry"](n * (G * g + j) + h + 1))
                            dve.tensor_tensor(sums[h][u][:, j, :], ps[u][b][:, j, :], carry_in[h][:, :], ALU.add).then_inc(s["sums"].sem, 1)

            def s0_turn(turn):
                selections(0, turn)
                carry(0, turn, [0], s0["h_mm"])
                for g, u in both(turn):
                    dve.wait_ge(*s0["h_mm"](g + 1))
                    dve.tensor_tensor(ps[u][1][:, :, :], ps[u][1][:, :, :], over_tiles(rows["b0"]), ALU.add).then_inc(s0["f"].sem, 1)
                moments(turn, bank(1), s0["f"], s0["st1"], s0["mv1"])
                for g, u in both(turn):
                    dve.wait_ge(*s0["mv1"](g + 1))
                    scale_row(u, ps[u][1], ps[u][1], rows["gamma0"]).then_inc(s0["fg"].sem, 1)
                for g, u in both(turn):
                    dve.wait_ge(*s0["rs1"](g + 1))
                    dve.wait_ge(*s0["fg"](g + 1))
                    dve.wait_ge(*s0["xb"](g + 1))
                    scale_add(u, bA2[u], ps[u][1], lambda j: bD[u][:, j, :]).then_inc(s0["y"].sem, 1)
                moments(turn, bA2, s0["y"], s0["st2"], s0["mv2"])
                for g, u in both(turn):
                    dve.wait_ge(*s0["rs2"](g + 1))
                    if not (isinstance(turn, int) and turn == 0):
                        dve.wait_ge(*s0d["x_st"][u](16 * turn))
                    normalize(u, bF[u], bA2[u]).then_inc(s0["x"].sem, 1)

            turns(dve, s0_turn, EDGE_GROUPS)
            slots_done(dve, 0)

            def by_four(t, lo, n):
                return t[:, :, lo:lo + n * MUL].rearrange("p j (q m) -> p j q m", m=MUL)

            def s1_turn(turn):
                selections(1, turn)
                for g, u in both(turn):
                    dve.tensor_copy(rh[u][:, :, :], rhat[:, tiles_of(g), :]).then_inc(s1["rh"].sem, 1)
                    wv, up, md = bB[u], ps[u][1], mid[u]
                    unit = rh[u][:, :, :].unsqueeze(3).broadcast_to((P, G, 3, MUL))
                    dve.wait_ge(*s1["up"](g + 1))
                    dve.wait_ge(*s1d["w_in"][u](16 * (turn + 1)))
                    reuse(dve, seg[1]["agg"], g)
                    dve.tensor_tensor(by_four(md, 0, 2), by_four(wv, 0, 2), by_four(up, 0, 1).broadcast_to((P, G, 2, MUL)),
                                      ALU.mult).then_inc(s1["m0b"].sem, 1)
                    dve.wait_ge(*s1["rh"](g + 1))
                    dve.tensor_tensor(vr[u][:, :, :, :], by_four(up, MUL, 3), unit, ALU.mult).then_inc(s1["vr"].sem, 1)
                    dve.wait_ge(*s1["m0b"](g + 1))
                    dve.tensor_tensor(by_four(md, 2 * MUL, 3), by_four(md, MUL, 1).broadcast_to((P, G, 3, MUL)), unit,
                                      ALU.mult).then_inc(s1["m1"].sem, 1)
                    dve.wait_ge(*s1["vr"](g + 1))
                    dve.tensor_tensor(rq[u][:, :, :], vr[u][:, :, 0, :], vr[u][:, :, 1, :], ALU.add).then_inc(s1["vr01"].sem, 1)
                    dve.wait_ge(*s1["vr01"](g + 1))
                    dve.tensor_tensor(rq[u][:, :, :], rq[u][:, :, :], vr[u][:, :, 2, :], ALU.add).then_inc(s1["vr012"].sem, 1)
                    dve.wait_ge(*s1["vr012"](g + 1))
                    dve.wait_ge(*s1["m1"](g + 1))
                    dve.tensor_tensor(md[:, :, MUL:2 * MUL], wv[:, :, 3 * MUL:4 * MUL], rq[u][:, :, :], ALU.mult).then_inc(s1["m3"].sem, 1)
                    dve.tensor_tensor(by_four(md, 5 * MUL, 3), by_four(wv, 2 * MUL, 1).broadcast_to((P, G, 3, MUL)),
                                      by_four(up, MUL, 3), ALU.mult).then_inc(s1["m2"].sem, 1)
                carry(1, turn, [2, 3], s1["h_mm"])
                for g, u in both(turn):
                    dve.wait_ge(*s1["h_mm"](g + 1))
                    dve.wait_ge(*s1d["x_in"][u](16 * (turn + 1)))
                    dve.tensor_tensor(bA2[u][:, :, :], ps[u][0][:, :, :], bC[u][:, :, :], ALU.add).then_inc(s1["y"].sem, 1)
                moments(turn, bA2, s1["y"], s1["st1"], s1["mv1"])
                for g, u in both(turn):
                    dve.wait_ge(*s1["rs1"](g + 1))
                    if not (isinstance(turn, int) and turn == 0):
                        dve.wait_ge(*s1d["x_st"][u](16 * turn))
                    normalize(u, bF[u], bA2[u]).then_inc(s1["x"].sem, 1)

            turns(dve, s1_turn, EDGE_GROUPS)
            slots_done(dve, 1)

            def s2_turn(turn):
                selections(2, turn)
                for g, u in both(turn):
                    dve.wait_ge(*s2["r_mm"](g + 1))
                    dve.tensor_tensor(bE[u][:, :, :], ps[u][3][:, :, :], over_tiles(rows["bl"]), ALU.add).then_inc(s2["rb"].sem, 1)
                    dve.tensor_copy(cinv[u][:, :], count_inv[:, tiles_of(g)]).then_inc(s2["cinv"].sem, 1)
                carry(2, turn, [1], s2["l_mm"])
                for g, u in both(turn):
                    dve.wait_ge(*s2["l_mm"](g + 1))
                    dve.wait_ge(*s2["rb"](g + 1))
                    dve.wait_ge(*s2["cinv"](g + 1))
                    for j in range(G):
                        last = dve.scalar_tensor_tensor(ps[u][2][:, j, :], ps[u][2][:, j, :], cinv[u][:, j:j + 1], bE[u][:, j, :],
                                                        ALU.mult, ALU.add)
                    last.then_inc(s2["f"].sem, 1)
                moments(turn, bank(2), s2["gelu"], s2["st1"], s2["mv1"])
                for g, u in both(turn):
                    dve.wait_ge(*s2["mv1"](g + 1))
                    scale_row(u, ps[u][2], ps[u][2], rows["gamma2"]).then_inc(s2["fg"].sem, 1)
                for g, u in both(turn):
                    dve.wait_ge(*s2["rs1"](g + 1))
                    dve.wait_ge(*s2["fg"](g + 1))
                    dve.wait_ge(*s2["xb"](g + 1))
                    scale_add(u, bA2[u], ps[u][2], lambda j: bD[u][:, j, :]).then_inc(s2["y"].sem, 1)
                moments(turn, bA2, s2["y"], s2["st2"], s2["mv2"])
                for g, u in both(turn):
                    dve.wait_ge(*s2["rs2"](g + 1))
                    normalize(u, bF[u], bA2[u]).then_inc(s2["x"].sem, 1)

            turns(dve, s2_turn, EDGE_GROUPS)
            slots_done(dve, 2)

            def s3_turn(turn):
                selections(3, turn, gated=True)
                moments(turn, bank(2), s3["h_mm"], s3["st1"], s3["mv1"])
                for g, u in both(turn):
                    dve.wait_ge(*s3["mv1"](g + 1))
                    scale_row(u, ps[u][2], ps[u][2], rows["ln_g3"]).then_inc(s3["fg"].sem, 1)
                for g, u in both(turn):
                    dve.wait_ge(*s3["rs1"](g + 1))
                    dve.wait_ge(*s3["fg"](g + 1))
                    reuse(dve, seg[3]["agg"], g)
                    scale_add(u, bE[u], ps[u][2], lambda j: rows["ln_b3"][:, :]).then_inc(s3["y"].sem, 1)
                carry(3, turn, [3], s3["a2_mm"])
                for g, u in both(turn):
                    dve.wait_ge(*s3["r_tanh"](g + 1))
                    dve.wait_ge(*s3["hn"](g + 1))
                    dve.scalar_tensor_tensor(flat(bG[u]), flat(gr[u]), 1.0, flat(ps[u][0]), ALU.add, ALU.mult).then_inc(s3["rh"].sem, 1)
                for g, u in both(turn):
                    dve.wait_ge(*s3["rh"](g + 1))
                    dve.wait_ge(*s3["in_mm"](g + 1))
                    dve.scalar_tensor_tensor(flat(ps[u][3]), flat(bG[u]), 0.5, flat(ps[u][3]), ALU.mult, ALU.add).then_inc(s3["ni"].sem, 1)
                for g, u in both(turn):
                    dve.wait_ge(*s3["z_tanh"](g + 1))
                    dve.wait_ge(*s3["ni"](g + 1))
                    dve.scalar_tensor_tensor(flat(bG[u]), flat(ps[u][2]), 3.0, flat(xt3[u]), ALU.add, ALU.mult).then_inc(s3["ya"].sem, 1)
                for g, u in both(turn):
                    dve.wait_ge(*s3["n"](g + 1))
                    dve.scalar_tensor_tensor(flat(ps[u][2]), flat(ps[u][2]), -1.0, flat(gn[u]), ALU.add, ALU.mult).then_inc(s3["yb"].sem, 1)
                for g, u in both(turn):
                    dve.wait_ge(*s3["ya"](g + 1))
                    dve.wait_ge(*s3["yb"](g + 1))
                    reuse(dve, s3["tr4"], g)
                    dve.tensor_tensor(flat(bE2[u]), flat(bG[u]), flat(ps[u][2]), ALU.subtract).then_inc(s3["yt"].sem, 1)
                moments(turn, bank(1), s3["tr4"], s3["st2"], s3["mv2"])
                for g, u in both(turn):
                    dve.wait_ge(*s3["rs2"](g + 1))
                    if not (isinstance(turn, int) and turn == 0):
                        dve.wait_ge(*segd[3]["scattered"][u](16 * G * turn))
                    normalize(u, bF[u], ps[u][1]).then_inc(s3["x"].sem, 1)

            turns(dve, s3_turn, EDGE_GROUPS)
            slots_done(dve, 3)


def kernel(**inputs):
    import numpy as np
    import concourse.bacc as bacc
    from concourse.bass_utils import run_bass_kernel_spmd

    v = {k: np.asarray(a) for k, a in inputs.items()}

    def row(a):
        return np.ascontiguousarray(a.reshape(1, -1))

    def t(a):
        return np.ascontiguousarray(a.T)

    def padded(a, n, fill=0):
        out = np.full((n,) + a.shape[1:], fill, a.dtype)
        out[:a.shape[0]] = a
        return out

    tiles = EDGE_GROUPS * G
    src = padded(v["src"], EDGES_PAD)
    dst = padded(v["dst"], EDGES_PAD, LAST_ROW)
    after = np.concatenate([dst[1:], np.full(1, -1, dst.dtype)])

    def columns(a):
        return a.reshape(EDGE_GROUPS, G, P).transpose(0, 2, 1)

    wup = np.zeros((D, D), np.float32)
    wup[:MUL, :MUL] = v["L1_gnn_W_up0"]
    wo = np.zeros((2 * D, D), np.float32)
    wo[0:2 * MUL, :MUL] = v["L1_gnn_W_out0"]
    for c in range(3):
        wup[MUL + c::3, MUL + MUL * c:MUL + MUL * (c + 1)] = v["L1_gnn_W_up1"]
        wo[MUL * (2 + c):MUL * (3 + c), MUL + c::3] = v["L1_gnn_W_out1"][:MUL]
        wo[MUL * (5 + c):MUL * (6 + c), MUL + c::3] = v["L1_gnn_W_out1"][MUL:]
    attr = padded(v["edge_attr_64"], EDGES_PAD).T
    w1 = v["L3_gnn_W1"]
    arrays = {
        "x": padded(v["x"], NODES_PAD),
        "edge_idx": np.ascontiguousarray(np.concatenate([columns(src), columns(dst), columns(after)], axis=2)),
        "dst_line": row(np.concatenate([np.full(1, -1, dst.dtype), dst])),
        "edge_vec": np.ascontiguousarray(padded(v["edge_attr_3"], EDGES_PAD).reshape(tiles, P, 3).transpose(1, 0, 2)).reshape(P, tiles * 3),
        "edge_r": row(padded(v["edge_weight"], EDGES_PAD)),
        "attr_t": np.concatenate([attr, np.ones((1, EDGES_PAD), np.float32)]),
        "b0": row(v["L0_gnn_b"]), "gamma0": row(v["L0_gnn_gamma"]), "beta0": row(v["L0_gnn_beta"]), "w0t": t(v["L0_gnn_W"]),
        "wup": wup, "wo": wo, "m0": v["L1_gnn_mlp_w0"], "m1": v["L1_gnn_mlp_w1"],
        "m2": np.concatenate([v["L1_gnn_mlp_w2"], row(v["L1_gnn_mlp_b2"])]),
        "mb0": v["L1_gnn_mlp_b0"].reshape(-1, 1), "mb1": v["L1_gnn_mlp_b1"].reshape(-1, 1),
        "wl": v["L2_gnn_W_l"], "bl": row(v["L2_gnn_b_l"]), "wr": v["L2_gnn_W_r"],
        "gamma2": row(v["L2_gnn_gamma"]), "beta2": row(v["L2_gnn_beta"]),
        "w1ab": w1[:2 * D], "w1c": np.concatenate([w1[2 * D:], row(v["L3_gnn_b1"])]),
        "ln_g3": row(v["L3_gnn_ln_g"]), "ln_b3": row(v["L3_gnn_ln_b"]), "w2": v["L3_gnn_W2"], "b2row": row(v["L3_gnn_b2"]),
        "gate_w": v["L3_gnn_gate_w"], "gate_b": v["L3_gnn_gate_b"].reshape(1, 1),
        "wih": t(v["L3_gnn_W_ih"]), "whh": t(v["L3_gnn_W_hh"]),
        "bih": t(v["L3_gnn_b_ih"].reshape(3, D)), "bhh": t(v["L3_gnn_b_hh"].reshape(3, D)),
    }
    nc = bacc.Bacc("TRN2", target_bir_lowering=False, num_devices=1)
    feeds, aps = {}, {}
    for name, a in arrays.items():
        a = np.ascontiguousarray(a)
        feeds[f"in_{name}"] = a
        aps[name] = nc.dram_tensor(f"in_{name}", a.shape, mybir.dt.from_np(a.dtype), kind="ExternalInput").ap()
    out = nc.dram_tensor("out_0", (NODES_PAD, D), F32, kind="ExternalOutput").ap()
    build(nc, aps, out)
    r = run_bass_kernel_spmd(nc, [feeds], core_ids=[0])
    return r.results[0]["out_0"][:N_NODES]
```

```python
from contextlib import ExitStack

import concourse.bass as bass
from concourse import mybir

F32 = mybir.dt.float32
I32 = mybir.dt.int32
U32 = mybir.dt.uint32
ALU = mybir.AluOpType
ACT = mybir.ActivationFunctionType

P = 128
D = 128
G = 4
GP = G * P
U = 2
N_NODES = 50000
N_EDGES = 25000
NODE_GROUPS = -(-N_NODES // (GP * U)) * U
EDGE_GROUPS = -(-N_EDGES // (GP * U)) * U
NODES_PAD = NODE_GROUPS * GP
EDGES_PAD = EDGE_GROUPS * GP
MUL = 32
NB = 8
H1 = 64
ED = 64
R_MAX = 1.0
SIGMA = 1.0 / (NB - 1)
LN_EPS = 1e-5
SKIP = 1 << 20
LAST_ROW = NODES_PAD - 1
BN = 6
SCALED = 23
SUMS = (G, 2 * G, G, G)


class Signal:

    def __init__(self, sem, base):
        self.sem, self.base = sem, base

    def __call__(self, n):
        return self.sem, self.base + n


def build(nc, A, O):
    with ExitStack() as ctx:
        def sb(name, shape, dt=F32):
            return ctx.enter_context(nc.sbuf_tensor(name, shape, dt))

        pool_of_sems = {}

        def signal(name, total):
            sem, base = pool_of_sems.get(name) or (ctx.enter_context(nc.semaphore(name)), 0)
            pool_of_sems[name] = (sem, base + total)
            return Signal(sem, base)

        def signals(names, total):
            return {n.partition("*")[0]: signal(n.partition("*")[0], total * int(n.partition("*")[2] or 1))
                    for n in names.split()}

        def signals_by_buffer(names, total):
            return {n.partition("*")[0]: [signal(n.partition("*")[0] + str(u), total * int(n.partition("*")[2] or 1))
                                          for u in range(U)] for n in names.split()}

        def table(name, shape):
            return nc.dram_tensor(name, shape, F32, kind="Internal").ap()

        def pair(name, shape, dt=F32):
            return [sb(f"{name}{u}", shape, dt) for u in range(U)]

        x1_table, x2_table, x3_table = (table(f"x{k}_table", (NODES_PAD, D)) for k in (1, 2, 3))
        x1_slots, x2_slots = (table(f"x{k}_slots", (EDGE_GROUPS, P, G * D)) for k in (1, 2))
        radial_w = table("radial_w", (EDGE_GROUPS, P, G * D))
        gate_sums = table("gate_sums", (1, EDGES_PAD))
        x0_table, out = A["x"], O

        def node_rows(t, g):
            return t.rearrange("(g p j) d -> g p (j d)", p=P, j=G)[g]

        ident = sb("ident", [P, P])
        neg_half = sb("neg_half", [P, 8])
        rows = {}
        for name in ("b0", "gamma0", "beta0", "bl", "gamma2", "beta2", "ln_g3", "ln_b3"):
            rows[name] = sb(f"row_{name}", [P, D])
        half_beta2 = sb("half_beta2", [P, D])
        center = sb("center", [P, P])
        neg_center = sb("neg_center", [P, P])
        center_gamma2 = sb("center_gamma2", [P, P])
        bl_col = sb("bl_col", [D, 1])
        empty0 = sb("empty0", [P, D])
        w0t = sb("w0t", [D, D])
        wup = sb("wup", [D, D])
        wo = [sb(f"wo{h}", [P, D]) for h in range(2)]
        wl = sb("wl", [D, D])
        wr = sb("wr", [D, D])
        w1a = sb("w1a", [D, D])
        w1b = sb("w1b", [D, D])
        w1c = sb("w1c", [ED + 1, D])
        w2 = sb("w2", [D, D])
        b2row = sb("b2row", [1, D])
        wih = sb("wih", [D, 3 * D])
        whh = sb("whh", [D, 3 * D])
        bih = sb("bih", [D, 3])
        bhh = sb("bhh", [D, 3])
        brz = sb("brz", [D, 3])
        m0 = sb("m0", [NB, H1])
        m1 = sb("m1", [H1, H1])
        m2 = sb("m2", [H1 + 1, D])
        mb0 = sb("mb0", [H1, 1])
        mb1 = sb("mb1", [H1, 1])
        mb0h = sb("mb0h", [H1, 1])
        mb1h = sb("mb1h", [H1, 1])
        neg_centers = sb("neg_centers", [NB, 1])
        gate_w = sb("gate_w", [ED, 1])
        gate_b = sb("gate_b", [P, 1])
        gate_bh = sb("gate_bh", [P, 1])
        NT = EDGE_GROUPS * G
        rhat = sb("rhat", [P, NT, 3])
        count_inv = sb("count_inv", [P, NT])
        gates = sb("gates", [P, NT])
        empty_st = sb("empty_st", [P, BN])
        empty_mv = sb("empty_mv", [P, 2])
        empty_v = sb("empty_v", [P, 1])
        empty_r = sb("empty_r", [P, 1])
        always = sb("always", [P, 1])
        half = sb("half", [P, NT])
        sq_vec = sb("sq_vec", [P, NT, 3])
        norm = sb("norm", [P, NT])
        ones_row = sb("ones_row", [1, GP])

        bA = pair("bA", [P, G, D])
        bB = pair("bB", [P, G, D])
        bC = pair("bC", [P, G, D])
        bD = pair("bD", [P, G, D])
        bE = pair("bE", [P, G, D])
        bF = pair("bF", [P, G, D])
        bS = pair("bS", [P, G, D])
        bG = pair("bG", [P, G, D])
        bO = pair("bO", [P, G, D])
        gel = pair("gel", [P, G, D])
        bA2 = pair("bA2", [P, G, D])
        bE2 = pair("bE2", [P, G, D])
        xt = pair("xt", [P, G, D])
        xt3 = pair("xt3", [P, G, D])
        gr = pair("gr", [P, G, D])
        gn = pair("gn", [P, G, D])
        vr = pair("vr", [P, G, 3, MUL])
        rh = pair("rh", [P, G, 3])
        cinv = pair("cinv", [P, G])
        cnt_max = pair("cnt_max", [P, G])
        gate_t = pair("gate_t", [P, G])
        gate_row_t = pair("gate_row_t", [1, GP])
        sq_row = pair("sq_row", [NB, GP])
        exp_row = pair("exp_row", [NB, GP])
        emb_row = pair("emb_row", [NB, GP])
        hid_t = pair("hid_t", [H1, GP])
        hid0 = pair("hid0", [H1, GP])
        hid1 = pair("hid1", [H1 + 1, GP])
        mid = pair("mid", [P, G, 2 * D])
        sums = [pair(f"sums{h}_", [P, G, D]) for h in range(2)]
        NORMS = 4
        stats = [pair(f"stats{n}_", [P, G, BN]) for n in range(NORMS)]
        mv = [pair(f"mv{n}_", [P, G, 2]) for n in range(NORMS)]
        vv = [pair(f"vv{n}_", [P, 2, G]) for n in range(NORMS)]
        rstd = [pair(f"rstd{n}_", [P, 2, G]) for n in range(NORMS)]
        cols = pair("cols", [P, 2 * G], I32)
        mask = pair("mask", [P, G, D])
        idx = pair("idx", [P, 2 * G], I32)
        scat = pair("scat", [P, G], U32)
        is_mid = pair("is_mid", [P, G])
        dst_row = pair("dst_row", [P, GP + 1], I32)
        dst_col = pair("dst_col", [P, G])
        dst_before = pair("dst_before", [P, G])
        attr = pair("attr", [ED + 1, GP])
        r_row = pair("r_row", [NB, GP])
        e_row = pair("e_row", [NB, GP])
        same_row = pair("same_row", [1, GP])
        cnt_row = pair("cnt_row", [1, GP])
        gate_row = pair("gate_row", [1, GP])
        gsum_row = pair("gsum_row", [1, GP])
        rq = pair("rq", [P, G, MUL])

        ps = [[ctx.enter_context(nc.psum_tensor(f"ps{u}{k}", [P, G, D], F32)) for k in range(4)]
              for u in range(U)]


        CONST_TILES = [(t, A[n]) for t, n in (
            (w0t, "w0t"), (wup, "wup"), (wl, "wl"), (wr, "wr"), (w1c, "w1c"), (w2, "w2"), (b2row, "b2row"),
            (wih, "wih"), (whh, "whh"), (bih, "bih"), (bhh, "bhh"), (m0, "m0"), (m1, "m1"), (m2, "m2"),
            (mb0, "mb0"), (mb1, "mb1"), (gate_w, "gate_w"), (bl_col, "bl_col"))]
        CONST_TILES += [(w1a, A["w1ab"][0:D, :]), (w1b, A["w1ab"][D:2 * D, :]), (wo[0], A["wo"][0:P, :]),
                        (wo[1], A["wo"][P:2 * P, :]), (gate_b, A["gate_b"].broadcast_to((P, 1)))]
        CONST_LOADS = len(rows) + len(CONST_TILES) + 1

        def flat(t):
            return t[:, :, :].rearrange("p j d -> p (j d)")

        def over_tiles(row):
            return row[:, :].unsqueeze(1).broadcast_to((P, G, D))

        def edges_of(g):
            return bass.ds(g * GP, GP)

        def tiles_of(g):
            return bass.ds(g * G, G)

        def tile_edges(j):
            return slice(j * P, (j + 1) * P)

        def reuse(eng, sem, g, each=1, stand=False):
            if isinstance(g, int) and g < U:
                return
            if stand:
                apart(eng, *sem(each * (g - (U - 1))))
            else:
                eng.wait_ge(*sem(each * (g - (U - 1))))

        def pipeline(eng, step, groups, last_lag, first_lag=0):
            def turn_of(turn, steps=range(U)):
                for v in steps:
                    def at(lag, stage):
                        g, u = turn * U + (v - lag), (v - lag) % U
                        if isinstance(g, int) and not 0 <= g < groups:
                            return
                        stage(g, u, turn + (v - lag - u) // U)
                    step(at)
            peeled = 1 - (-last_lag // U)
            if first_lag < 0:
                turn_of(-1)
            for turn in range(peeled):
                turn_of(turn)
            ends = groups // U + first_lag
            with eng.Fori(peeled, ends) as turn:
                turn_of(turn)
            for turn in range(ends, groups // U - (-last_lag // U)):
                turn_of(turn)

        def reuse_dma(eng, sem, u, use, each=16, stand=False):
            if isinstance(use, int) and use == 0:
                return
            if stand:
                apart(eng, *sem[u](each * use))
            else:
                eng.wait_ge(*sem[u](each * use))

        A_TURNS = EDGE_GROUPS // U
        N_TURNS = NODE_GROUPS // U

        su = signals("go loaded consts ident scaled e_stats e_mv e_add e_rstd e_norm e_gamma empty sq ssum root "
                                       "root_eps rinv rhat", 0)
        E, N, T, NT_ = EDGE_GROUPS, NODE_GROUPS, A_TURNS, N_TURNS
        pa = signals("clipped squared exped emb h0_mm h0_tanh h0_lin h0 h1_mm h1_tanh h1_lin h1 w_mm "
                                       "w_copied logit_mm gate_tanh grow_tanh gate grow same cnt cnt_mm cnt_max cnt_inv gsum", E)
        pad = signals_by_buffer("r_in*16 attr_in*16 dst_in*16 w_st*16 gs_st*16", T)
        nd = signals("y0 st1 mv1 var1 rs1 x1 x2 tr xt f_mm gelu rows_mm fg_mm st2 mv2 var2 rs2 xb y st3 mv3 var3 rs3 x3 "
                                       "tr3 xt3 r_mm z_mm n_mm r_tanh z_tanh hn rh n ya yb tr4 st4 mv4 var4 rs4 x", N)
        ndd = signals_by_buffer("x_in*16 x1_st*16 x2_st*16 x3_st*16 x_st*16", NT_)
        seg = [signals(f"dcol dbefore mid scat S mask agg sums*{SUMS[k]}", E) for k in range(4)]
        segd = [signals_by_buffer(f"idx_in*16 cols_in*16 dst_in*16 src_in*{16 * G} scattered*{16 * G}", T) for k in range(4)]
        s0 = signals("h_mm f st1 mv1 var1 rs1 fg xb y st2 mv2 var2 rs2 x", E)
        s0d = signals_by_buffer(f"xd_in*{16 * G} x_st*16", T)
        s1 = signals("tr xt up rh m0b m1 vr vr01 vr012 m3 m2 h_mm y st1 mv1 var1 rs1 x", E)
        s1d = signals_by_buffer("w_in*16 x_in*16 x_st*16", T)
        s2 = signals("tr xt l_mm r_mm rb f gelu cinv st1 mv1 var1 rs1 fg xb y st2 mv2 var2 rs2 x", E)
        s2d = signals_by_buffer("x_in*16", T)
        s3 = signals("trs tr xt xt3 h_mm st1 mv1 var1 rs1 fg y relu gcol a2_mm a2 r_mm z_mm in_mm n_mm "
                                       "r_tanh z_tanh hn rh ni n ya yb yt tr4 st2 mv2 var2 rs2 x", E)
        s3d = signals_by_buffer(f"xd_in*{16 * G} attr_in*16 gs_in*16", T)

        def apart(eng, sem, value):
            value = value if isinstance(value, int) else eng.to_reg(value)
            eng.wait_ge(*su["go"](1))
            eng.wait_ge(sem, value)

        def all_of(eng, sem_pair, value):
            for q in sem_pair:
                eng.wait_ge(*q(value))

        def edge_phase_done(eng):
            all_of(eng, pad["w_st"], 16 * A_TURNS)
            all_of(eng, pad["gs_st"], 16 * A_TURNS)
            eng.wait_ge(*pa["gate"](EDGE_GROUPS))
            eng.wait_ge(*pa["cnt_inv"](EDGE_GROUPS))

        def node_phase_done(eng):
            for q in (ndd["x1_st"], ndd["x2_st"], ndd["x3_st"], ndd["x_st"]):
                all_of(eng, q, 16 * N_TURNS)

        def slots_done(eng, k):
            all_of(eng, segd[k]["scattered"], 16 * G * A_TURNS)
            if k == 0:
                all_of(eng, s0d["x_st"], 16 * A_TURNS)
            if k == 1:
                all_of(eng, s1d["x_st"], 16 * A_TURNS)

        block = ctx.enter_context(nc.Block())

        @block.sync
        def _(sp):
            for name in rows:
                sp.dma_start(rows[name][:, :], A[name].broadcast_to((P, D))).then_inc(su["loaded"].sem, 16)
            for t, source in CONST_TILES:
                sp.dma_start(t[:, :], source).then_inc(su["loaded"].sem, 16)
            sp.dma_start(rhat[:, :, :].rearrange("p t c -> p (t c)"), A["edge_vec"]).then_inc(su["loaded"].sem, 16)

            def edge_load(g, u, use):
                reuse(sp, pa["emb"], g)
                sp.dma_start(r_row[u][:, :], A["edge_r"][:, edges_of(g)].broadcast_to((NB, GP))).then_inc(pad["r_in"][u].sem, 16)
                reuse(sp, pa["logit_mm"], g)
                sp.dma_start(attr[u][0:ED, :], A["attr_t"][0:ED, edges_of(g)]).then_inc(pad["attr_in"][u].sem, 16)
                reuse(sp, pa["same"], g)
                sp.dma_start(dst_row[u][0:1, :], A["dst_line"][:, bass.ds(g * GP, GP + 1)]).then_inc(pad["dst_in"][u].sem, 16)

            def edge_store(g, u, use):
                sp.wait_ge(*pa["gsum"](g + 1))
                sp.dma_start(gate_sums[:, edges_of(g)], gsum_row[u][0:1, :]).then_inc(pad["gs_st"][u].sem, 16)

            def edge_store_w(g, u, use):
                sp.wait_ge(*pa["w_copied"](g + 1))
                sp.dma_start(radial_w[g], flat(bA[u])).then_inc(pad["w_st"][u].sem, 16)

            def edge_step(at):
                at(-1, edge_load)
                at(1, edge_store_w)
                at(0, edge_store)

            pipeline(sp, edge_step, EDGE_GROUPS, 1, -1)
            edge_phase_done(sp)

            def node_load(g, u, use):
                reuse(sp, nd["y0"], g)
                sp.dma_start(flat(bA[u]), node_rows(x0_table, g)).then_inc(ndd["x_in"][u].sem, 16)

            def node_store(ready, table_, buf, done):
                def stage(g, u, use):
                    sp.wait_ge(*ready(g + 1))
                    sp.dma_start(node_rows(table_, g), flat(buf[u])).then_inc(done[u].sem, 16)
                return stage

            def node_step(at):
                at(-1, node_load)
                at(0, node_store(nd["x1"], x1_table, bC, ndd["x1_st"]))
                at(0, node_store(nd["x2"], x2_table, bD, ndd["x2_st"]))
                at(3, node_store(nd["x"], out, bO, ndd["x_st"]))
                at(1, node_store(nd["x3"], x3_table, bF, ndd["x3_st"]))

            pipeline(sp, node_step, NODE_GROUPS, 3, -1)
            node_phase_done(sp)

            def idx_load(k):
                def stage(g, u, use):
                    reuse_dma(sp, segd[k]["src_in"], u, use, 16 * G, stand=True)
                    if k in (0, 3):
                        reuse_dma(sp, (s0d if k == 0 else s3d)["xd_in"], u, use, 16 * G, stand=True)
                    sp.dma_start(idx[u][:, :], A["edge_idx"][g]).then_inc(segd[k]["idx_in"][u].sem, 16)
                return stage

            def dst_load(k):
                def stage(g, u, use):
                    reuse(sp, seg[k]["mid"], g, stand=True)
                    sp.dma_start(cols[u][:, :], A["edge_cols"][g]).then_inc(segd[k]["cols_in"][u].sem, 16)
                    reuse(sp, seg[k]["mask"], g, stand=True)
                    sp.dma_start(dst_row[u][:, :], A["dst_line"][:, bass.ds(g * GP, GP + 1)]
                                 .broadcast_to((P, GP + 1))).then_inc(segd[k]["dst_in"][u].sem, 16)
                return stage

            def slots_store(ready, slots, done):
                def stage(g, u, use):
                    sp.wait_ge(*ready(g + 1))
                    sp.dma_start(slots[g], flat(bF[u])).then_inc(done[u].sem, 16)
                return stage

            def s0_step(at):
                at(-1, idx_load(0))
                at(-1, dst_load(0))
                at(1, slots_store(s0["x"], x1_slots, s0d["x_st"]))

            pipeline(sp, s0_step, EDGE_GROUPS, 1, -1)
            slots_done(sp, 0)

            def s1_load(g, u, use):
                reuse(sp, s1["m2"], g)
                sp.dma_start(flat(bB[u]), radial_w[g]).then_inc(s1d["w_in"][u].sem, 16)
                reuse(sp, s1["y"], g)
                sp.dma_start(flat(bC[u]), x1_slots[g]).then_inc(s1d["x_in"][u].sem, 16)

            def s1_step(at):
                at(2, slots_store(s1["x"], x2_slots, s1d["x_st"]))
                at(-1, idx_load(1))
                at(-1, dst_load(1))
                at(-1, s1_load)

            pipeline(sp, s1_step, EDGE_GROUPS, 2, -1)
            slots_done(sp, 1)

            def s2_load(g, u, use):
                reuse(sp, s2["tr"], g)
                reuse(sp, s2["xb"], g)
                sp.dma_start(flat(bC[u]), x2_slots[g]).then_inc(s2d["x_in"][u].sem, 16)

            def s2_step(at):
                at(-1, idx_load(2))
                at(0, dst_load(2))
                at(0, s2_load)

            pipeline(sp, s2_step, EDGE_GROUPS, 0, -1)
            slots_done(sp, 2)

            def s3_load(g, u, use):
                reuse(sp, s3["h_mm"], g)
                sp.dma_start(attr[u][:, :], A["attr_t"][:, edges_of(g)]).then_inc(s3d["attr_in"][u].sem, 16)
                reuse(sp, s3["a2_mm"], g)
                sp.dma_start(gsum_row[u][0:1, :], gate_sums[:, edges_of(g)]).then_inc(s3d["gs_in"][u].sem, 16)

            def s3_step(at):
                at(-1, idx_load(3))
                at(1, dst_load(3))
                at(1, s3_load)

            pipeline(sp, s3_step, EDGE_GROUPS, 1, -1)
            slots_done(sp, 3)

        @block.gpsimd
        def _(pool):
            pool.memset(always[:, :], 0.0).then_inc(su["go"].sem, 1)
            pool.memset(neg_half[:, :], -0.5).then_inc(su["consts"].sem, 1)
            pool.memset(half[:, :], 0.5).then_inc(su["consts"].sem, 1)
            pool.memset(ident[:, :], 0.0).then_inc(su["ident"].sem, 1)
            pool.wait_ge(*su["ident"](1))
            pool.affine_select(out=ident[:, :], in_=ident[:, :], compare_op=ALU.not_equal, fill=1.0, base=0,
                               pattern=[[-1, P]], channel_multiplier=1).then_inc(su["ident"].sem, 1)
            pool.iota(neg_centers[:, :], pattern=[[0, 1]], base=0, channel_multiplier=-1,
                      allow_small_or_imprecise_dtypes=True).then_inc(su["consts"].sem, 1)
            pool.wait_ge(*su["consts"](2))
            pool.wait_ge(*su["e_add"](1))
            pool.tensor_tensor(empty_r[:, :], empty_v[:, :], neg_half[:, 0:1], ALU.pow).then_inc(su["e_rstd"].sem, 1)
            pool.wait_ge(*su["ssum"](1))
            pool.tensor_tensor(norm[:, :], norm[:, :], half[:, :], ALU.pow).then_inc(su["root"].sem, 1)

            def rsqrt(n, s, m, mult, add):
                def stage(g, u, use):
                    apart(pool, *s[f"mv{m}"](g + 1))
                    pool.tensor_scalar(vv[n][u][:, 0, :], mv[n][u][:, :, 1], mult, add, ALU.mult, ALU.add).then_inc(s[f"var{m}"].sem, 1)
                    pool.wait_ge(*s[f"var{m}"](g + 1))
                    pool.tensor_tensor(rstd[n][u][:, 0, :], vv[n][u][:, 0, :], neg_half[:, 0:G], ALU.pow).then_inc(s[f"rs{m}"].sem, 1)
                return stage

            pool.wait_ge(*su["empty"](1))
            edge_phase_done(pool)

            def node_y0(g, u, use):
                pool.wait_ge(*ndd["x_in"][u](16 * (use + 1)))
                reuse(pool, nd["x2"], g)
                pool.tensor_tensor(bB[u][:, :, :], bA[u][:, :, :], over_tiles(empty0), ALU.add).then_inc(nd["y0"].sem, 1)

            def node_rs1(g, u, use):
                apart(pool, *nd["mv1"](g + 1))
                pool.tensor_scalar(vv[0][u][:, 0, :], mv[0][u][:, :, 1], 1.0, LN_EPS, ALU.mult, ALU.add)
                pool.tensor_scalar(vv[0][u][:, 1, :], mv[0][u][:, :, 1], 1.0 + LN_EPS, LN_EPS * LN_EPS,
                                   ALU.mult, ALU.add).then_inc(nd["var1"].sem, 1)
                pool.wait_ge(*nd["var1"](g + 1))
                pool.tensor_tensor(rstd[0][u][:, :, :], vv[0][u][:, :, :],
                                   neg_half[:, :].rearrange("p (a b) -> p a b", a=2), ALU.pow).then_inc(nd["rs1"].sem, 1)

            def node_xb(g, u, use):
                pool.wait_ge(*nd["x2"](g + 1))
                reuse(pool, nd["y"], g)
                pool.tensor_tensor(bE[u][:, :, :], bD[u][:, :, :], over_tiles(half_beta2), ALU.add).then_inc(nd["xb"].sem, 1)

            def node_step(at):
                at(0, node_y0)
                at(0, node_rs1)
                at(1, rsqrt(1, nd, 2, 4.0, 4.0 * LN_EPS))
                at(3, rsqrt(3, nd, 4, 1.0, LN_EPS * 4.0))
                at(0, node_xb)
                at(1, rsqrt(2, nd, 3, 1.0, LN_EPS / 4.0))

            pipeline(pool, node_step, NODE_GROUPS, 3)
            node_phase_done(pool)

            def gather(table_, buf, col, done, u, tiles=range(G)):
                for j in tiles:
                    pool.indirect_dma_start(
                        out=buf[u][:, j, :], out_offset=None, in_=table_,
                        in_offset=bass.IndirectOffsetOnAxis(ap=idx[u][:, col + j:col + j + 1].bitcast(U32), axis=0),
                    ).then_inc(done[u].sem, 16)

            def gather_src(k, table_, free):
                def stage(g, u, use):
                    apart(pool, *segd[k]["idx_in"][u](16 * (use + 1)))
                    reuse(pool, free, g, stand=True)
                    gather(table_, bA, 0, segd[k]["src_in"], u)
                return stage

            def gather_half(k, table_, free, half_):
                def stage(g, u, use):
                    if half_ == 0:
                        apart(pool, *segd[k]["idx_in"][u](16 * (use + 1)))
                        reuse(pool, free, g, stand=True)
                    gather(table_, bA, 0, segd[k]["src_in"], u, range(half_ * G // 2, (half_ + 1) * G // 2))
                return stage

            def gather_dst(table_, free, done):
                def stage(g, u, use):
                    reuse(pool, free, g, stand=True)
                    gather(table_, bC, G, done, u)
                return stage

            def scatter(k, table_, x_ready):
                def stage(g, u, use):
                    apart(pool, *x_ready(g + 1))
                    for j in range(G):
                        pool.indirect_dma_start(
                            out=table_, out_offset=bass.IndirectOffsetOnAxis(ap=scat[u][:, j:j + 1], axis=0),
                            in_=bF[u][:, j, :], in_offset=None, bounds_check=LAST_ROW, oob_is_err=False,
                        ).then_inc(segd[k]["scattered"][u].sem, 16)
                return stage

            def s0_step(at):
                at(0, gather_src(0, x0_table, seg[0]["agg"]))
                at(1, rsqrt(1, s0, 2, 1.0, LN_EPS))
                at(0, gather_dst(x0_table, s0["xb"], s0d["xd_in"]))
                at(1, scatter(0, x1_table, s0["x"]))
                at(0, rsqrt(0, s0, 1, 1.0, LN_EPS))

            pipeline(pool, s0_step, EDGE_GROUPS, 1)
            slots_done(pool, 0)

            def s1_step(at):
                at(0, gather_src(1, x1_table, s1["tr"]))
                at(2, scatter(1, x2_table, s1["x"]))
                at(1, rsqrt(0, s1, 1, 1.0, LN_EPS))

            pipeline(pool, s1_step, EDGE_GROUPS, 2)
            slots_done(pool, 1)

            def s2_step(at):
                at(3, scatter(2, x3_table, s2["x"]))
                at(2, rsqrt(0, s2, 1, 4.0, 4.0 * LN_EPS))
                at(0, gather_half(2, x2_table, seg[2]["agg"], 0))
                at(2, rsqrt(1, s2, 2, 1.0, LN_EPS / 4.0))
                at(0, gather_half(2, x2_table, seg[2]["agg"], 1))

            pipeline(pool, s2_step, EDGE_GROUPS, 3)
            slots_done(pool, 2)

            def s3_step(at):
                at(4, rsqrt(1, s3, 2, 1.0, 4.0 * LN_EPS))
                at(0, gather_half(3, x3_table, s3["trs"], 0))
                at(2, rsqrt(0, s3, 1, 1.0, LN_EPS))
                at(0, gather_half(3, x3_table, s3["trs"], 1))
                at(4, scatter(3, out, s3["x"]))
                at(0, gather_dst(x3_table, s3["tr"], s3d["xd_in"]))

            pipeline(pool, s3_step, EDGE_GROUPS, 4)
            slots_done(pool, 3)

        @block.scalar
        def _(act):
            act.wait_ge(*su["loaded"](16 * CONST_LOADS))
            act.wait_ge(*su["consts"](3))
            act.wait_ge(*su["scaled"](SCALED))

            def edge_square(g, u, use):
                act.wait_ge(*pa["clipped"](g + 1))
                reuse(act, pa["exped"], g)
                act.activation(sq_row[u][:, :], e_row[u][:, :], ACT.Square, bias=neg_centers[:, 0:1],
                               scale=1.0 / SIGMA).then_inc(pa["squared"].sem, 1)

            def edge_exp(g, u, use):
                act.wait_ge(*pa["squared"](g + 1))
                reuse(act, pa["emb"], g)
                act.activation(exp_row[u][:, :], sq_row[u][:, :], ACT.Exp, scale=-0.5).then_inc(pa["exped"].sem, 1)

            def edge_hidden(n, bias_half, bias):
                def stage(g, u, use):
                    act.wait_ge(*pa[f"h{n}_mm"](g + 1))
                    if n == 0:
                        reuse(act, pa["h1"], g)
                    h = flat(ps[u][0])[0:H1, :]
                    act.activation(hid_t[u][:, :], h, ACT.Tanh, bias=bias_half[:, 0:1], scale=0.5).then_inc(pa[f"h{n}_tanh"].sem, 1)
                    act.activation(h, h, ACT.Identity, bias=bias[:, 0:1]).then_inc(pa[f"h{n}_lin"].sem, 1)
                return stage

            def edge_gate(g, u, use):
                act.wait_ge(*pa["logit_mm"](g + 1))
                reuse(act, pa["gate"], g)
                reuse(act, pa["grow"], g)
                act.activation(gate_t[u][:, :], flat(ps[u][3])[:, 0:G], ACT.Tanh, bias=gate_bh[:, 0:1],
                               scale=0.5).then_inc(pa["gate_tanh"].sem, 1)
                act.activation(gate_row_t[u][:, :], flat(ps[u][1])[0:1, :], ACT.Tanh, bias=gate_bh[0:1, 0:1],
                               scale=0.5).then_inc(pa["grow_tanh"].sem, 1)

            def edge_copy(g, u, use):
                act.wait_ge(*pa["w_mm"](g + 1))
                reuse_dma(act, pad["w_st"], u, use)
                act.copy(flat(bA[u]), flat(ps[u][2])).then_inc(pa["w_copied"].sem, 1)

            def edge_step(at):
                at(0, edge_square)
                at(0, edge_exp)
                at(1, edge_hidden(1, mb1h, mb1))
                at(0, edge_gate)
                at(1, edge_copy)
                at(0, edge_hidden(0, mb0h, mb0))

            pipeline(act, edge_step, EDGE_GROUPS, 1)
            edge_phase_done(act)

            def node_gates(g, u, use):
                act.wait_ge(*nd["r_mm"](g + 1))
                reuse(act, nd["rh"], g)
                act.activation(flat(gr[u]), flat(ps[u][1]), ACT.Tanh, bias=brz[:, 0:1], scale=0.5).then_inc(nd["r_tanh"].sem, 1)
                act.wait_ge(*nd["n_mm"](g + 1))
                act.activation(flat(ps[u][3]), flat(ps[u][3]), ACT.Identity, bias=bhh[:, 2:3]).then_inc(nd["hn"].sem, 1)
                act.wait_ge(*nd["z_mm"](g + 1))
                act.activation(flat(ps[u][2]), flat(ps[u][2]), ACT.Tanh, bias=brz[:, 1:2], scale=0.5).then_inc(nd["z_tanh"].sem, 1)

            def node_xt(g, u, use):
                act.wait_ge(*nd["tr"](g + 1))
                reuse(act, nd["f_mm"], g)
                act.copy(flat(xt[u]), flat(ps[u][0])).then_inc(nd["xt"].sem, 1)

            def node_x(g, u, use):
                act.wait_ge(*nd["rs4"](g + 1))
                reuse_dma(act, ndd["x_st"], u, use)
                for j in range(G):
                    last = act.activation(bO[u][:, j, :], ps[u][3][:, j, :], ACT.Copy, scale=rstd[3][u][:, 0, j:j + 1])
                last.then_inc(nd["x"].sem, 1)

            def node_gelu(g, u, use):
                act.wait_ge(*nd["f_mm"](g + 1))
                reuse(act, nd["fg_mm"], g)
                act.activation(flat(gel[u]), flat(ps[u][0]), ACT.Gelu, bias=bl_col[:, 0:1]).then_inc(nd["gelu"].sem, 1)

            def node_n(g, u, use):
                act.wait_ge(*nd["rh"](g + 1))
                reuse(act, nd["yb"], g)
                act.activation(flat(gn[u]), flat(ps[u][3]), ACT.Tanh, bias=bih[:, 2:3], scale=0.5).then_inc(nd["n"].sem, 1)

            def node_xt3(g, u, use):
                act.wait_ge(*nd["tr3"](g + 1))
                reuse(act, nd["ya"], g)
                act.copy(flat(xt3[u]), flat(ps[u][1])).then_inc(nd["xt3"].sem, 1)

            def node_step(at):
                at(2, node_gates)
                at(0, node_xt)
                at(3, node_x)
                at(0, node_gelu)
                at(2, node_n)
                at(1, node_xt3)

            pipeline(act, node_step, NODE_GROUPS, 3)
            node_phase_done(act)

            slots_done(act, 0)

            def copy_out(source, target, ready, done, free):
                def stage(g, u, use):
                    act.wait_ge(*ready(g + 1))
                    reuse(act, free, g)
                    act.copy(flat(target[u]), flat(ps[u][source])).then_inc(done.sem, 1)
                return stage

            def s1_step(at):
                at(0, copy_out(0, xt, s1["tr"], s1["xt"], s1["up"]))

            pipeline(act, s1_step, EDGE_GROUPS, 0)
            slots_done(act, 1)

            def s2_gelu(g, u, use):
                act.wait_ge(*s2["f"](g + 1))
                act.activation(flat(ps[u][2]), flat(ps[u][2]), ACT.Gelu).then_inc(s2["gelu"].sem, 1)

            def s2_step(at):
                at(1, copy_out(0, xt, s2["tr"], s2["xt"], s2["r_mm"]))
                at(2, s2_gelu)
                at(1, copy_out(3, bE, s2["r_mm"], s2["rb"], s2["f"]))

            pipeline(act, s2_step, EDGE_GROUPS, 2)
            slots_done(act, 2)

            def s3_relu(g, u, use):
                act.wait_ge(*s3["y"](g + 1))
                act.activation(flat(bE[u]), flat(bE[u]), ACT.Relu).then_inc(s3["relu"].sem, 1)

            def s3_gates(g, u, use):
                act.wait_ge(*s3["r_mm"](g + 1))
                reuse(act, s3["rh"], g)
                act.activation(flat(gr[u]), flat(ps[u][1]), ACT.Tanh, bias=brz[:, 0:1], scale=0.5).then_inc(s3["r_tanh"].sem, 1)
                act.wait_ge(*s3["n_mm"](g + 1))
                act.activation(flat(ps[u][0]), flat(ps[u][0]), ACT.Identity, bias=bhh[:, 2:3]).then_inc(s3["hn"].sem, 1)

            def s3_z(g, u, use):
                act.wait_ge(*s3["z_mm"](g + 1))
                act.activation(flat(ps[u][2]), flat(ps[u][2]), ACT.Tanh, bias=brz[:, 1:2], scale=0.5).then_inc(s3["z_tanh"].sem, 1)

            def s3_n(g, u, use):
                act.wait_ge(*s3["ni"](g + 1))
                reuse(act, s3["yb"], g)
                act.activation(flat(gn[u]), flat(ps[u][3]), ACT.Tanh, bias=bih[:, 2:3]).then_inc(s3["n"].sem, 1)

            def s3_step(at):
                at(3, s3_gates)
                at(2, s3_relu)
                at(3, s3_z)
                at(3, s3_n)
                at(2, copy_out(3, bB, s3["a2_mm"], s3["a2"], s3["in_mm"]))
                at(1, copy_out(0, xt, s3["trs"], s3["xt"], s3["h_mm"]))
                at(1, copy_out(1, xt3, s3["tr"], s3["xt3"], s3["ya"]))

            pipeline(act, s3_step, EDGE_GROUPS, 3)
            slots_done(act, 3)

        @block.tensor
        def _(pe):
            pe.wait_ge(*su["loaded"](16 * CONST_LOADS))
            pe.wait_ge(*su["ident"](2))
            pe.wait_ge(*su["scaled"](SCALED))

            def transposes(target, source):
                for j in range(G):
                    last = pe.transpose(target[:, j, :], source[:, j, :], ident[:, :])
                return last

            def rows_by(target, source_t, weights, start=True, stop=True):
                for j in range(G):
                    last = pe.matmul(target[:, j, :], source_t[:, j, :], weights, start=start, stop=stop)
                return last

            def edge_h0(g, u, use):
                pe.wait_ge(*pa["emb"](g + 1))
                reuse(pe, pa["h1"], g)
                pe.matmul(flat(ps[u][0])[0:H1, :], m0[:, :], emb_row[u][:, :], start=True, stop=True).then_inc(pa["h0_mm"].sem, 1)

            def edge_h1(g, u, use):
                apart(pe, *pa["h0"](g + 1))
                pe.matmul(flat(ps[u][0])[0:H1, :], m1[:, :], hid0[u][:, :], start=True, stop=True).then_inc(pa["h1_mm"].sem, 1)

            def edge_logits(g, u, use):
                pe.wait_ge(*pad["attr_in"][u](16 * (use + 1)))
                reuse(pe, pa["gate_tanh"], g)
                reuse(pe, pa["cnt_max"], g)
                reuse(pe, pa["grow_tanh"], g)
                for j in range(G):
                    pe.matmul(flat(ps[u][3])[:, j:j + 1], attr[u][0:ED, tile_edges(j)], gate_w[:, :], start=True, stop=True)
                pe.matmul(flat(ps[u][1])[0:1, :], gate_w[:, :], attr[u][0:ED, :], start=True, stop=True).then_inc(pa["logit_mm"].sem, 1)

            def edge_counts(g, u, use):
                pe.wait_ge(*pa["cnt"](g + 1))
                pe.wait_ge(*pa["gate_tanh"](g + 1))
                for j in range(G):
                    last = pe.matmul(flat(ps[u][3])[:, G + j:G + j + 1], cnt_row[u][0:1, tile_edges(j)],
                                     ones_row[0:1, 0:1], start=True, stop=True)
                last.then_inc(pa["cnt_mm"].sem, 1)

            def edge_w(g, u, use):
                pe.wait_ge(*pa["h1"](g + 1))
                reuse(pe, pa["w_copied"], g)
                for j in range(G):
                    last = pe.matmul(ps[u][2][:, j, :], hid1[u][:, tile_edges(j)], m2[:, :], start=True, stop=True)
                last.then_inc(pa["w_mm"].sem, 1)

            def edge_step(at):
                at(1, edge_h1)
                at(0, edge_logits)
                at(1, edge_w)
                at(0, edge_counts)
                at(0, edge_h0)

            pipeline(pe, edge_step, EDGE_GROUPS, 1)
            edge_phase_done(pe)

            def node_tr4(g, u, use):
                pe.wait_ge(*nd["ya"](g + 1))
                pe.wait_ge(*nd["yb"](g + 1))
                pe.wait_ge(*nd["n"](g + 1))
                for j in range(G):
                    pe.matmul(ps[u][3][:, j, :], bG[u][:, j, :], center[:, :], start=True, stop=False)
                    last = pe.matmul(ps[u][3][:, j, :], bE2[u][:, j, :], neg_center[:, :], start=False, stop=True)
                last.then_inc(nd["tr4"].sem, 1)

            def node_gates(g, u, use):
                pe.wait_ge(*nd["xt3"](g + 1))
                pe.matmul(flat(ps[u][1]), whh[:, 0:D], flat(xt3[u]), start=True, stop=True).then_inc(nd["r_mm"].sem, 1)
                reuse(pe, nd["x"], g)
                pe.matmul(flat(ps[u][3]), whh[:, 2 * D:3 * D], flat(xt3[u]), start=True, stop=True).then_inc(nd["n_mm"].sem, 1)
                reuse(pe, nd["yb"], g)
                pe.matmul(flat(ps[u][2]), whh[:, D:2 * D], flat(xt3[u]), start=True, stop=True).then_inc(nd["z_mm"].sem, 1)

            def node_tr(g, u, use):
                pe.wait_ge(*nd["x2"](g + 1))
                reuse(pe, nd["y"], g)
                transposes(ps[u][0], bD[u]).then_inc(nd["tr"].sem, 1)

            def node_f(g, u, use):
                pe.wait_ge(*nd["xt"](g + 1))
                pe.matmul(flat(ps[u][0]), wr[:, :], flat(xt[u]), start=True, stop=True).then_inc(nd["f_mm"].sem, 1)

            def node_rows_of_gelu(g, u, use):
                pe.wait_ge(*nd["gelu"](g + 1))
                reuse(pe, nd["r_tanh"], g)
                transposes(ps[u][1], gel[u]).then_inc(nd["rows_mm"].sem, 1)
                rows_by(ps[u][0], gel[u], center_gamma2[:, :]).then_inc(nd["fg_mm"].sem, 1)

            def node_tr3(g, u, use):
                pe.wait_ge(*nd["x3"](g + 1))
                pe.wait_ge(*nd["st2"](g + 1))
                transposes(ps[u][1], bF[u]).then_inc(nd["tr3"].sem, 1)

            def node_step(at):
                at(3, node_tr4)
                at(2, node_gates)
                at(0, node_tr)
                at(0, node_f)
                at(0, node_rows_of_gelu)
                at(1, node_tr3)

            pipeline(pe, node_step, NODE_GROUPS, 3)
            node_phase_done(pe)

            def sum_runs(k, messages, banks, ready, free):
                def stage(g, u, use):
                    pe.wait_ge(*seg[k]["S"](g + 1))
                    if isinstance(ready, list):
                        pe.wait_ge(*ready[u](16 * G * (use + 1)))
                    else:
                        pe.wait_ge(*ready(g + 1))
                    reuse(pe, seg[k]["sums"], g, SUMS[k])
                    if free:
                        reuse(pe, free, g)
                    for h, bank in enumerate(banks):
                        for j in range(G):
                            last = pe.matmul(ps[u][bank][:, j, :], messages[u][:, j, h * D:(h + 1) * D], bS[u][:, j, :],
                                             start=True, stop=True)
                    last.then_inc(seg[k]["agg"].sem, 1)
                return stage

            def s0_h(g, u, use):
                pe.wait_ge(*seg[0]["sums"](SUMS[0] * (g + 1)))
                reuse(pe, s0["y"], g)
                rows_by(ps[u][1], sums[0][u], w0t[:, :]).then_inc(s0["h_mm"].sem, 1)

            def s0_step(at):
                at(0, sum_runs(0, bA, [0], segd[0]["src_in"], None))
                at(0, s0_h)

            pipeline(pe, s0_step, EDGE_GROUPS, 0)
            slots_done(pe, 0)

            def s1_tr(g, u, use):
                pe.wait_ge(*segd[1]["src_in"][u](16 * G * (use + 1)))
                reuse(pe, s1["y"], g)
                transposes(ps[u][0], bA[u]).then_inc(s1["tr"].sem, 1)

            def s1_up(g, u, use):
                pe.wait_ge(*s1["xt"](g + 1))
                reuse(pe, s1["m2"], g)
                rows_by(ps[u][1], xt[u], wup[:, :]).then_inc(s1["up"].sem, 1)

            def s1_h(g, u, use):
                pe.wait_ge(*seg[1]["sums"](SUMS[1] * (g + 1)))
                for j in range(G):
                    pe.matmul(ps[u][0][:, j, :], sums[0][u][:, j, :], wo[0][:, :], start=True, stop=False)
                    last = pe.matmul(ps[u][0][:, j, :], sums[1][u][:, j, :], wo[1][:, :], start=False, stop=True)
                last.then_inc(s1["h_mm"].sem, 1)

            def s1_step(at):
                at(1, sum_runs(1, mid, [2, 3], s1["m2"], None))
                at(1, s1_h)
                at(0, s1_tr)
                at(0, s1_up)

            pipeline(pe, s1_step, EDGE_GROUPS, 1)
            slots_done(pe, 1)

            def s2_tr(g, u, use):
                pe.wait_ge(*s2d["x_in"][u](16 * (use + 1)))
                reuse(pe, s2["xt"], g)
                transposes(ps[u][0], bC[u]).then_inc(s2["tr"].sem, 1)

            def s2_r(g, u, use):
                pe.wait_ge(*s2["xt"](g + 1))
                reuse(pe, s2["rb"], g)
                for j in range(G):
                    pe.matmul(ps[u][3][:, j, :], xt[u][:, j, :], wr[:, :], start=True, stop=False)
                    last = pe.matmul(ps[u][3][:, j, :], ones_row[0:1, 0:P], rows["bl"][0:1, :], start=False, stop=True)
                last.then_inc(s2["r_mm"].sem, 1)

            def s2_l(g, u, use):
                pe.wait_ge(*seg[2]["sums"](SUMS[2] * (g + 1)))
                reuse(pe, s2["y"], g)
                rows_by(ps[u][2], sums[0][u], wl[:, :]).then_inc(s2["l_mm"].sem, 1)

            def s2_step(at):
                at(1, s2_tr)
                at(1, s2_r)
                at(1, sum_runs(2, bA, [1], segd[2]["src_in"], None))
                at(1, s2_l)

            pipeline(pe, s2_step, EDGE_GROUPS, 1)
            slots_done(pe, 2)

            def s3_trs(g, u, use):
                pe.wait_ge(*segd[3]["src_in"][u](16 * G * (use + 1)))
                reuse(pe, s3["rh"], g)
                transposes(ps[u][0], bA[u]).then_inc(s3["trs"].sem, 1)

            def s3_tr(g, u, use):
                pe.wait_ge(*s3d["xd_in"][u](16 * G * (use + 1)))
                reuse(pe, s3["r_tanh"], g)
                transposes(ps[u][1], bC[u]).then_inc(s3["tr"].sem, 1)

            def s3_h(g, u, use):
                pe.wait_ge(*s3["xt"](g + 1))
                pe.wait_ge(*s3["xt3"](g + 1))
                pe.wait_ge(*s3d["attr_in"][u](16 * (use + 1)))
                reuse(pe, s3["yt"], g)
                for j in range(G):
                    pe.matmul(ps[u][2][:, j, :], xt[u][:, j, :], w1a[:, :], start=True, stop=False)
                    pe.matmul(ps[u][2][:, j, :], xt3[u][:, j, :], w1b[:, :], start=False, stop=False)
                    last = pe.matmul(ps[u][2][:, j, :], attr[u][:, tile_edges(j)], w1c[:, :], start=False, stop=True)
                last.then_inc(s3["h_mm"].sem, 1)

            def s3_a2(g, u, use):
                pe.wait_ge(*seg[3]["sums"](SUMS[3] * (g + 1)))
                pe.wait_ge(*s3d["gs_in"][u](16 * (use + 1)))
                pe.matmul(flat(ps[u][3]), w2[:, :], flat(sums[0][u]), start=True, stop=False)
                pe.matmul(flat(ps[u][3]), b2row[:, :], gsum_row[u][:, :], start=False, stop=True).then_inc(s3["a2_mm"].sem, 1)

            def s3_gates(g, u, use):
                pe.wait_ge(*s3["a2"](g + 1))
                x, a = flat(xt3[u]), flat(bB[u])
                pe.matmul(flat(ps[u][1]), wih[:, 0:D], a, start=True, stop=False)
                pe.matmul(flat(ps[u][1]), whh[:, 0:D], x, start=False, stop=True).then_inc(s3["r_mm"].sem, 1)
                pe.matmul(flat(ps[u][0]), whh[:, 2 * D:3 * D], x, start=True, stop=True).then_inc(s3["n_mm"].sem, 1)
                pe.wait_ge(*s3["y"](g + 1))
                pe.matmul(flat(ps[u][2]), wih[:, D:2 * D], a, start=True, stop=False)
                pe.matmul(flat(ps[u][2]), whh[:, D:2 * D], x, start=False, stop=True).then_inc(s3["z_mm"].sem, 1)
                pe.matmul(flat(ps[u][3]), wih[:, 2 * D:3 * D], a, start=True, stop=True).then_inc(s3["in_mm"].sem, 1)

            def s3_tr4(g, u, use):
                pe.wait_ge(*s3["n"](g + 1))
                pe.wait_ge(*s3["yt"](g + 1))
                transposes(ps[u][3], bE2[u]).then_inc(s3["tr4"].sem, 1)

            def s3_step(at):
                at(2, s3_h)
                at(3, s3_gates)
                at(2, sum_runs(3, bE, [3], s3["relu"], s3["x"]))
                at(2, s3_a2)
                at(3, s3_tr4)
                at(1, s3_trs)
                at(1, s3_tr)

            pipeline(pe, s3_step, EDGE_GROUPS, 3)
            slots_done(pe, 3)

        @block.vector
        def _(dve):
            dve.wait_ge(*su["loaded"](16 * CONST_LOADS))
            done = [0]

            def scaled(ins):
                done[0] += 1
                ins.then_inc(su["scaled"].sem, 1)

            s_up, s_out, s3_ = MUL ** -0.5, (2 * MUL) ** -0.5 / 16.0, 3.0 ** 0.5
            scaled(dve.tensor_scalar(wup[:, :], wup[:, :], s_up, None, ALU.mult))
            scaled(dve.tensor_scalar(wo[0][0:64, :], wo[0][0:64, :], s_out, None, ALU.mult))
            scaled(dve.tensor_scalar(wo[0][64:128, :], wo[0][64:128, :], s_out * s3_, None, ALU.mult))
            scaled(dve.tensor_scalar(wo[1][0:32, :], wo[1][0:32, :], s_out * s3_, None, ALU.mult))
            scaled(dve.tensor_scalar(wo[1][32:64, :], wo[1][32:64, :], s_out, None, ALU.mult))
            scaled(dve.tensor_scalar(wo[1][64:128, :], wo[1][64:128, :], s_out, None, ALU.mult))
            scaled(dve.tensor_scalar(m1[:, :], m1[:, :], 0.5, None, ALU.mult))
            scaled(dve.tensor_scalar(m2[0:H1, :], m2[0:H1, :], 0.5, None, ALU.mult))
            scaled(dve.tensor_scalar(mb0h[:, :], mb0[:, :], 0.5, None, ALU.mult))
            scaled(dve.tensor_scalar(mb1h[:, :], mb1[:, :], 0.5, None, ALU.mult))
            scaled(dve.tensor_scalar(gate_bh[:, :], gate_b[:, :], 0.5, None, ALU.mult))
            scaled(dve.tensor_scalar(half_beta2[:, :], rows["beta2"][:, :], 0.5, None, ALU.mult))
            scaled(dve.tensor_tensor(brz[:, :], bih[:, :], bhh[:, :], ALU.add))
            scaled(dve.memset(ones_row[:, :], 1.0))
            scaled(dve.tensor_scalar(m0[:, :], m0[:, :], NB ** 0.5, None, ALU.mult))
            dve.wait_ge(*su["ident"](2))
            scaled(dve.tensor_scalar(center[:, :], ident[:, :], 1.0 / D, None, ALU.subtract))
            scaled(dve.memset(sums[0][1][:, :, :], 0.0))
            scaled(dve.memset(sums[1][1][:, :, :], 0.0))
            for u in range(U):
                scaled(dve.memset(hid1[u][H1:H1 + 1, :], 1.0))
            dve.wait_ge(*su["scaled"](done[0]))
            scaled(dve.tensor_scalar(brz[:, :], brz[:, :], 0.5, None, ALU.mult))
            scaled(dve.tensor_scalar(neg_center[:, :], center[:, :], -1.0, None, ALU.mult))
            scaled(dve.tensor_tensor(center_gamma2[:, :], center[:, :], rows["gamma2"][:, :], ALU.mult))
            assert done[0] == SCALED

            dve.bn_stats(empty_st[:, :], rows["b0"][:, :]).then_inc(su["e_stats"].sem, 1)
            dve.wait_ge(*su["e_stats"](1))
            dve.bn_aggr(empty_mv[:, :], empty_st[:, :]).then_inc(su["e_mv"].sem, 1)
            dve.wait_ge(*su["e_mv"](1))
            dve.tensor_scalar(empty_v[:, :], empty_mv[:, 1:2], LN_EPS, None, ALU.add).then_inc(su["e_add"].sem, 1)
            dve.wait_ge(*su["e_rstd"](1))
            dve.tensor_scalar(empty0[:, :], rows["b0"][:, :], empty_mv[:, 0:1], empty_r[:, 0:1],
                              ALU.subtract, ALU.mult).then_inc(su["e_norm"].sem, 1)
            dve.wait_ge(*su["e_norm"](1))
            dve.tensor_tensor(empty0[:, :], empty0[:, :], rows["gamma0"][:, :], ALU.mult).then_inc(su["e_gamma"].sem, 1)
            dve.wait_ge(*su["e_gamma"](1))
            dve.tensor_tensor(empty0[:, :], empty0[:, :], rows["beta0"][:, :], ALU.add).then_inc(su["empty"].sem, 1)

            dve.tensor_tensor(sq_vec[:, :, :], rhat[:, :, :], rhat[:, :, :], ALU.mult).then_inc(su["sq"].sem, 1)
            dve.wait_ge(*su["sq"](1))
            dve.tensor_reduce(norm[:, :], sq_vec[:, :, :], mybir.AxisListType.X, ALU.add).then_inc(su["ssum"].sem, 1)
            dve.wait_ge(*su["root"](1))
            dve.tensor_scalar(norm[:, :], norm[:, :], 1e-12, None, ALU.add).then_inc(su["root_eps"].sem, 1)
            dve.wait_ge(*su["root_eps"](1))
            dve.reciprocal(norm[:, :], norm[:, :]).then_inc(su["rinv"].sem, 1)
            dve.wait_ge(*su["rinv"](1))
            dve.tensor_tensor(rhat[:, :, :], rhat[:, :, :], norm[:, :].unsqueeze(2).broadcast_to((P, NT, 3)),
                              ALU.mult).then_inc(su["rhat"].sem, 1)

            def edge_clip(g, u, use):
                dve.wait_ge(*pad["r_in"][u](16 * (use + 1)))
                reuse(dve, pa["squared"], g)
                dve.tensor_scalar(e_row[u][:, :], r_row[u][:, :], 0.0, 1.0, ALU.max, ALU.min).then_inc(pa["clipped"].sem, 1)

            def edge_count(g, u, use):
                dve.wait_ge(*pad["dst_in"][u](16 * (use + 1)))
                dve.tensor_tensor(same_row[u][:, :], dst_row[u][0:1, 1:GP + 1], dst_row[u][0:1, 0:GP],
                                  ALU.is_equal).then_inc(pa["same"].sem, 1)
                dve.wait_ge(*pa["same"](g + 1))
                reuse(dve, pa["cnt_mm"], g)
                first = isinstance(g, int) and g == 0
                if not first:
                    dve.wait_ge(*pa["cnt"](g))
                dve.tensor_tensor_scan(cnt_row[u][:, :], same_row[u][:, :], ones_row[:, :],
                                       0.0 if first else cnt_row[1 - u][:, GP - 1:GP], ALU.mult, ALU.add).then_inc(pa["cnt"].sem, 1)

            def edge_emb(g, u, use):
                dve.wait_ge(*pa["exped"](g + 1))
                reuse(dve, pa["h0_mm"], g)
                dve.scalar_tensor_tensor(emb_row[u][:, :], r_row[u][:, :], R_MAX, exp_row[u][:, :],
                                         ALU.is_le, ALU.mult).then_inc(pa["emb"].sem, 1)

            def edge_hidden(n, target, free):
                def stage(g, u, use):
                    dve.wait_ge(*pa[f"h{n}_tanh"](g + 1))
                    dve.wait_ge(*pa[f"h{n}_lin"](g + 1))
                    reuse(dve, pa[free], g)
                    dve.scalar_tensor_tensor(target[u][0:H1, :], hid_t[u][:, :], 1.0, flat(ps[u][0])[0:H1, :],
                                             ALU.add, ALU.mult).then_inc(pa[f"h{n}"].sem, 1)
                return stage

            def edge_gate(g, u, use):
                dve.wait_ge(*pa["gate_tanh"](g + 1))
                dve.tensor_scalar(gates[:, tiles_of(g)], gate_t[u][:, :], 0.5, 0.5, ALU.mult, ALU.add).then_inc(pa["gate"].sem, 1)
                dve.wait_ge(*pa["grow_tanh"](g + 1))
                dve.tensor_scalar(gate_row[u][:, :], gate_row_t[u][:, :], 0.5, 0.5, ALU.mult, ALU.add).then_inc(pa["grow"].sem, 1)
                dve.wait_ge(*pa["grow"](g + 1))
                reuse_dma(dve, pad["gs_st"], u, use)
                first = isinstance(g, int) and g == 0
                if not first:
                    dve.wait_ge(*pa["gsum"](g))
                dve.tensor_tensor_scan(gsum_row[u][:, :], same_row[u][:, :], gate_row[u][:, :],
                                       0.0 if first else gsum_row[1 - u][:, GP - 1:GP], ALU.mult, ALU.add).then_inc(pa["gsum"].sem, 1)

            def edge_count_inv(g, u, use):
                dve.wait_ge(*pa["cnt_mm"](g + 1))
                dve.tensor_scalar(cnt_max[u][:, :], flat(ps[u][3])[:, G:2 * G], 1.0, None, ALU.max).then_inc(pa["cnt_max"].sem, 1)
                dve.wait_ge(*pa["cnt_max"](g + 1))
                dve.reciprocal(count_inv[:, tiles_of(g)], cnt_max[u][:, :]).then_inc(pa["cnt_inv"].sem, 1)

            def edge_step(at):
                at(0, edge_clip)
                at(0, edge_count)
                at(1, edge_hidden(1, hid1, "w_mm"))
                at(0, edge_emb)
                at(0, edge_gate)
                at(0, edge_count_inv)
                at(0, edge_hidden(0, hid0, "h1_mm"))

            pipeline(dve, edge_step, EDGE_GROUPS, 1)
            edge_phase_done(dve)

            def moments(n, source, s, m, ready):
                def stage(g, u, use):
                    dve.wait_ge(*ready(g + 1))
                    for j in range(G):
                        last = dve.bn_stats(stats[n][u][:, j, :], source[u][:, j, :])
                    last.then_inc(s[f"st{m}"].sem, 1)
                    apart(dve, *s[f"st{m}"](g + 1))
                    for j in range(G):
                        last = dve.bn_aggr(mv[n][u][:, j, :], stats[n][u][:, j, :])
                    last.then_inc(s[f"mv{m}"].sem, 1)
                return stage

            def normalize(n, u, target, source, which=0):
                for j in range(G):
                    last = dve.tensor_scalar(target[:, j, :], source[:, j, :], mv[n][u][:, j, 0:1], rstd[n][u][:, which, j:j + 1],
                                             ALU.subtract, ALU.mult)
                return last

            def scale_row(n, u, bank_, row):
                for j in range(G):
                    last = dve.scalar_tensor_tensor(bank_[:, j, :], bank_[:, j, :], mv[n][u][:, j, 0:1], row[:, :],
                                                    ALU.subtract, ALU.mult)
                return last

            def scale_add(n, u, target, source, other):
                for j in range(G):
                    last = dve.scalar_tensor_tensor(target[:, j, :], source[:, j, :], rstd[n][u][:, 0, j:j + 1], other(j),
                                                    ALU.mult, ALU.add)
                return last

            bank = lambda k: [ps[u][k] for u in range(U)]

            def node_x12(g, u, use):
                dve.wait_ge(*nd["rs1"](g + 1))
                reuse_dma(dve, ndd["x1_st"], u, use)
                normalize(0, u, bC[u], bB[u], 0).then_inc(nd["x1"].sem, 1)
                reuse_dma(dve, ndd["x2_st"], u, use)
                reuse(dve, nd["tr"], g)
                reuse(dve, nd["xb"], g)
                normalize(0, u, bD[u], bB[u], 1).then_inc(nd["x2"].sem, 1)

            def node_y(g, u, use):
                dve.wait_ge(*nd["rs2"](g + 1))
                dve.wait_ge(*nd["fg_mm"](g + 1))
                dve.wait_ge(*nd["xb"](g + 1))
                scale_add(1, u, bA2[u], ps[u][0], lambda j: bE[u][:, j, :]).then_inc(nd["y"].sem, 1)

            def node_rh(g, u, use):
                dve.wait_ge(*nd["r_tanh"](g + 1))
                dve.wait_ge(*nd["hn"](g + 1))
                dve.scalar_tensor_tensor(flat(ps[u][3]), flat(gr[u]), 1.0, flat(ps[u][3]), ALU.add, ALU.mult).then_inc(nd["rh"].sem, 1)

            def node_ya(g, u, use):
                dve.wait_ge(*nd["z_tanh"](g + 1))
                dve.wait_ge(*nd["xt3"](g + 1))
                reuse(dve, nd["tr4"], g)
                dve.scalar_tensor_tensor(flat(bG[u]), flat(ps[u][2]), 3.0, flat(xt3[u]), ALU.add, ALU.mult).then_inc(nd["ya"].sem, 1)

            def node_x3(g, u, use):
                dve.wait_ge(*nd["rs3"](g + 1))
                reuse_dma(dve, ndd["x3_st"], u, use)
                reuse(dve, nd["tr3"], g)
                normalize(2, u, bF[u], bA2[u]).then_inc(nd["x3"].sem, 1)

            def node_yb(g, u, use):
                dve.wait_ge(*nd["n"](g + 1))
                reuse(dve, nd["tr4"], g)
                dve.scalar_tensor_tensor(flat(bE2[u]), flat(ps[u][2]), -1.0, flat(gn[u]), ALU.add, ALU.mult).then_inc(nd["yb"].sem, 1)

            def node_step(at):
                at(0, moments(0, bB, nd, 1, nd["y0"]))
                at(1, moments(1, bank(1), nd, 2, nd["rows_mm"]))
                at(3, moments(3, bank(3), nd, 4, nd["tr4"]))
                at(0, node_x12)
                at(1, node_y)
                at(1, moments(2, bA2, nd, 3, nd["y"]))
                at(2, node_rh)
                at(2, node_ya)
                at(1, node_x3)
                at(2, node_yb)

            pipeline(dve, node_step, NODE_GROUPS, 3)
            node_phase_done(dve)

            def select(k, gated=False):
                s, d = seg[k], segd[k]

                def stage(g, u, use):
                    dve.wait_ge(*d["cols_in"][u](16 * (use + 1)))
                    reuse(dve, s["scat"], g)
                    dve.tensor_copy(dst_col[u][:, :], cols[u][:, 0:G]).then_inc(s["dcol"].sem, 1)
                    dve.tensor_tensor(is_mid[u][:, :], cols[u][:, 0:G], cols[u][:, G:2 * G], ALU.is_equal).then_inc(s["mid"].sem, 1)
                    dve.wait_ge(*d["dst_in"][u](16 * (use + 1)))
                    dve.tensor_copy(dst_before[u][:, :], dst_row[u][:, 0:GP:P]).then_inc(s["dbefore"].sem, 1)
                    if gated:
                        dve.tensor_copy(gate_t[u][:, :], gates[:, tiles_of(g)]).then_inc(s3["gcol"].sem, 1)
                    dve.wait_ge(*s["dcol"](g + 1))
                    if gated:
                        dve.wait_ge(*s3["gcol"](g + 1))
                    reuse(dve, s["agg"], g)
                    for j in range(G):
                        last = dve.tensor_scalar(bS[u][:, j, :], dst_row[u][:, 1 + j * P:1 + (j + 1) * P], dst_col[u][:, j:j + 1],
                                                 gate_t[u][:, j:j + 1] if gated else None,
                                                 ALU.is_equal, *([ALU.mult] if gated else []))
                    last.then_inc(s["S"].sem, 1)
                    dve.wait_ge(*s["dbefore"](g + 1))
                    reuse(dve, s["sums"], g, SUMS[k])
                    for j in range(G):
                        last = dve.tensor_scalar(mask[u][:, j, :], dst_row[u][:, 1 + j * P:1 + (j + 1) * P],
                                                 dst_before[u][:, j:j + 1], None, ALU.is_equal)
                    last.then_inc(s["mask"].sem, 1)
                return stage

            def rows_to_write(k):
                def stage(g, u, use):
                    dve.wait_ge(*seg[k]["mid"](g + 1))
                    dve.wait_ge(*seg[k]["dcol"](g + 1))
                    reuse_dma(dve, segd[k]["scattered"], u, use, 16 * G)
                    dve.scalar_tensor_tensor(scat[u][:, :], is_mid[u][:, :], float(SKIP), dst_col[u][:, :],
                                             ALU.mult, ALU.add).then_inc(seg[k]["scat"].sem, 1)
                return stage

            def carry(k, banks, used):
                s = seg[k]
                n = len(banks)

                def stage(g, u, use):
                    dve.wait_ge(*s["agg"](g + 1))
                    dve.wait_ge(*s["mask"](g + 1))
                    reuse(dve, used, g)
                    for j in range(G):
                        for h, b in enumerate(banks):
                            if not (isinstance(g, int) and g == 0 and j == 0):
                                dve.wait_ge(*s["sums"](n * (G * g + j - 1) + h + 1))
                            before = sums[h][u][:, j - 1, P - 1:P] if j else sums[h][1 - u][:, G - 1, P - 1:P]
                            dve.scalar_tensor_tensor(sums[h][u][:, j, :], mask[u][:, j, :], before, ps[u][b][:, j, :],
                                                     ALU.mult, ALU.add).then_inc(s["sums"].sem, 1)
                return stage

            def s0_xb(g, u, use):
                dve.wait_ge(*s0d["xd_in"][u](16 * G * (use + 1)))
                reuse(dve, s0["y"], g)
                dve.tensor_tensor(bD[u][:, :, :], bC[u][:, :, :], over_tiles(rows["beta0"]), ALU.add).then_inc(s0["xb"].sem, 1)

            def s0_f(g, u, use):
                dve.wait_ge(*s0["h_mm"](g + 1))
                dve.tensor_tensor(ps[u][1][:, :, :], ps[u][1][:, :, :], over_tiles(rows["b0"]), ALU.add).then_inc(s0["f"].sem, 1)

            def scaled_by(row, bank_, s):
                def stage(g, u, use):
                    dve.wait_ge(*s["mv1"](g + 1))
                    scale_row(0, u, ps[u][bank_], row).then_inc(s["fg"].sem, 1)
                return stage

            def residual(s, bank_):
                def stage(g, u, use):
                    dve.wait_ge(*s["rs1"](g + 1))
                    dve.wait_ge(*s["fg"](g + 1))
                    dve.wait_ge(*s["xb"](g + 1))
                    scale_add(0, u, bA2[u], ps[u][bank_], lambda j: bD[u][:, j, :]).then_inc(s["y"].sem, 1)
                return stage

            def x_of(k, n, s, m, source, stored):
                def stage(g, u, use):
                    dve.wait_ge(*s[f"rs{m}"](g + 1))
                    reuse_dma(dve, segd[k]["scattered"], u, use, 16 * G)
                    if stored:
                        reuse_dma(dve, stored, u, use)
                    normalize(n, u, bF[u], source[u]).then_inc(s["x"].sem, 1)
                return stage

            def s0_step(at):
                at(1, residual(s0, 1))
                at(1, moments(1, bA2, s0, 2, s0["y"]))
                at(0, select(0))
                at(1, rows_to_write(0))
                at(1, x_of(0, 1, s0, 2, bA2, s0d["x_st"]))
                at(0, carry(0, [0], s0["h_mm"]))
                at(0, s0_f)
                at(0, moments(0, bank(1), s0, 1, s0["f"]))
                at(0, scaled_by(rows["gamma0"], 1, s0))
                at(0, s0_xb)

            pipeline(dve, s0_step, EDGE_GROUPS, 1)
            slots_done(dve, 0)

            def by_four(t, lo, n):
                return t[:, :, lo:lo + n * MUL].rearrange("p j (q m) -> p j q m", m=MUL)

            def s1_messages(g, u, use):
                dve.tensor_copy(rh[u][:, :, :], rhat[:, tiles_of(g), :]).then_inc(s1["rh"].sem, 1)
                wv, up, md = bB[u], ps[u][1], mid[u]
                unit = rh[u][:, :, :].unsqueeze(3).broadcast_to((P, G, 3, MUL))
                dve.wait_ge(*s1["up"](g + 1))
                dve.wait_ge(*s1d["w_in"][u](16 * (use + 1)))
                reuse(dve, seg[1]["agg"], g)
                dve.tensor_tensor(by_four(md, 0, 2), by_four(wv, 0, 2), by_four(up, 0, 1).broadcast_to((P, G, 2, MUL)),
                                  ALU.mult).then_inc(s1["m0b"].sem, 1)
                dve.wait_ge(*s1["rh"](g + 1))
                dve.tensor_tensor(vr[u][:, :, :, :], by_four(up, MUL, 3), unit, ALU.mult).then_inc(s1["vr"].sem, 1)
                dve.wait_ge(*s1["m0b"](g + 1))
                dve.tensor_tensor(by_four(md, 2 * MUL, 3), by_four(md, MUL, 1).broadcast_to((P, G, 3, MUL)), unit,
                                  ALU.mult).then_inc(s1["m1"].sem, 1)
                dve.wait_ge(*s1["vr"](g + 1))
                dve.tensor_tensor(rq[u][:, :, :], vr[u][:, :, 0, :], vr[u][:, :, 1, :], ALU.add).then_inc(s1["vr01"].sem, 1)
                dve.tensor_tensor(by_four(md, 5 * MUL, 3), by_four(wv, 2 * MUL, 1).broadcast_to((P, G, 3, MUL)),
                                  by_four(up, MUL, 3), ALU.mult)
                dve.wait_ge(*s1["vr01"](g + 1))
                dve.tensor_tensor(rq[u][:, :, :], rq[u][:, :, :], vr[u][:, :, 2, :], ALU.add).then_inc(s1["vr012"].sem, 1)
                dve.wait_ge(*s1["vr012"](g + 1))
                dve.wait_ge(*s1["m1"](g + 1))
                dve.tensor_tensor(md[:, :, MUL:2 * MUL], wv[:, :, 3 * MUL:4 * MUL], rq[u][:, :, :], ALU.mult).then_inc(s1["m2"].sem, 1)

            def s1_y(g, u, use):
                dve.wait_ge(*s1["h_mm"](g + 1))
                dve.wait_ge(*s1d["x_in"][u](16 * (use + 1)))
                dve.tensor_tensor(bA2[u][:, :, :], ps[u][0][:, :, :], bC[u][:, :, :], ALU.add).then_inc(s1["y"].sem, 1)

            def s1_step(at):
                at(2, x_of(1, 0, s1, 1, bA2, s1d["x_st"]))
                at(1, carry(1, [2, 3], s1["h_mm"]))
                at(0, select(1))
                at(1, s1_y)
                at(1, moments(0, bA2, s1, 1, s1["y"]))
                at(1, rows_to_write(1))
                at(0, s1_messages)

            pipeline(dve, s1_step, EDGE_GROUPS, 2)
            slots_done(dve, 1)

            def s2_xb(g, u, use):
                dve.wait_ge(*s2d["x_in"][u](16 * (use + 1)))
                reuse(dve, s2["y"], g)
                dve.tensor_tensor(bD[u][:, :, :], bC[u][:, :, :], over_tiles(half_beta2), ALU.add).then_inc(s2["xb"].sem, 1)
                dve.tensor_copy(cinv[u][:, :], count_inv[:, tiles_of(g)]).then_inc(s2["cinv"].sem, 1)

            def s2_f(g, u, use):
                dve.wait_ge(*s2["l_mm"](g + 1))
                dve.wait_ge(*s2["rb"](g + 1))
                dve.wait_ge(*s2["cinv"](g + 1))
                for j in range(G):
                    last = dve.scalar_tensor_tensor(ps[u][2][:, j, :], ps[u][2][:, j, :], cinv[u][:, j:j + 1], bE[u][:, j, :],
                                                    ALU.mult, ALU.add)
                last.then_inc(s2["f"].sem, 1)

            def s2_step(at):
                at(2, s2_xb)
                at(2, s2_f)
                at(1, select(2))
                at(2, moments(0, bank(2), s2, 1, s2["gelu"]))
                at(2, scaled_by(rows["gamma2"], 2, s2))
                at(2, residual(s2, 2))
                at(2, moments(1, bA2, s2, 2, s2["y"]))
                at(1, carry(2, [1], s2["l_mm"]))
                at(2, rows_to_write(2))
                at(2, x_of(2, 1, s2, 2, bA2, None))

            pipeline(dve, s2_step, EDGE_GROUPS, 2)
            slots_done(dve, 2)

            def s3_y(g, u, use):
                dve.wait_ge(*s3["rs1"](g + 1))
                dve.wait_ge(*s3["fg"](g + 1))
                reuse(dve, seg[3]["agg"], g)
                scale_add(0, u, bE[u], ps[u][2], lambda j: rows["ln_b3"][:, :]).then_inc(s3["y"].sem, 1)

            def s3_rh(g, u, use):
                dve.wait_ge(*s3["r_tanh"](g + 1))
                dve.wait_ge(*s3["hn"](g + 1))
                dve.scalar_tensor_tensor(flat(bG[u]), flat(gr[u]), 1.0, flat(ps[u][0]), ALU.add, ALU.mult).then_inc(s3["rh"].sem, 1)

            def s3_ya(g, u, use):
                dve.wait_ge(*s3["z_tanh"](g + 1))
                dve.scalar_tensor_tensor(flat(bD[u]), flat(ps[u][2]), 3.0, flat(xt3[u]), ALU.add, ALU.mult).then_inc(s3["ya"].sem, 1)

            def s3_ni(g, u, use):
                dve.wait_ge(*s3["rh"](g + 1))
                dve.wait_ge(*s3["in_mm"](g + 1))
                dve.scalar_tensor_tensor(flat(ps[u][3]), flat(bG[u]), 0.5, flat(ps[u][3]), ALU.mult, ALU.add).then_inc(s3["ni"].sem, 1)

            def s3_yb(g, u, use):
                dve.wait_ge(*s3["n"](g + 1))
                dve.scalar_tensor_tensor(flat(ps[u][2]), flat(ps[u][2]), -1.0, flat(gn[u]), ALU.add, ALU.mult).then_inc(s3["yb"].sem, 1)

            def s3_yt(g, u, use):
                dve.wait_ge(*s3["ya"](g + 1))
                dve.wait_ge(*s3["yb"](g + 1))
                reuse(dve, s3["tr4"], g)
                dve.tensor_tensor(flat(bE2[u]), flat(bD[u]), flat(ps[u][2]), ALU.subtract).then_inc(s3["yt"].sem, 1)

            def s3_step(at):
                at(4, moments(1, bank(3), s3, 2, s3["tr4"]))
                at(2, select(3, gated=True))
                at(2, moments(0, bank(2), s3, 1, s3["h_mm"]))
                at(2, scaled_by(rows["ln_g3"], 2, s3))
                at(2, s3_y)
                at(3, s3_rh)
                at(4, x_of(3, 1, s3, 2, bank(3), None))
                at(3, s3_ya)
                at(3, s3_ni)
                at(2, carry(3, [3], s3["a2_mm"]))
                at(3, s3_yb)
                at(3, s3_yt)
                at(3, rows_to_write(3))

            pipeline(dve, s3_step, EDGE_GROUPS, 4)
            slots_done(dve, 3)


def kernel(**inputs):
    import numpy as np
    import concourse.bacc as bacc
    from concourse.bass_utils import run_bass_kernel_spmd

    v = {k: np.asarray(a) for k, a in inputs.items()}

    def row(a):
        return np.ascontiguousarray(a.reshape(1, -1))

    def t(a):
        return np.ascontiguousarray(a.T)

    def padded(a, n, fill=0):
        out = np.full((n,) + a.shape[1:], fill, a.dtype)
        out[:a.shape[0]] = a
        return out

    tiles = EDGE_GROUPS * G
    src = padded(v["src"], EDGES_PAD)
    dst = padded(v["dst"], EDGES_PAD, LAST_ROW)
    after = np.concatenate([dst[1:], np.full(1, -1, dst.dtype)])

    def columns(a):
        return a.reshape(EDGE_GROUPS, G, P).transpose(0, 2, 1)

    wup = np.zeros((D, D), np.float32)
    wup[:MUL, :MUL] = v["L1_gnn_W_up0"]
    wo = np.zeros((2 * D, D), np.float32)
    wo[0:2 * MUL, :MUL] = v["L1_gnn_W_out0"]
    for c in range(3):
        wup[MUL + c::3, MUL + MUL * c:MUL + MUL * (c + 1)] = v["L1_gnn_W_up1"]
        wo[MUL * (2 + c):MUL * (3 + c), MUL + c::3] = v["L1_gnn_W_out1"][:MUL]
        wo[MUL * (5 + c):MUL * (6 + c), MUL + c::3] = v["L1_gnn_W_out1"][MUL:]
    attr = padded(v["edge_attr_64"], EDGES_PAD).T
    w1 = v["L3_gnn_W1"]
    arrays = {
        "x": padded(v["x"], NODES_PAD),
        "edge_idx": np.ascontiguousarray(np.concatenate([columns(src), columns(dst)], axis=2)),
        "edge_cols": np.ascontiguousarray(np.concatenate([columns(dst), columns(after)], axis=2)),
        "dst_line": row(np.concatenate([np.full(1, -1, dst.dtype), dst])),
        "edge_vec": np.ascontiguousarray(padded(v["edge_attr_3"], EDGES_PAD).reshape(tiles, P, 3).transpose(1, 0, 2)).reshape(P, tiles * 3),
        "edge_r": row(padded(v["edge_weight"], EDGES_PAD)),
        "attr_t": np.concatenate([attr, np.ones((1, EDGES_PAD), np.float32)]),
        "b0": row(v["L0_gnn_b"]), "gamma0": row(v["L0_gnn_gamma"]), "beta0": row(v["L0_gnn_beta"]), "w0t": t(v["L0_gnn_W"]),
        "wup": wup, "wo": wo, "m0": v["L1_gnn_mlp_w0"], "m1": v["L1_gnn_mlp_w1"],
        "m2": np.concatenate([v["L1_gnn_mlp_w2"], row(v["L1_gnn_mlp_b2"])]),
        "mb0": v["L1_gnn_mlp_b0"].reshape(-1, 1), "mb1": v["L1_gnn_mlp_b1"].reshape(-1, 1),
        "wl": v["L2_gnn_W_l"], "bl": row(v["L2_gnn_b_l"]), "wr": v["L2_gnn_W_r"], "bl_col": v["L2_gnn_b_l"].reshape(-1, 1),
        "gamma2": row(v["L2_gnn_gamma"]), "beta2": row(v["L2_gnn_beta"]),
        "w1ab": w1[:2 * D], "w1c": np.concatenate([w1[2 * D:], row(v["L3_gnn_b1"])]),
        "ln_g3": row(v["L3_gnn_ln_g"]), "ln_b3": row(v["L3_gnn_ln_b"]), "w2": v["L3_gnn_W2"], "b2row": row(v["L3_gnn_b2"]),
        "gate_w": v["L3_gnn_gate_w"], "gate_b": v["L3_gnn_gate_b"].reshape(1, 1),
        "wih": t(v["L3_gnn_W_ih"]), "whh": t(v["L3_gnn_W_hh"]),
        "bih": t(v["L3_gnn_b_ih"].reshape(3, D)), "bhh": t(v["L3_gnn_b_hh"].reshape(3, D)),
    }
    nc = bacc.Bacc("TRN2", target_bir_lowering=False, num_devices=1)
    feeds, aps = {}, {}
    for name, a in arrays.items():
        a = np.ascontiguousarray(a)
        feeds[f"in_{name}"] = a
        aps[name] = nc.dram_tensor(f"in_{name}", a.shape, mybir.dt.from_np(a.dtype), kind="ExternalInput").ap()
    out = nc.dram_tensor("out_0", (NODES_PAD, D), F32, kind="ExternalOutput").ap()
    build(nc, aps, out)
    r = run_bass_kernel_spmd(nc, [feeds], core_ids=[0])
    return r.results[0]["out_0"][:N_NODES]
```

```python
from contextlib import ExitStack

import concourse.bass as bass
from concourse import mybir

F32 = mybir.dt.float32
I32 = mybir.dt.int32
U32 = mybir.dt.uint32
ALU = mybir.AluOpType
ACT = mybir.ActivationFunctionType

P = 128
D = 128
G = 4
GP = G * P
U = 2
N_NODES = 50000
N_EDGES = 25000
NODE_GROUPS = -(-N_NODES // (GP * U)) * U
EDGE_GROUPS = -(-N_EDGES // GP)
NODES_PAD = NODE_GROUPS * GP
EDGES_PAD = EDGE_GROUPS * GP
PER_PART = EDGES_PAD // P
CHUNKS = 7
PER_CHUNK = PER_PART // CHUNKS
assert PER_CHUNK * CHUNKS == PER_PART
HALF_TILES = EDGES_PAD // P // 2
MUL = 32
NB = 8
H1 = 64
ED = 64
R_MAX = 1.0
SIGMA = 1.0 / (NB - 1)
LN_EPS = 1e-5
SKIP = 1 << 20
LAST_ROW = NODES_PAD - 1
BN = 6
SCALED = 26
SUMS = (G, 2 * G, G, G)


class Signal:

    def __init__(self, sem, base):
        self.sem, self.base = sem, base

    def __call__(self, n):
        return self.sem, self.base + n


def build(nc, A, O):
    with ExitStack() as ctx:
        def sb(name, shape, dt=F32):
            return ctx.enter_context(nc.sbuf_tensor(name, shape, dt))

        pool_of_sems = {}

        def signal(name, total):
            sem, base = pool_of_sems.get(name) or (ctx.enter_context(nc.semaphore(name)), 0)
            pool_of_sems[name] = (sem, base + total)
            return Signal(sem, base)

        def uses(groups, u):
            return (groups + U - 1 - u) // U

        def signals(names, total):
            made = {}
            for n in names.split():
                n, _, times = n.partition("*")
                name, _, sem = n.partition("=")
                made[name] = signal(sem or name, total * int(times or 1))
            return made

        def signals_by_buffer(names, groups):
            return {n.partition("*")[0]: [signal(n.partition("*")[0] + str(u), uses(groups, u) * int(n.partition("*")[2] or 1))
                                          for u in range(U)] for n in names.split()}

        def table(name, shape):
            return nc.dram_tensor(name, shape, F32, kind="Internal").ap()

        def pair(name, shape, dt=F32):
            return [sb(f"{name}{u}", shape, dt) for u in range(U)]

        x1_table, x2_table, x3_table = (table(f"x{k}_table", (NODES_PAD, D)) for k in (1, 2, 3))
        x1_slots, x2_slots = (table(f"x{k}_slots", (EDGE_GROUPS, P, G * D)) for k in (1, 2))
        radial_w = table("radial_w", (EDGE_GROUPS, P, G * D))
        gate_sums, gate_line, count_line = (table(n, (1, EDGES_PAD)) for n in ("gate_sums", "gate_line", "count_line"))
        x0_table, out = A["x"], O

        def node_rows(t, g):
            return t.rearrange("(g p j) d -> g p (j d)", p=P, j=G)[g]

        ident = sb("ident", [P, P])
        neg_half = sb("neg_half", [P, 8])
        rows = {}
        for name in ("b0", "gamma0", "beta0", "bl", "gamma2", "beta2", "ln_g3", "ln_b3"):
            rows[name] = sb(f"row_{name}", [P, D])
        half_beta2 = sb("half_beta2", [P, D])
        center = sb("center", [P, P])
        neg_center = sb("neg_center", [P, P])
        center_gamma2 = sb("center_gamma2", [P, P])
        bl_col = sb("bl_col", [D, 1])
        empty0 = sb("empty0", [P, D])
        w0 = sb("w0", [D, D])
        b0_col = sb("b0_col", [D, 1])
        w0_center = sb("w0_center", [D, D])
        b0_center = sb("b0_center", [1, D])
        wup = sb("wup", [D, D])
        wo = [sb(f"wo{h}", [P, D]) for h in range(2)]
        wl = sb("wl", [D, D])
        wr = sb("wr", [D, D])
        w1a = sb("w1a", [D, D])
        w1b = sb("w1b", [D, D])
        w1c = sb("w1c", [ED + 1, D])
        w2 = sb("w2", [D, D])
        b2row = sb("b2row", [1, D])
        wih = sb("wih", [D, 3 * D])
        whh = sb("whh", [D, 3 * D])
        bih = sb("bih", [D, 3])
        bhh = sb("bhh", [D, 3])
        brz = sb("brz", [D, 3])
        m0 = sb("m0", [NB, H1])
        m1 = sb("m1", [H1, H1])
        m2 = sb("m2", [H1 + 1, D])
        mb0 = sb("mb0", [H1, 1])
        mb1 = sb("mb1", [H1, 1])
        mb0h = sb("mb0h", [H1, 1])
        mb1h = sb("mb1h", [H1, 1])
        neg_centers = sb("neg_centers", [NB, 1])
        gate_row = sb("gate_row", [P, ED])
        gate_b = sb("gate_b", [P, 1])
        gate_bh = sb("gate_bh", [P, 1])
        NT = EDGE_GROUPS * G
        rhat = sb("rhat", [P, NT, 3])
        count_inv = sb("count_inv", [P, NT])
        gates = sb("gates", [P, NT])
        empty_st = sb("empty_st", [P, BN])
        empty_mv = sb("empty_mv", [P, 2])
        empty_v = sb("empty_v", [P, 1])
        empty_r = sb("empty_r", [P, 1])
        always = sb("always", [P, 1])
        half = sb("half", [P, NT])
        sq_vec = sb("sq_vec", [P, NT, 3])
        norm = sb("norm", [P, NT])
        ones_row = sb("ones_row", [1, GP])
        dst_own, dst_prev = (sb(n, [P, PER_PART], I32) for n in ("dst_own", "dst_prev"))
        same, goes_on, run_counts, run_gates, gate_part, logits, ones_part, zeros_part = (
            sb(n, [P, PER_PART]) for n in ("same", "goes_on", "run_counts", "run_gates", "gate_part", "logits",
                                           "ones_part", "zeros_part"))
        attr_rows = [sb(f"attr_rows{c}", [P, PER_CHUNK, ED]) for c in range(U)]
        ends = sb("ends", [P, 3])
        ends_row = sb("ends_row", [1, 3, P])
        into_row = sb("into_row", [1, 2, P + 1])
        into = sb("into", [P, 2])
        tile_rows = sb("tile_rows", [HALF_TILES, 2, 2, P])

        bA = pair("bA", [P, G, D])
        bB = pair("bB", [P, G, D])
        bC = pair("bC", [P, G, D])
        bD = pair("bD", [P, G, D])
        bE = pair("bE", [P, G, D])
        bF = pair("bF", [P, G, D])
        bS = pair("bS", [P, G, D])
        bG = pair("bG", [P, G, D])
        bO = pair("bO", [P, G, D])
        gel = pair("gel", [P, G, D])
        square2 = pair("square2_", [P, G, D])
        square4 = pair("square4_", [P, G, D])
        ratio = pair("ratio", [P, G])
        root = pair("root", [P, G])
        bA2 = pair("bA2", [P, G, D])
        bE2 = pair("bE2", [P, G, D])
        xt = pair("xt", [P, G, D])
        xt3 = pair("xt3", [P, G, D])
        gr = pair("gr", [P, G, D])
        gn = pair("gn", [P, G, D])
        vr = pair("vr", [P, G, 3, MUL])
        rh = pair("rh", [P, G, 3])
        cinv = pair("cinv", [P, G])
        gate_t = pair("gate_t", [P, G])
        sq_row = pair("sq_row", [NB, GP])
        exp_row = pair("exp_row", [NB, GP])
        emb_row = pair("emb_row", [NB, GP])
        hid_t = pair("hid_t", [H1, GP])
        hid0 = pair("hid0", [H1, GP])
        hid1 = pair("hid1", [H1 + 1, GP])
        mid = pair("mid", [P, G, 2 * D])
        sums = [pair(f"sums{h}_", [P, G, D]) for h in range(2)]
        NORMS = 4
        stats = [pair(f"stats{n}_", [P, G, BN]) for n in range(NORMS)]
        mv = [pair(f"mv{n}_", [P, G, 2]) for n in range(NORMS)]
        vv = [pair(f"vv{n}_", [P, 2, G]) for n in range(NORMS)]
        rstd = [pair(f"rstd{n}_", [P, 2, G]) for n in range(NORMS)]
        cols = pair("cols", [P, 2 * G], I32)
        mask = pair("mask", [P, G, D])
        idx = pair("idx", [P, 2 * G], I32)
        scat = pair("scat", [P, G], U32)
        is_mid = pair("is_mid", [P, G])
        dst_row = pair("dst_row", [P, GP + 1], I32)
        dst_col = pair("dst_col", [P, G])
        dst_before = pair("dst_before", [P, G])
        attr = pair("attr", [ED + 1, GP])
        r_row = pair("r_row", [NB, GP])
        e_row = pair("e_row", [NB, GP])
        gsum_row = pair("gsum_row", [1, GP])
        shifts = pair("shifts", [P, G])
        rq = pair("rq", [P, G, MUL])

        ps = [[ctx.enter_context(nc.psum_tensor(f"ps{u}{k}", [P, G, D], F32)) for k in range(4)]
              for u in range(U)]

        CONST_TILES = [(t, A[n]) for t, n in (
            (w0, "w0"), (b0_col, "b0_col"), (wup, "wup"), (wl, "wl"), (wr, "wr"), (w1c, "w1c"), (w2, "w2"), (b2row, "b2row"),
            (wih, "wih"), (whh, "whh"), (bih, "bih"), (bhh, "bhh"), (m0, "m0"), (m1, "m1"), (m2, "m2"),
            (mb0, "mb0"), (mb1, "mb1"), (bl_col, "bl_col"))]
        CONST_TILES += [(w1a, A["w1ab"][0:D, :]), (w1b, A["w1ab"][D:2 * D, :]), (wo[0], A["wo"][0:P, :]),
                        (wo[1], A["wo"][P:2 * P, :]), (gate_b, A["gate_b"].broadcast_to((P, 1))),
                        (gate_row, A["gate_w"].broadcast_to((P, ED)))]
        CONST_LOADS = len(rows) + len(CONST_TILES) + 1

        def flat(t):
            return t[:, :, :].rearrange("p j d -> p (j d)")

        def over_tiles(row):
            return row[:, :].unsqueeze(1).broadcast_to((P, G, D))

        def edges_of(g):
            return bass.ds(g * GP, GP)

        def tiles_of(g):
            return bass.ds(g * G, G)

        def tile_edges(j):
            return slice(j * P, (j + 1) * P)

        def reuse(eng, sem, g, each=1, stand=False):
            if isinstance(g, int) and g < U:
                return
            if stand:
                apart(eng, *sem(each * (g - (U - 1))))
            else:
                eng.wait_ge(*sem(each * (g - (U - 1))))

        def pipeline(eng, step, groups, last_lag, first_lag=0):
            def turn_of(turn, steps=range(U)):
                for v in steps:
                    def at(lag, stage):
                        g, u = turn * U + (v - lag), (v - lag) % U
                        if isinstance(g, int) and not 0 <= g < groups:
                            return
                        stage(g, u, turn + (v - lag - u) // U)
                    step(at)
            peeled = 1 - (-last_lag // U)
            for turn in range(first_lag // U, peeled):
                turn_of(turn)
            ends = groups // U + first_lag // U
            with eng.Fori(peeled, ends) as turn:
                turn_of(turn)
            for turn in range(ends, -(-(groups + last_lag) // U)):
                turn_of(turn)

        def reuse_dma(eng, sem, u, use, each=16, stand=False):
            if isinstance(use, int) and use == 0:
                return
            if stand:
                apart(eng, *sem[u](each * use))
            else:
                eng.wait_ge(*sem[u](each * use))

        su = signals("go loaded consts ident scaled e_stats e_mv e_add e_rstd e_norm e_gamma empty sq ssum root "
                                       "root_eps rinv rhat", 0)
        T_ATTR = " ".join(f"t_attr_in{c}=r_in{c}*{16 * uses(CHUNKS, c)}" for c in range(U)) + " "
        su.update(signals("w0_mm=h_mm w0_center=fg*2 " + T_ATTR + "t_dst_in=dst_in0*32 t_stored=w_st0*48 "
                          "t_tiles_in=w_st1*64 t_same=mid " + f"t_weighted=emb*{CHUNKS} t_logit=n_mm*{CHUNKS} " + "t_tanh=r_tanh t_gate=hn t_scan=st1*3 "
                          "t_ends=st2 t_ends_mm=tr t_ends_row=st3 t_into=mv1*2 t_into_mm=tr3 t_into_col=mv2 t_gsum=y "
                          "t_count=x1 t_count_max=x2 t_count_inv=x3 t_tiles_mm=tr4 t_columns=xt*2", 1))
        E, N = EDGE_GROUPS, NODE_GROUPS
        pa = signals("clipped squared exped emb h0_mm h0_tanh h0_lin h0 h1_mm h1_tanh h1_lin h1 w_mm w_copied", E)
        pad = signals_by_buffer("r_in*16 w_st*16", E)
        nd = signals("y0 st1 mv1 var1 rs1 v_rstd ratio x1 x2 tr xt f_mm gelu rows_mm fg_mm sq2 mv2 var2 rs2 xb y st3 mv3 var3 rs3 x3 "
                                       "tr3 xt3 r_mm z_mm n_mm r_tanh z_tanh hn rh n ya yb tr4 sq4 mv4 var4 rs4 x", N)
        ndd = signals_by_buffer("x_in*16 x1_st*16 x2_st*16 x3_st*16 x_st*16", N)
        seg = [signals(f"dcol dbefore mid scat S mask agg sums*{SUMS[k]}", E) for k in range(4)]
        segd = [signals_by_buffer(f"idx_in*16 cols_in*16 dst_in*16 src_in*{16 * G} scattered*{16 * G}", E) for k in range(4)]
        s0 = signals("h_mm sq2 fg mv1 var1 rs1 xb y st2 mv2 var2 rs2 shift x", E)
        s0d = signals_by_buffer(f"xd_in*{16 * G} x_st*16", E)
        s1 = signals("tr xt up rh m0b m1 vr vr01 vr012 m2 h_mm y st1 mv1 var1 rs1 shift x", E)
        s1d = signals_by_buffer("w_in*16 x_in*16 x_st*16", E)
        s2 = signals("tr xt l_mm r_mm rb f gelu cinv st1 mv1 var1 rs1 fg xb y st2 mv2 var2 rs2 shift x", E)
        s2d = signals_by_buffer("x_in*16", E)
        s3 = signals("trs tr xt xt3 h_mm st1 mv1 var1 rs1 fg y relu gcol a2_mm a2 r_mm z_mm in_mm n_mm "
                                       "r_tanh z_tanh hn rh ni n ya yb yt tr4 st2 mv2 var2 rs2 shift x", E)
        s3d = signals_by_buffer(f"xd_in*{16 * G} attr_in*16 gs_in*16", E)

        def apart(eng, sem, value):
            value = value if isinstance(value, int) else eng.to_reg(value)
            eng.wait_ge(*su["go"](1))
            eng.wait_ge(sem, value)

        def all_of(eng, by_buffer, groups, each=16):
            for u in range(U):
                eng.wait_ge(*by_buffer[u](each * uses(groups, u)))

        def tables_done(eng):
            eng.wait_ge(*su["t_columns"](2))
            eng.wait_ge(*su["w0_center"](2))

        def node_phase_done(eng):
            for q in (ndd["x1_st"], ndd["x2_st"], ndd["x3_st"], ndd["x_st"]):
                all_of(eng, q, N)

        def slots_done(eng, k):
            all_of(eng, segd[k]["scattered"], E, 16 * G)
            if k == 0:
                all_of(eng, s0d["x_st"], E)
                all_of(eng, pad["w_st"], E)
            if k == 1:
                all_of(eng, s1d["x_st"], E)

        block = ctx.enter_context(nc.Block())

        @block.sync
        def _(sp):
            for t, source in CONST_TILES:
                sp.dma_start(t[:, :], source).then_inc(su["loaded"].sem, 16)
            sp.dma_start(rhat[:, :, :].rearrange("p t c -> p (t c)"), A["edge_vec"]).then_inc(su["loaded"].sem, 16)

            by_part = lambda line: line.rearrange("o (p t) -> (o p) t", p=P)
            by_tile = lambda line, h: line.rearrange("o (t e) -> (o t) e", e=P)[h * HALF_TILES:(h + 1) * HALF_TILES]
            sp.dma_start(dst_own[:, :], by_part(A["dst_line"][:, 1:EDGES_PAD + 1])).then_inc(su["t_dst_in"].sem, 16)
            sp.dma_start(dst_prev[:, :], by_part(A["dst_line"][:, 0:EDGES_PAD])).then_inc(su["t_dst_in"].sem, 16)
            for c in range(CHUNKS):
                if c >= U:
                    sp.wait_ge(*su["t_logit"](c - 1))
                sp.dma_start(attr_rows[c % U][:, :, :], A["attr"].rearrange("(p t) k -> p t k", p=P)
                             [:, c * PER_CHUNK:(c + 1) * PER_CHUNK, :]).then_inc(su[f"t_attr_in{c % U}"].sem, 16)
            sp.wait_ge(*su["t_gsum"](1))
            sp.dma_start(by_part(gate_sums), run_gates[:, :]).then_inc(su["t_stored"].sem, 16)
            sp.dma_start(by_part(gate_line), gate_part[:, :]).then_inc(su["t_stored"].sem, 16)
            sp.wait_ge(*su["t_count_inv"](1))
            sp.dma_start(by_part(count_line), run_counts[:, :]).then_inc(su["t_stored"].sem, 16)
            sp.wait_ge(*su["t_stored"](48))
            for h in range(2):
                sp.dma_start(tile_rows[:, 0, h, :], by_tile(gate_line, h)).then_inc(su["t_tiles_in"].sem, 16)
                sp.dma_start(tile_rows[:, 1, h, :], by_tile(count_line, h)).then_inc(su["t_tiles_in"].sem, 16)

            tables_done(sp)

            def node_load(g, u, use):
                reuse(sp, nd["y0"], g)
                sp.dma_start(flat(bA[u]), node_rows(x0_table, g)).then_inc(ndd["x_in"][u].sem, 16)

            def node_store(ready, table_, buf, done):
                def stage(g, u, use):
                    sp.wait_ge(*ready(g + 1))
                    sp.dma_start(node_rows(table_, g), flat(buf[u])).then_inc(done[u].sem, 16)
                return stage

            def node_step(at):
                at(-2, node_load)
                at(2, node_store(nd["x3"], x3_table, bF, ndd["x3_st"]))
                at(4, node_store(nd["x"], out, bO, ndd["x_st"]))
                at(0, node_store(nd["x1"], x1_table, bC, ndd["x1_st"]))
                at(0, node_store(nd["x2"], x2_table, bD, ndd["x2_st"]))

            pipeline(sp, node_step, NODE_GROUPS, 4, -2)
            node_phase_done(sp)

            def idx_load(k):
                def stage(g, u, use):
                    reuse_dma(sp, segd[k]["src_in"], u, use, 16 * G, stand=True)
                    if k in (0, 3):
                        reuse_dma(sp, (s0d if k == 0 else s3d)["xd_in"], u, use, 16 * G, stand=True)
                    sp.dma_start(idx[u][:, :], A["edge_idx"][g]).then_inc(segd[k]["idx_in"][u].sem, 16)
                return stage

            def dst_load(k):
                def stage(g, u, use):
                    reuse(sp, seg[k]["mid"], g, stand=True)
                    sp.dma_start(cols[u][:, :], A["edge_cols"][g]).then_inc(segd[k]["cols_in"][u].sem, 16)
                    reuse(sp, seg[k]["mask"], g, stand=True)
                    sp.dma_start(dst_row[u][:, :], A["dst_line"][:, bass.ds(g * GP, GP + 1)]
                                 .broadcast_to((P, GP + 1))).then_inc(segd[k]["dst_in"][u].sem, 16)
                return stage

            def slots_store(ready, slots, done):
                def stage(g, u, use):
                    sp.wait_ge(*ready(g + 1))
                    sp.dma_start(slots[g], flat(bF[u])).then_inc(done[u].sem, 16)
                return stage

            def radius_load(g, u, use):
                reuse(sp, pa["emb"], g)
                sp.dma_start(r_row[u][:, :], A["edge_r"][:, edges_of(g)].broadcast_to((NB, GP))).then_inc(pad["r_in"][u].sem, 16)

            def radial_store(g, u, use):
                sp.wait_ge(*pa["w_copied"](g + 1))
                sp.dma_start(radial_w[g], flat(bB[u])).then_inc(pad["w_st"][u].sem, 16)

            def s0_step(at):
                at(-1, idx_load(0))
                at(-1, radius_load)
                at(0, dst_load(0))
                at(1, radial_store)
                at(2, slots_store(s0["x"], x1_slots, s0d["x_st"]))

            pipeline(sp, s0_step, EDGE_GROUPS, 2, -1)
            slots_done(sp, 0)

            def s1_w_load(g, u, use):
                reuse(sp, s1["m2"], g)
                sp.dma_start(flat(bB[u]), radial_w[g]).then_inc(s1d["w_in"][u].sem, 16)

            def s1_x_load(g, u, use):
                reuse(sp, s1["y"], g)
                sp.dma_start(flat(bC[u]), x1_slots[g]).then_inc(s1d["x_in"][u].sem, 16)

            def s1_step(at):
                at(-2, idx_load(1))
                at(0, dst_load(1))
                at(0, s1_w_load)
                at(1, s1_x_load)
                at(3, slots_store(s1["x"], x2_slots, s1d["x_st"]))

            pipeline(sp, s1_step, EDGE_GROUPS, 3, -2)
            slots_done(sp, 1)

            def s2_load(g, u, use):
                reuse(sp, s2["tr"], g, stand=True)
                reuse(sp, s2["xb"], g)
                sp.dma_start(flat(bC[u]), x2_slots[g]).then_inc(s2d["x_in"][u].sem, 16)

            def s2_step(at):
                at(-1, idx_load(2))
                at(0, dst_load(2))
                at(0, s2_load)

            pipeline(sp, s2_step, EDGE_GROUPS, 0, -1)
            slots_done(sp, 2)

            def s3_load(g, u, use):
                reuse(sp, s3["h_mm"], g)
                sp.dma_start(attr[u][:, :], A["attr_t"][:, edges_of(g)]).then_inc(s3d["attr_in"][u].sem, 16)
                reuse(sp, s3["a2_mm"], g)
                sp.dma_start(gsum_row[u][0:1, :], gate_sums[:, edges_of(g)]).then_inc(s3d["gs_in"][u].sem, 16)

            def s3_step(at):
                at(-1, idx_load(3))
                at(1, dst_load(3))
                at(1, s3_load)

            pipeline(sp, s3_step, EDGE_GROUPS, 1, -1)
            slots_done(sp, 3)

        @block.gpsimd
        def _(pool):
            pool.memset(always[:, :], 0.0).then_inc(su["go"].sem, 1)
            pool.memset(neg_half[:, :], -0.5).then_inc(su["consts"].sem, 1)
            pool.memset(half[:, :], 0.5).then_inc(su["consts"].sem, 1)
            pool.memset(ident[:, :], 0.0).then_inc(su["ident"].sem, 1)
            pool.wait_ge(*su["ident"](1))
            pool.affine_select(out=ident[:, :], in_=ident[:, :], compare_op=ALU.not_equal, fill=1.0, base=0,
                               pattern=[[-1, P]], channel_multiplier=1).then_inc(su["ident"].sem, 1)
            pool.iota(neg_centers[:, :], pattern=[[0, 1]], base=0, channel_multiplier=-1,
                      allow_small_or_imprecise_dtypes=True).then_inc(su["consts"].sem, 1)
            pool.wait_ge(*su["consts"](2))
            pool.wait_ge(*su["e_add"](1))
            pool.tensor_tensor(empty_r[:, :], empty_v[:, :], neg_half[:, 0:1], ALU.pow).then_inc(su["e_rstd"].sem, 1)
            pool.wait_ge(*su["ssum"](1))
            pool.tensor_tensor(norm[:, :], norm[:, :], half[:, :], ALU.pow).then_inc(su["root"].sem, 1)

            def rsqrt(n, s, m, mult, add):
                def stage(g, u, use):
                    apart(pool, *s[f"mv{m}"](g + 1))
                    pool.tensor_scalar(vv[n][u][:, 0, :], mv[n][u][:, :, 1], mult, add, ALU.mult, ALU.add).then_inc(s[f"var{m}"].sem, 1)
                    pool.wait_ge(*s[f"var{m}"](g + 1))
                    pool.tensor_tensor(rstd[n][u][:, 0, :], vv[n][u][:, 0, :], neg_half[:, 0:G], ALU.pow).then_inc(s[f"rs{m}"].sem, 1)
                return stage

            tables_done(pool)

            pool.wait_ge(*su["empty"](1))

            def node_y0(g, u, use):
                pool.wait_ge(*ndd["x_in"][u](16 * (use + 1)))
                reuse(pool, nd["x1"], g)
                pool.tensor_tensor(bB[u][:, :, :], bA[u][:, :, :], over_tiles(empty0), ALU.add).then_inc(nd["y0"].sem, 1)

            def node_rs1(g, u, use):
                apart(pool, *nd["mv1"](g + 1))
                pool.tensor_scalar(vv[0][u][:, 0, :], mv[0][u][:, :, 1], 1.0, LN_EPS, ALU.mult, ALU.add)
                pool.tensor_scalar(vv[0][u][:, 1, :], mv[0][u][:, :, 1], 1.0 + LN_EPS, LN_EPS * LN_EPS,
                                   ALU.mult, ALU.add).then_inc(nd["var1"].sem, 1)
                pool.wait_ge(*nd["var1"](g + 1))
                pool.tensor_tensor(rstd[0][u][:, :, :], vv[0][u][:, :, :],
                                   neg_half[:, :].rearrange("p (a b) -> p a b", a=2), ALU.pow).then_inc(nd["rs1"].sem, 1)

            def node_xb(g, u, use):
                pool.wait_ge(*nd["x2"](g + 1))
                reuse(pool, nd["y"], g)
                pool.tensor_tensor(bE[u][:, :, :], bD[u][:, :, :], over_tiles(half_beta2), ALU.add).then_inc(nd["xb"].sem, 1)

            def node_step(at):
                at(1, node_xb)
                at(-1, node_y0)
                at(0, node_rs1)
                at(4, rsqrt(3, nd, 4, 1.0 / D, LN_EPS * 4.0))
                at(2, rsqrt(2, nd, 3, 1.0, LN_EPS / 4.0))
                at(1, rsqrt(1, nd, 2, 4.0 / D, 4.0 * LN_EPS))

            pipeline(pool, node_step, NODE_GROUPS, 4, -1)
            node_phase_done(pool)

            def gather(table_, buf, col, done, u, tiles=range(G)):
                for j in tiles:
                    pool.indirect_dma_start(
                        out=buf[u][:, j, :], out_offset=None, in_=table_,
                        in_offset=bass.IndirectOffsetOnAxis(ap=idx[u][:, col + j:col + j + 1].bitcast(U32), axis=0),
                    ).then_inc(done[u].sem, 16)

            def gather_src(k, table_, free):
                def stage(g, u, use):
                    apart(pool, *segd[k]["idx_in"][u](16 * (use + 1)))
                    reuse(pool, free, g, stand=True)
                    gather(table_, bA, 0, segd[k]["src_in"], u)
                return stage

            def gather_dst(table_, free, done, tiles=range(G)):
                def stage(g, u, use):
                    if tiles[0] == 0:
                        reuse(pool, free, g, stand=True)
                    gather(table_, bC, G, done, u, tiles)
                return stage

            def scatter(k, table_, x_ready, tiles=range(G)):
                def stage(g, u, use):
                    if tiles[0] == 0:
                        apart(pool, *x_ready(g + 1))
                    for j in tiles:
                        pool.indirect_dma_start(
                            out=table_, out_offset=bass.IndirectOffsetOnAxis(ap=scat[u][:, j:j + 1], axis=0),
                            in_=bF[u][:, j, :], in_offset=None, bounds_check=LAST_ROW, oob_is_err=False,
                        ).then_inc(segd[k]["scattered"][u].sem, 16)
                return stage

            def s0_step(at):
                at(0, gather_src(0, x0_table, seg[0]["agg"]))
                at(0, gather_dst(x0_table, s0["xb"], s0d["xd_in"], range(1)))
                at(2, rsqrt(1, s0, 2, 1.0, LN_EPS))
                at(0, gather_dst(x0_table, s0["xb"], s0d["xd_in"], range(1, G)))
                at(2, scatter(0, x1_table, s0["x"]))
                at(1, rsqrt(0, s0, 1, 1.0 / D, LN_EPS))

            pipeline(pool, s0_step, EDGE_GROUPS, 2)
            slots_done(pool, 0)

            def s1_step(at):
                at(3, rsqrt(0, s1, 1, 1.0, LN_EPS))
                at(-1, gather_src(1, x1_table, s1["tr"]))
                at(3, scatter(1, x2_table, s1["x"]))

            pipeline(pool, s1_step, EDGE_GROUPS, 3, -1)
            slots_done(pool, 1)

            def s2_step(at):
                at(3, rsqrt(1, s2, 2, 1.0, LN_EPS / 4.0))
                at(0, gather_src(2, x2_table, seg[2]["agg"]))
                at(2, rsqrt(0, s2, 1, 4.0, 4.0 * LN_EPS))
                at(3, scatter(2, x3_table, s2["x"]))

            pipeline(pool, s2_step, EDGE_GROUPS, 3)
            slots_done(pool, 2)

            def s3_step(at):
                at(0, gather_src(3, x3_table, s3["trs"]))
                at(4, rsqrt(1, s3, 2, 1.0, 4.0 * LN_EPS))
                at(2, rsqrt(0, s3, 1, 1.0, LN_EPS))
                at(0, gather_dst(x3_table, s3["tr"], s3d["xd_in"]))
                at(4, scatter(3, out, s3["x"]))

            pipeline(pool, s3_step, EDGE_GROUPS, 4)
            slots_done(pool, 3)

        @block.scalar
        def _(act):
            for name in rows:
                act.dma_start(rows[name][:, :], A[name].broadcast_to((P, D))).then_inc(su["loaded"].sem, 16)
            act.wait_ge(*su["loaded"](16 * CONST_LOADS))
            act.wait_ge(*su["consts"](3))
            act.wait_ge(*su["scaled"](SCALED))

            act.wait_ge(*su["t_logit"](CHUNKS))
            act.activation(gate_part[:, :], logits[:, :], ACT.Tanh, bias=gate_bh[:, 0:1], scale=0.5).then_inc(su["t_tanh"].sem, 1)

            tables_done(act)

            def node_gates(g, u, use):
                act.wait_ge(*nd["r_mm"](g + 1))
                reuse(act, nd["rh"], g)
                act.activation(flat(gr[u]), flat(ps[u][1]), ACT.Tanh, bias=brz[:, 0:1], scale=0.5).then_inc(nd["r_tanh"].sem, 1)
                act.wait_ge(*nd["n_mm"](g + 1))
                act.activation(flat(ps[u][3]), flat(ps[u][3]), ACT.Identity, bias=bhh[:, 2:3]).then_inc(nd["hn"].sem, 1)

            def node_gate_z(g, u, use):
                act.wait_ge(*nd["z_mm"](g + 1))
                act.activation(flat(ps[u][2]), flat(ps[u][2]), ACT.Tanh, bias=brz[:, 1:2], scale=0.5).then_inc(nd["z_tanh"].sem, 1)

            def node_xt(g, u, use):
                act.wait_ge(*nd["tr"](g + 1))
                reuse(act, nd["f_mm"], g)
                act.copy(flat(xt[u]), flat(ps[u][0])).then_inc(nd["xt"].sem, 1)

            def node_x(g, u, use):
                act.wait_ge(*nd["rs4"](g + 1))
                reuse_dma(act, ndd["x_st"], u, use)
                for j in range(G):
                    last = act.activation(bO[u][:, j, :], ps[u][3][:, j, :], ACT.Copy, scale=rstd[3][u][:, 0, j:j + 1])
                last.then_inc(nd["x"].sem, 1)

            def node_x2(g, u, use):
                act.wait_ge(*nd["ratio"](g + 1))
                act.wait_ge(*nd["x1"](g + 1))
                reuse_dma(act, ndd["x2_st"], u, use)
                reuse(act, nd["tr"], g)
                reuse(act, nd["xb"], g)
                for j in range(G):
                    last = act.activation(bD[u][:, j, :], bC[u][:, j, :], ACT.Copy, scale=ratio[u][:, j:j + 1])
                last.then_inc(nd["x2"].sem, 1)

            def x_of(n, s, m, k, source, stored):
                def stage(g, u, use):
                    act.wait_ge(*s["shift"](g + 1))
                    reuse_dma(act, segd[k]["scattered"], u, use, 16 * G)
                    if stored:
                        reuse_dma(act, stored, u, use)
                    for j in range(G):
                        last = act.activation(bF[u][:, j, :], source[u][:, j, :], ACT.Identity, bias=shifts[u][:, j:j + 1],
                                              scale=rstd[n][u][:, 0, j:j + 1])
                    last.then_inc(s["x"].sem, 1)
                return stage

            def square_of(source, target, ready, done, free):
                def stage(g, u, use):
                    act.wait_ge(*ready(g + 1))
                    reuse(act, free, g)
                    act.activation(flat(target[u]), flat(ps[u][source]), ACT.Square).then_inc(done.sem, 1)
                return stage

            def node_gelu(g, u, use):
                act.wait_ge(*nd["f_mm"](g + 1))
                reuse(act, nd["fg_mm"], g)
                act.activation(flat(gel[u]), flat(ps[u][0]), ACT.Gelu, bias=bl_col[:, 0:1]).then_inc(nd["gelu"].sem, 1)

            def node_n(g, u, use):
                act.wait_ge(*nd["rh"](g + 1))
                reuse(act, nd["yb"], g)
                act.activation(flat(gn[u]), flat(ps[u][3]), ACT.Tanh, bias=bih[:, 2:3], scale=0.5).then_inc(nd["n"].sem, 1)

            def node_xt3(g, u, use):
                act.wait_ge(*nd["tr3"](g + 1))
                reuse(act, nd["ya"], g)
                act.copy(flat(xt3[u]), flat(ps[u][1])).then_inc(nd["xt3"].sem, 1)

            def node_step(at):
                at(3, node_gates)
                at(1, node_gelu)
                at(3, node_gate_z)
                at(3, node_n)
                at(1, square_of(1, square2, nd["rows_mm"], nd["sq2"], nd["mv2"]))
                at(0, node_x2)
                at(4, node_x)
                at(2, node_xt3)
                at(0, node_xt)
                at(3, square_of(3, square4, nd["tr4"], nd["sq4"], nd["mv4"]))

            pipeline(act, node_step, NODE_GROUPS, 4)
            node_phase_done(act)

            def radial_square(g, u, use):
                act.wait_ge(*pa["clipped"](g + 1))
                reuse(act, pa["exped"], g)
                act.activation(sq_row[u][:, :], e_row[u][:, :], ACT.Square, bias=neg_centers[:, 0:1],
                               scale=1.0 / SIGMA).then_inc(pa["squared"].sem, 1)

            def radial_exp(g, u, use):
                act.wait_ge(*pa["squared"](g + 1))
                reuse(act, pa["emb"], g)
                act.activation(exp_row[u][:, :], sq_row[u][:, :], ACT.Exp, scale=-0.5).then_inc(pa["exped"].sem, 1)

            def radial_hidden(n, bias_half, bias):
                def stage(g, u, use):
                    act.wait_ge(*pa[f"h{n}_mm"](g + 1))
                    if n == 0:
                        reuse(act, pa["h1"], g)
                    h = flat(ps[u][2])[0:H1, :]
                    act.activation(hid_t[u][:, :], h, ACT.Tanh, bias=bias_half[:, 0:1], scale=0.5).then_inc(pa[f"h{n}_tanh"].sem, 1)
                    act.activation(h, h, ACT.Identity, bias=bias[:, 0:1]).then_inc(pa[f"h{n}_lin"].sem, 1)
                return stage

            def radial_copy(g, u, use):
                act.wait_ge(*pa["w_mm"](g + 1))
                reuse_dma(act, pad["w_st"], u, use)
                act.copy(flat(bB[u]), flat(ps[u][3])).then_inc(pa["w_copied"].sem, 1)

            def s0_step(at):
                at(0, radial_square)
                at(0, radial_exp)
                at(0, radial_hidden(0, mb0h, mb0))
                at(2, x_of(1, s0, 2, 0, bA2, s0d["x_st"]))
                at(1, square_of(1, square2, s0["h_mm"], s0["sq2"], s0["mv1"]))
                at(0, radial_hidden(1, mb1h, mb1))
                at(0, radial_copy)

            pipeline(act, s0_step, EDGE_GROUPS, 2)
            slots_done(act, 0)

            def copy_out(source, target, ready, done, free):
                def stage(g, u, use):
                    act.wait_ge(*ready(g + 1))
                    reuse(act, free, g)
                    act.copy(flat(target[u]), flat(ps[u][source])).then_inc(done.sem, 1)
                return stage

            def s1_step(at):
                at(3, x_of(0, s1, 1, 1, bA2, s1d["x_st"]))
                at(0, copy_out(0, xt, s1["tr"], s1["xt"], s1["up"]))

            pipeline(act, s1_step, EDGE_GROUPS, 3)
            slots_done(act, 1)

            def s2_gelu(g, u, use):
                act.wait_ge(*s2["f"](g + 1))
                act.activation(flat(ps[u][2]), flat(ps[u][2]), ACT.Gelu).then_inc(s2["gelu"].sem, 1)

            def s2_step(at):
                at(1, copy_out(0, xt, s2["tr"], s2["xt"], s2["r_mm"]))
                at(2, s2_gelu)
                at(3, x_of(1, s2, 2, 2, bA2, None))
                at(1, copy_out(3, bE, s2["r_mm"], s2["rb"], s2["f"]))

            pipeline(act, s2_step, EDGE_GROUPS, 3)
            slots_done(act, 2)

            def s3_relu(g, u, use):
                act.wait_ge(*s3["y"](g + 1))
                act.activation(flat(bE[u]), flat(bE[u]), ACT.Relu).then_inc(s3["relu"].sem, 1)

            def s3_gates(g, u, use):
                act.wait_ge(*s3["r_mm"](g + 1))
                reuse(act, s3["rh"], g)
                act.activation(flat(gr[u]), flat(ps[u][1]), ACT.Tanh, bias=brz[:, 0:1], scale=0.5).then_inc(s3["r_tanh"].sem, 1)
                act.wait_ge(*s3["n_mm"](g + 1))
                act.activation(flat(ps[u][0]), flat(ps[u][0]), ACT.Identity, bias=bhh[:, 2:3]).then_inc(s3["hn"].sem, 1)

            def s3_z(g, u, use):
                act.wait_ge(*s3["z_mm"](g + 1))
                act.activation(flat(ps[u][2]), flat(ps[u][2]), ACT.Tanh, bias=brz[:, 1:2], scale=0.5).then_inc(s3["z_tanh"].sem, 1)

            def s3_n(g, u, use):
                act.wait_ge(*s3["ni"](g + 1))
                reuse(act, s3["yb"], g)
                act.activation(flat(gn[u]), flat(ps[u][3]), ACT.Tanh, bias=bih[:, 2:3]).then_inc(s3["n"].sem, 1)

            def s3_step(at):
                at(3, s3_gates)
                at(4, x_of(1, s3, 2, 3, [ps[u][3] for u in range(U)], None))
                at(3, s3_z)
                at(2, s3_relu)
                at(3, s3_n)
                at(1, copy_out(0, xt, s3["trs"], s3["xt"], s3["h_mm"]))
                at(1, copy_out(1, xt3, s3["tr"], s3["xt3"], s3["ya"]))
                at(2, copy_out(3, bB, s3["a2_mm"], s3["a2"], s3["in_mm"]))

            pipeline(act, s3_step, EDGE_GROUPS, 4)
            slots_done(act, 3)

        @block.tensor
        def _(pe):
            pe.wait_ge(*su["loaded"](16 * CONST_LOADS))
            pe.wait_ge(*su["ident"](2))
            pe.wait_ge(*su["scaled"](SCALED))

            def transposes(target, source):
                for j in range(G):
                    last = pe.transpose(target[:, j, :], source[:, j, :], ident[:, :])
                return last

            def rows_by(target, source_t, weights, start=True, stop=True):
                for j in range(G):
                    last = pe.matmul(target[:, j, :], source_t[:, j, :], weights, start=start, stop=stop)
                return last

            pe.matmul(ps[0][0][:, 0, :], w0[:, :], center[:, :], start=True, stop=True)
            pe.matmul(ps[0][1][0:1, 0, :], b0_col[:, :], center[:, :], start=True, stop=True).then_inc(su["w0_mm"].sem, 1)

            pe.wait_ge(*su["t_ends"](1))
            for n in range(3):
                last = pe.matmul(ps[0][2][0:1, n, :], ends[:, n:n + 1], ident[:, :], start=True, stop=True)
            last.then_inc(su["t_ends_mm"].sem, 1)
            pe.wait_ge(*su["t_into"](2))
            for n in range(2):
                last = pe.matmul(ps[0][3][:, 0, n:n + 1], into_row[0:1, n, 0:P], ones_row[0:1, 0:1], start=True, stop=True)
            last.then_inc(su["t_into_mm"].sem, 1)
            pe.wait_ge(*su["t_tiles_in"](64))
            for n in range(2):
                for h in range(2):
                    last = pe.transpose(ps[1][n][:, h, 0:HALF_TILES], tile_rows[:, n, h, :], ident[0:HALF_TILES, 0:HALF_TILES])
            last.then_inc(su["t_tiles_mm"].sem, 1)

            tables_done(pe)

            def node_tr4(g, u, use):
                pe.wait_ge(*nd["ya"](g + 1))
                pe.wait_ge(*nd["yb"](g + 1))
                pe.wait_ge(*nd["n"](g + 1))
                for j in range(G):
                    pe.matmul(ps[u][3][:, j, :], bG[u][:, j, :], center[:, :], start=True, stop=False)
                    last = pe.matmul(ps[u][3][:, j, :], bE2[u][:, j, :], neg_center[:, :], start=False, stop=True)
                last.then_inc(nd["tr4"].sem, 1)

            def node_gates(g, u, use):
                pe.wait_ge(*nd["xt3"](g + 1))
                pe.matmul(flat(ps[u][1]), whh[:, 0:D], flat(xt3[u]), start=True, stop=True).then_inc(nd["r_mm"].sem, 1)
                reuse(pe, nd["x"], g)
                pe.matmul(flat(ps[u][3]), whh[:, 2 * D:3 * D], flat(xt3[u]), start=True, stop=True).then_inc(nd["n_mm"].sem, 1)

            def node_gate_z(g, u, use):
                reuse(pe, nd["yb"], g)
                pe.matmul(flat(ps[u][2]), whh[:, D:2 * D], flat(xt3[u]), start=True, stop=True).then_inc(nd["z_mm"].sem, 1)

            def node_tr(g, u, use):
                pe.wait_ge(*nd["x2"](g + 1))
                reuse(pe, nd["y"], g)
                transposes(ps[u][0], bD[u]).then_inc(nd["tr"].sem, 1)

            def node_f(g, u, use):
                pe.wait_ge(*nd["xt"](g + 1))
                pe.matmul(flat(ps[u][0]), wr[:, :], flat(xt[u]), start=True, stop=True).then_inc(nd["f_mm"].sem, 1)

            def node_rows_of_gelu(g, u, use):
                pe.wait_ge(*nd["gelu"](g + 1))
                reuse(pe, nd["r_tanh"], g)
                rows_by(ps[u][1], gel[u], center[:, :]).then_inc(nd["rows_mm"].sem, 1)
                rows_by(ps[u][0], gel[u], center_gamma2[:, :]).then_inc(nd["fg_mm"].sem, 1)

            def node_tr3(g, u, use):
                pe.wait_ge(*nd["x3"](g + 1))
                pe.wait_ge(*nd["sq2"](g + 1))
                transposes(ps[u][1], bF[u]).then_inc(nd["tr3"].sem, 1)

            def node_step(at):
                at(3, node_gates)
                at(1, node_f)
                at(3, node_gate_z)
                at(1, node_rows_of_gelu)
                at(3, node_tr4)
                at(2, node_tr3)
                at(0, node_tr)

            pipeline(pe, node_step, NODE_GROUPS, 3)
            node_phase_done(pe)

            def sum_runs(k, messages, banks, ready, free):
                def stage(g, u, use):
                    pe.wait_ge(*seg[k]["S"](g + 1))
                    if isinstance(ready, list):
                        pe.wait_ge(*ready[u](16 * G * (use + 1)))
                    else:
                        pe.wait_ge(*ready(g + 1))
                    reuse(pe, seg[k]["sums"], g, SUMS[k])
                    if free:
                        reuse(pe, free, g)
                    for h, bank in enumerate(banks):
                        for j in range(G):
                            last = pe.matmul(ps[u][bank][:, j, :], messages[u][:, j, h * D:(h + 1) * D], bS[u][:, j, :],
                                             start=True, stop=True)
                    last.then_inc(seg[k]["agg"].sem, 1)
                return stage

            def radial_h0(g, u, use):
                pe.wait_ge(*pa["emb"](g + 1))
                reuse(pe, pa["h1"], g)
                pe.matmul(flat(ps[u][2])[0:H1, :], m0[:, :], emb_row[u][:, :], start=True, stop=True).then_inc(pa["h0_mm"].sem, 1)

            def radial_h1(g, u, use):
                apart(pe, *pa["h0"](g + 1))
                pe.matmul(flat(ps[u][2])[0:H1, :], m1[:, :], hid0[u][:, :], start=True, stop=True).then_inc(pa["h1_mm"].sem, 1)

            def radial_out(g, u, use):
                pe.wait_ge(*pa["h1"](g + 1))
                reuse(pe, pa["w_copied"], g)
                for j in range(G):
                    last = pe.matmul(ps[u][3][:, j, :], hid1[u][:, tile_edges(j)], m2[:, :], start=True, stop=True)
                last.then_inc(pa["w_mm"].sem, 1)

            def rows_and_bias(target, source_t, weights, bias):
                for j in range(G):
                    pe.matmul(target[:, j, :], source_t[:, j, :], weights, start=True, stop=False)
                    last = pe.matmul(target[:, j, :], ones_row[0:1, 0:P], bias, start=False, stop=True)
                return last

            def s0_h(g, u, use):
                pe.wait_ge(*seg[0]["sums"](SUMS[0] * (g + 1)))
                reuse(pe, s0["y"], g)
                rows_and_bias(ps[u][1], sums[0][u], w0_center[:, :], b0_center[0:1, :]).then_inc(s0["h_mm"].sem, 1)

            def s0_step(at):
                at(1, sum_runs(0, bA, [0], segd[0]["src_in"], None))
                at(0, radial_h0)
                at(1, s0_h)
                at(0, radial_h1)
                at(0, radial_out)

            pipeline(pe, s0_step, EDGE_GROUPS, 1)
            slots_done(pe, 0)

            def s1_tr(g, u, use):
                pe.wait_ge(*segd[1]["src_in"][u](16 * G * (use + 1)))
                reuse(pe, s1["y"], g)
                transposes(ps[u][0], bA[u]).then_inc(s1["tr"].sem, 1)

            def s1_up(g, u, use):
                pe.wait_ge(*s1["xt"](g + 1))
                reuse(pe, s1["m2"], g)
                rows_by(ps[u][1], xt[u], wup[:, :]).then_inc(s1["up"].sem, 1)

            def s1_h(g, u, use):
                pe.wait_ge(*seg[1]["sums"](SUMS[1] * (g + 1)))
                for j in range(G):
                    pe.matmul(ps[u][0][:, j, :], sums[0][u][:, j, :], wo[0][:, :], start=True, stop=False)
                    last = pe.matmul(ps[u][0][:, j, :], sums[1][u][:, j, :], wo[1][:, :], start=False, stop=True)
                last.then_inc(s1["h_mm"].sem, 1)

            def s1_step(at):
                at(1, sum_runs(1, mid, [2, 3], s1["m2"], None))
                at(0, s1_tr)
                at(0, s1_up)
                at(1, s1_h)

            pipeline(pe, s1_step, EDGE_GROUPS, 1)
            slots_done(pe, 1)

            def s2_tr(g, u, use):
                pe.wait_ge(*s2d["x_in"][u](16 * (use + 1)))
                reuse(pe, s2["xt"], g)
                transposes(ps[u][0], bC[u]).then_inc(s2["tr"].sem, 1)

            def s2_r(g, u, use):
                pe.wait_ge(*s2["xt"](g + 1))
                reuse(pe, s2["rb"], g)
                rows_and_bias(ps[u][3], xt[u], wr[:, :], rows["bl"][0:1, :]).then_inc(s2["r_mm"].sem, 1)

            def s2_l(g, u, use):
                pe.wait_ge(*seg[2]["sums"](SUMS[2] * (g + 1)))
                reuse(pe, s2["y"], g)
                rows_by(ps[u][2], sums[0][u], wl[:, :]).then_inc(s2["l_mm"].sem, 1)

            def s2_step(at):
                at(1, s2_tr)
                at(1, s2_r)
                at(1, sum_runs(2, bA, [1], segd[2]["src_in"], None))
                at(1, s2_l)

            pipeline(pe, s2_step, EDGE_GROUPS, 1)
            slots_done(pe, 2)

            def s3_trs(g, u, use):
                pe.wait_ge(*segd[3]["src_in"][u](16 * G * (use + 1)))
                reuse(pe, s3["rh"], g)
                transposes(ps[u][0], bA[u]).then_inc(s3["trs"].sem, 1)

            def s3_tr(g, u, use):
                pe.wait_ge(*s3d["xd_in"][u](16 * G * (use + 1)))
                reuse(pe, s3["r_tanh"], g)
                transposes(ps[u][1], bC[u]).then_inc(s3["tr"].sem, 1)

            def s3_h(g, u, use):
                pe.wait_ge(*s3["xt"](g + 1))
                pe.wait_ge(*s3["xt3"](g + 1))
                pe.wait_ge(*s3d["attr_in"][u](16 * (use + 1)))
                reuse(pe, s3["yt"], g)
                for j in range(G):
                    pe.matmul(ps[u][2][:, j, :], xt[u][:, j, :], w1a[:, :], start=True, stop=False)
                    pe.matmul(ps[u][2][:, j, :], xt3[u][:, j, :], w1b[:, :], start=False, stop=False)
                    last = pe.matmul(ps[u][2][:, j, :], attr[u][:, tile_edges(j)], w1c[:, :], start=False, stop=True)
                last.then_inc(s3["h_mm"].sem, 1)

            def s3_a2(g, u, use):
                pe.wait_ge(*seg[3]["sums"](SUMS[3] * (g + 1)))
                pe.wait_ge(*s3d["gs_in"][u](16 * (use + 1)))
                pe.matmul(flat(ps[u][3]), w2[:, :], flat(sums[0][u]), start=True, stop=False)
                pe.matmul(flat(ps[u][3]), b2row[:, :], gsum_row[u][:, :], start=False, stop=True).then_inc(s3["a2_mm"].sem, 1)

            def s3_gates(g, u, use):
                pe.wait_ge(*s3["a2"](g + 1))
                x, a = flat(xt3[u]), flat(bB[u])
                pe.matmul(flat(ps[u][1]), wih[:, 0:D], a, start=True, stop=False)
                pe.matmul(flat(ps[u][1]), whh[:, 0:D], x, start=False, stop=True).then_inc(s3["r_mm"].sem, 1)
                pe.matmul(flat(ps[u][0]), whh[:, 2 * D:3 * D], x, start=True, stop=True).then_inc(s3["n_mm"].sem, 1)
                pe.wait_ge(*s3["y"](g + 1))
                pe.matmul(flat(ps[u][2]), wih[:, D:2 * D], a, start=True, stop=False)
                pe.matmul(flat(ps[u][2]), whh[:, D:2 * D], x, start=False, stop=True).then_inc(s3["z_mm"].sem, 1)
                pe.matmul(flat(ps[u][3]), wih[:, 2 * D:3 * D], a, start=True, stop=True).then_inc(s3["in_mm"].sem, 1)

            def s3_tr4(g, u, use):
                pe.wait_ge(*s3["n"](g + 1))
                pe.wait_ge(*s3["yt"](g + 1))
                transposes(ps[u][3], bE2[u]).then_inc(s3["tr4"].sem, 1)

            def s3_step(at):
                at(2, s3_h)
                at(3, s3_gates)
                at(2, sum_runs(3, bE, [3], s3["relu"], s3["x"]))
                at(1, s3_trs)
                at(1, s3_tr)
                at(2, s3_a2)
                at(3, s3_tr4)

            pipeline(pe, s3_step, EDGE_GROUPS, 3)
            slots_done(pe, 3)

        @block.vector
        def _(dve):
            dve.wait_ge(*su["loaded"](16 * CONST_LOADS))
            done = [0]

            def scaled(ins):
                done[0] += 1
                ins.then_inc(su["scaled"].sem, 1)

            s_up, s_out, s3_ = MUL ** -0.5, (2 * MUL) ** -0.5 / 16.0, 3.0 ** 0.5
            scaled(dve.tensor_scalar(wup[:, :], wup[:, :], s_up, None, ALU.mult))
            scaled(dve.tensor_scalar(wo[0][0:64, :], wo[0][0:64, :], s_out, None, ALU.mult))
            scaled(dve.tensor_scalar(wo[0][64:128, :], wo[0][64:128, :], s_out * s3_, None, ALU.mult))
            scaled(dve.tensor_scalar(wo[1][0:32, :], wo[1][0:32, :], s_out * s3_, None, ALU.mult))
            scaled(dve.tensor_scalar(wo[1][32:64, :], wo[1][32:64, :], s_out, None, ALU.mult))
            scaled(dve.tensor_scalar(wo[1][64:128, :], wo[1][64:128, :], s_out, None, ALU.mult))
            scaled(dve.tensor_scalar(m1[:, :], m1[:, :], 0.5, None, ALU.mult))
            scaled(dve.tensor_scalar(m2[0:H1, :], m2[0:H1, :], 0.5, None, ALU.mult))
            scaled(dve.tensor_scalar(mb0h[:, :], mb0[:, :], 0.5, None, ALU.mult))
            scaled(dve.tensor_scalar(mb1h[:, :], mb1[:, :], 0.5, None, ALU.mult))
            scaled(dve.tensor_scalar(gate_bh[:, :], gate_b[:, :], 0.5, None, ALU.mult))
            scaled(dve.tensor_scalar(half_beta2[:, :], rows["beta2"][:, :], 0.5, None, ALU.mult))
            scaled(dve.tensor_tensor(brz[:, :], bih[:, :], bhh[:, :], ALU.add))
            scaled(dve.memset(ones_row[:, :], 1.0))
            scaled(dve.tensor_scalar(m0[:, :], m0[:, :], NB ** 0.5, None, ALU.mult))
            scaled(dve.memset(ones_part[:, :], 1.0))
            scaled(dve.memset(zeros_part[:, :], 0.0))
            scaled(dve.memset(into_row[:, :, :], 0.0))
            dve.wait_ge(*su["ident"](2))
            scaled(dve.tensor_scalar(center[:, :], ident[:, :], 1.0 / D, None, ALU.subtract))
            scaled(dve.memset(sums[0][1][:, :, :], 0.0))
            scaled(dve.memset(sums[1][1][:, :, :], 0.0))
            for u in range(U):
                scaled(dve.memset(hid1[u][H1:H1 + 1, :], 1.0))
            dve.wait_ge(*su["scaled"](done[0]))
            scaled(dve.tensor_scalar(brz[:, :], brz[:, :], 0.5, None, ALU.mult))
            scaled(dve.tensor_scalar(neg_center[:, :], center[:, :], -1.0, None, ALU.mult))
            scaled(dve.tensor_tensor(center_gamma2[:, :], center[:, :], rows["gamma2"][:, :], ALU.mult))
            assert done[0] == SCALED

            dve.bn_stats(empty_st[:, :], rows["b0"][:, :]).then_inc(su["e_stats"].sem, 1)
            dve.wait_ge(*su["e_stats"](1))
            dve.bn_aggr(empty_mv[:, :], empty_st[:, :]).then_inc(su["e_mv"].sem, 1)
            dve.wait_ge(*su["e_mv"](1))
            dve.tensor_scalar(empty_v[:, :], empty_mv[:, 1:2], LN_EPS, None, ALU.add).then_inc(su["e_add"].sem, 1)
            dve.wait_ge(*su["e_rstd"](1))
            dve.tensor_scalar(empty0[:, :], rows["b0"][:, :], empty_mv[:, 0:1], empty_r[:, 0:1],
                              ALU.subtract, ALU.mult).then_inc(su["e_norm"].sem, 1)
            dve.wait_ge(*su["e_norm"](1))
            dve.tensor_tensor(empty0[:, :], empty0[:, :], rows["gamma0"][:, :], ALU.mult).then_inc(su["e_gamma"].sem, 1)
            dve.wait_ge(*su["e_gamma"](1))
            dve.tensor_tensor(empty0[:, :], empty0[:, :], rows["beta0"][:, :], ALU.add).then_inc(su["empty"].sem, 1)

            dve.tensor_tensor(sq_vec[:, :, :], rhat[:, :, :], rhat[:, :, :], ALU.mult).then_inc(su["sq"].sem, 1)
            dve.wait_ge(*su["sq"](1))
            dve.tensor_reduce(norm[:, :], sq_vec[:, :, :], mybir.AxisListType.X, ALU.add).then_inc(su["ssum"].sem, 1)

            dve.wait_ge(*su["w0_mm"](1))
            dve.tensor_copy(w0_center[:, :], ps[0][0][:, 0, :]).then_inc(su["w0_center"].sem, 1)
            dve.tensor_copy(b0_center[:, :], ps[0][1][0:1, 0, :]).then_inc(su["w0_center"].sem, 1)

            dve.wait_ge(*su["t_dst_in"](32))
            dve.tensor_tensor(same[:, :], dst_own[:, :], dst_prev[:, :], ALU.is_equal).then_inc(su["t_same"].sem, 1)
            weights = gate_row[:, :].unsqueeze(1).broadcast_to((P, PER_CHUNK, ED))
            for c in range(CHUNKS):
                rows_in = attr_rows[c % U]
                dve.wait_ge(*su[f"t_attr_in{c % U}"](16 * (c // U + 1)))
                dve.tensor_tensor(rows_in[:, :, :], rows_in[:, :, :], weights, ALU.mult).then_inc(su["t_weighted"].sem, 1)
                dve.wait_ge(*su["t_weighted"](c + 1))
                dve.tensor_reduce(logits[:, c * PER_CHUNK:(c + 1) * PER_CHUNK], rows_in[:, :, :],
                                  mybir.AxisListType.X, ALU.add).then_inc(su["t_logit"].sem, 1)
            dve.wait_ge(*su["t_tanh"](1))
            dve.tensor_scalar(gate_part[:, :], gate_part[:, :], 0.5, 0.5, ALU.mult, ALU.add).then_inc(su["t_gate"].sem, 1)
            dve.wait_ge(*su["t_same"](1))
            dve.tensor_tensor_scan(goes_on[:, :], same[:, :], zeros_part[:, :], 1.0, ALU.mult, ALU.add).then_inc(su["t_scan"].sem, 1)
            dve.tensor_tensor_scan(run_counts[:, :], same[:, :], ones_part[:, :], 0.0, ALU.mult, ALU.add).then_inc(su["t_scan"].sem, 1)
            dve.wait_ge(*su["t_gate"](1))
            dve.tensor_tensor_scan(run_gates[:, :], same[:, :], gate_part[:, :], 0.0, ALU.mult, ALU.add).then_inc(su["t_scan"].sem, 1)
            dve.wait_ge(*su["t_scan"](3))
            last_edge = slice(PER_PART - 1, PER_PART)
            dve.tensor_copy(ends[:, 0:1], run_counts[:, last_edge])
            dve.tensor_copy(ends[:, 1:2], run_gates[:, last_edge])
            dve.tensor_copy(ends[:, 2:3], goes_on[:, last_edge]).then_inc(su["t_ends"].sem, 1)
            dve.wait_ge(*su["t_ends_mm"](1))
            dve.tensor_copy(ends_row[:, :, :], ps[0][2][0:1, 0:3, :]).then_inc(su["t_ends_row"].sem, 1)
            dve.wait_ge(*su["t_ends_row"](1))
            for n in range(2):
                dve.tensor_tensor_scan(into_row[0:1, n, 1:P + 1], ends_row[0:1, 2, :], ends_row[0:1, n, :], 0.0,
                                       ALU.mult, ALU.add).then_inc(su["t_into"].sem, 1)
            dve.wait_ge(*su["t_into_mm"](1))
            dve.tensor_copy(into[:, :], ps[0][3][:, 0, 0:2]).then_inc(su["t_into_col"].sem, 1)
            dve.wait_ge(*su["t_into_col"](1))
            dve.scalar_tensor_tensor(run_gates[:, :], goes_on[:, :], into[:, 1:2], run_gates[:, :], ALU.mult, ALU.add).then_inc(su["t_gsum"].sem, 1)
            dve.scalar_tensor_tensor(run_counts[:, :], goes_on[:, :], into[:, 0:1], run_counts[:, :], ALU.mult, ALU.add).then_inc(su["t_count"].sem, 1)
            dve.wait_ge(*su["t_count"](1))
            dve.tensor_scalar(run_counts[:, :], run_counts[:, :], 1.0, None, ALU.max).then_inc(su["t_count_max"].sem, 1)
            dve.wait_ge(*su["t_count_max"](1))
            dve.reciprocal(run_counts[:, :], run_counts[:, :]).then_inc(su["t_count_inv"].sem, 1)

            dve.wait_ge(*su["root"](1))
            dve.tensor_scalar(norm[:, :], norm[:, :], 1e-12, None, ALU.add).then_inc(su["root_eps"].sem, 1)
            dve.wait_ge(*su["root_eps"](1))
            dve.reciprocal(norm[:, :], norm[:, :]).then_inc(su["rinv"].sem, 1)
            dve.wait_ge(*su["rinv"](1))
            dve.tensor_tensor(rhat[:, :, :], rhat[:, :, :], norm[:, :].unsqueeze(2).broadcast_to((P, NT, 3)),
                              ALU.mult).then_inc(su["rhat"].sem, 1)

            dve.wait_ge(*su["t_tiles_mm"](1))
            for n, by_column in enumerate((gates, count_inv)):
                dve.tensor_copy(by_column[:, :].rearrange("p (h t) -> p h t", h=2),
                                ps[1][n][:, 0:2, 0:HALF_TILES]).then_inc(su["t_columns"].sem, 1)
            dve.wait_ge(*su["t_columns"](2))

            def statistics(n, source, s, m, ready):
                def stage(g, u, use):
                    dve.wait_ge(*ready(g + 1))
                    for j in range(G):
                        last = dve.bn_stats(stats[n][u][:, j, :], source[u][:, j, :])
                    last.then_inc(s[f"st{m}"].sem, 1)
                return stage

            def aggregate(n, s, m):
                def stage(g, u, use):
                    apart(dve, *s[f"st{m}"](g + 1))
                    for j in range(G):
                        last = dve.bn_aggr(mv[n][u][:, j, :], stats[n][u][:, j, :])
                    last.then_inc(s[f"mv{m}"].sem, 1)
                return stage

            def sum_of_squares(n, squares, s, m, ready):
                def stage(g, u, use):
                    dve.wait_ge(*ready(g + 1))
                    dve.tensor_reduce(mv[n][u][:, :, 1], squares[u][:, :, :], mybir.AxisListType.X, ALU.add).then_inc(s[f"mv{m}"].sem, 1)
                return stage

            def moments(n, source, s, m, ready):
                def stage(g, u, use):
                    statistics(n, source, s, m, ready)(g, u, use)
                    aggregate(n, s, m)(g, u, use)
                return stage

            def normalize(n, u, target, source):
                for j in range(G):
                    last = dve.tensor_scalar(target[:, j, :], source[:, j, :], mv[n][u][:, j, 0:1], rstd[n][u][:, 0, j:j + 1],
                                             ALU.subtract, ALU.mult)
                return last

            def scale_row(n, u, bank_, row):
                for j in range(G):
                    last = dve.scalar_tensor_tensor(bank_[:, j, :], bank_[:, j, :], mv[n][u][:, j, 0:1], row[:, :],
                                                    ALU.subtract, ALU.mult)
                return last

            def scale_add(n, u, target, source, other):
                for j in range(G):
                    last = dve.scalar_tensor_tensor(target[:, j, :], source[:, j, :], rstd[n][u][:, 0, j:j + 1], other(j),
                                                    ALU.mult, ALU.add)
                return last

            bank = lambda k: [ps[u][k] for u in range(U)]

            tables_done(dve)

            def node_x1(g, u, use):
                dve.wait_ge(*nd["rs1"](g + 1))
                reuse(dve, nd["x2"], g)
                dve.tensor_tensor(root[u][:, :], vv[0][u][:, 0, :], rstd[0][u][:, 0, :], ALU.mult).then_inc(nd["v_rstd"].sem, 1)
                reuse_dma(dve, ndd["x1_st"], u, use)
                normalize(0, u, bC[u], bB[u]).then_inc(nd["x1"].sem, 1)
                dve.wait_ge(*nd["v_rstd"](g + 1))
                dve.tensor_tensor(ratio[u][:, :], root[u][:, :], rstd[0][u][:, 1, :], ALU.mult).then_inc(nd["ratio"].sem, 1)

            def node_y(g, u, use):
                dve.wait_ge(*nd["rs2"](g + 1))
                dve.wait_ge(*nd["fg_mm"](g + 1))
                dve.wait_ge(*nd["xb"](g + 1))
                scale_add(1, u, bA2[u], ps[u][0], lambda j: bE[u][:, j, :]).then_inc(nd["y"].sem, 1)

            def node_rh(g, u, use):
                dve.wait_ge(*nd["r_tanh"](g + 1))
                dve.wait_ge(*nd["hn"](g + 1))
                dve.scalar_tensor_tensor(flat(ps[u][3]), flat(gr[u]), 1.0, flat(ps[u][3]), ALU.add, ALU.mult).then_inc(nd["rh"].sem, 1)

            def node_ya(g, u, use):
                dve.wait_ge(*nd["z_tanh"](g + 1))
                dve.wait_ge(*nd["xt3"](g + 1))
                reuse(dve, nd["tr4"], g)
                dve.scalar_tensor_tensor(flat(bG[u]), flat(ps[u][2]), 3.0, flat(xt3[u]), ALU.add, ALU.mult).then_inc(nd["ya"].sem, 1)

            def node_x3(g, u, use):
                dve.wait_ge(*nd["rs3"](g + 1))
                reuse_dma(dve, ndd["x3_st"], u, use)
                reuse(dve, nd["tr3"], g)
                normalize(2, u, bF[u], bA2[u]).then_inc(nd["x3"].sem, 1)

            def node_yb(g, u, use):
                dve.wait_ge(*nd["n"](g + 1))
                reuse(dve, nd["tr4"], g)
                dve.scalar_tensor_tensor(flat(bE2[u]), flat(ps[u][2]), -1.0, flat(gn[u]), ALU.add, ALU.mult).then_inc(nd["yb"].sem, 1)

            def node_step(at):
                at(0, statistics(0, bB, nd, 1, nd["y0"]))
                at(2, node_y)
                at(0, aggregate(0, nd, 1))
                at(2, statistics(2, bA2, nd, 3, nd["y"]))
                at(2, aggregate(2, nd, 3))
                at(4, sum_of_squares(3, square4, nd, 4, nd["sq4"]))
                at(3, node_rh)
                at(0, node_x1)
                at(3, node_ya)
                at(3, node_yb)
                at(1, sum_of_squares(1, square2, nd, 2, nd["sq2"]))
                at(2, node_x3)

            pipeline(dve, node_step, NODE_GROUPS, 4)
            node_phase_done(dve)

            def select(k, gated=False):
                s, d = seg[k], segd[k]

                def stage(g, u, use):
                    dve.wait_ge(*d["cols_in"][u](16 * (use + 1)))
                    reuse(dve, s["scat"], g)
                    dve.tensor_copy(dst_col[u][:, :], cols[u][:, 0:G]).then_inc(s["dcol"].sem, 1)
                    dve.tensor_tensor(is_mid[u][:, :], cols[u][:, 0:G], cols[u][:, G:2 * G], ALU.is_equal).then_inc(s["mid"].sem, 1)
                    dve.wait_ge(*d["dst_in"][u](16 * (use + 1)))
                    dve.tensor_copy(dst_before[u][:, :], dst_row[u][:, 0:GP:P]).then_inc(s["dbefore"].sem, 1)
                    if gated:
                        dve.tensor_copy(gate_t[u][:, :], gates[:, tiles_of(g)]).then_inc(s3["gcol"].sem, 1)
                    dve.wait_ge(*s["dcol"](g + 1))
                    if gated:
                        dve.wait_ge(*s3["gcol"](g + 1))
                    reuse(dve, s["agg"], g)
                    for j in range(G):
                        last = dve.tensor_scalar(bS[u][:, j, :], dst_row[u][:, 1 + j * P:1 + (j + 1) * P], dst_col[u][:, j:j + 1],
                                                 gate_t[u][:, j:j + 1] if gated else None,
                                                 ALU.is_equal, *([ALU.mult] if gated else []))
                    last.then_inc(s["S"].sem, 1)
                    dve.wait_ge(*s["dbefore"](g + 1))
                    reuse(dve, s["sums"], g, SUMS[k])
                    for j in range(G):
                        last = dve.tensor_scalar(mask[u][:, j, :], dst_row[u][:, 1 + j * P:1 + (j + 1) * P],
                                                 dst_before[u][:, j:j + 1], None, ALU.is_equal)
                    last.then_inc(s["mask"].sem, 1)
                return stage

            def rows_to_write(k):
                def stage(g, u, use):
                    dve.wait_ge(*seg[k]["mid"](g + 1))
                    dve.wait_ge(*seg[k]["dcol"](g + 1))
                    reuse_dma(dve, segd[k]["scattered"], u, use, 16 * G)
                    dve.scalar_tensor_tensor(scat[u][:, :], is_mid[u][:, :], float(SKIP), dst_col[u][:, :],
                                             ALU.mult, ALU.add).then_inc(seg[k]["scat"].sem, 1)
                return stage

            def carry(k, banks, used):
                s = seg[k]
                n = len(banks)

                def stage(g, u, use):
                    dve.wait_ge(*s["agg"](g + 1))
                    dve.wait_ge(*s["mask"](g + 1))
                    reuse(dve, used, g)
                    for j in range(G):
                        for h, b in enumerate(banks):
                            if not (isinstance(g, int) and g == 0 and j == 0):
                                dve.wait_ge(*s["sums"](n * (G * g + j - 1) + h + 1))
                            before = sums[h][u][:, j - 1, P - 1:P] if j else sums[h][1 - u][:, G - 1, P - 1:P]
                            dve.scalar_tensor_tensor(sums[h][u][:, j, :], mask[u][:, j, :], before, ps[u][b][:, j, :],
                                                     ALU.mult, ALU.add).then_inc(s["sums"].sem, 1)
                return stage

            def s0_xb(g, u, use):
                dve.wait_ge(*s0d["xd_in"][u](16 * G * (use + 1)))
                reuse(dve, s0["y"], g)
                dve.tensor_tensor(bD[u][:, :, :], bC[u][:, :, :], over_tiles(rows["beta0"]), ALU.add).then_inc(s0["xb"].sem, 1)

            def s0_fg(g, u, use):
                dve.wait_ge(*s0["h_mm"](g + 1))
                dve.wait_ge(*s0["sq2"](g + 1))
                dve.tensor_tensor(ps[u][1][:, :, :], ps[u][1][:, :, :], over_tiles(rows["gamma0"]), ALU.mult).then_inc(s0["fg"].sem, 1)

            def radial_clip(g, u, use):
                dve.wait_ge(*pad["r_in"][u](16 * (use + 1)))
                reuse(dve, pa["squared"], g)
                dve.tensor_scalar(e_row[u][:, :], r_row[u][:, :], 0.0, 1.0, ALU.max, ALU.min).then_inc(pa["clipped"].sem, 1)

            def radial_emb(g, u, use):
                dve.wait_ge(*pa["exped"](g + 1))
                reuse(dve, pa["h0_mm"], g)
                dve.scalar_tensor_tensor(emb_row[u][:, :], r_row[u][:, :], R_MAX, exp_row[u][:, :],
                                         ALU.is_le, ALU.mult).then_inc(pa["emb"].sem, 1)

            def radial_hidden(n, target, free):
                def stage(g, u, use):
                    dve.wait_ge(*pa[f"h{n}_tanh"](g + 1))
                    dve.wait_ge(*pa[f"h{n}_lin"](g + 1))
                    reuse(dve, pa[free], g)
                    dve.scalar_tensor_tensor(target[u][0:H1, :], hid_t[u][:, :], 1.0, flat(ps[u][2])[0:H1, :],
                                             ALU.add, ALU.mult).then_inc(pa[f"h{n}"].sem, 1)
                return stage

            def scaled_by(row, bank_, s):
                def stage(g, u, use):
                    dve.wait_ge(*s["mv1"](g + 1))
                    scale_row(0, u, ps[u][bank_], row).then_inc(s["fg"].sem, 1)
                return stage

            def residual(s, bank_):
                def stage(g, u, use):
                    dve.wait_ge(*s["rs1"](g + 1))
                    dve.wait_ge(*s["fg"](g + 1))
                    dve.wait_ge(*s["xb"](g + 1))
                    reuse(dve, s["x"], g)
                    scale_add(0, u, bA2[u], ps[u][bank_], lambda j: bD[u][:, j, :]).then_inc(s["y"].sem, 1)
                return stage

            def shift(n, s, m):
                def stage(g, u, use):
                    dve.wait_ge(*s[f"rs{m}"](g + 1))
                    reuse(dve, s["x"], g)
                    dve.scalar_tensor_tensor(shifts[u][:, :], mv[n][u][:, :, 0], -1.0, rstd[n][u][:, 0, :],
                                             ALU.mult, ALU.mult).then_inc(s["shift"].sem, 1)
                return stage

            def s0_step(at):
                at(1, select(0))
                at(0, radial_clip)
                at(2, residual(s0, 1))
                at(2, statistics(1, bA2, s0, 2, s0["y"]))
                at(0, radial_emb)
                at(2, aggregate(1, s0, 2))
                at(1, carry(0, [0], s0["h_mm"]))
                at(1, s0_xb)
                at(2, rows_to_write(0))
                at(2, shift(1, s0, 2))
                at(0, radial_hidden(0, hid0, "h1_mm"))
                at(1, sum_of_squares(0, square2, s0, 1, s0["sq2"]))
                at(1, s0_fg)
                at(0, radial_hidden(1, hid1, "w_mm"))

            pipeline(dve, s0_step, EDGE_GROUPS, 2)
            slots_done(dve, 0)

            def by_four(t, lo, n):
                return t[:, :, lo:lo + n * MUL].rearrange("p j (q m) -> p j q m", m=MUL)

            def s1_messages(g, u, use):
                dve.tensor_copy(rh[u][:, :, :], rhat[:, tiles_of(g), :]).then_inc(s1["rh"].sem, 1)
                wv, up, md = bB[u], ps[u][1], mid[u]
                unit = rh[u][:, :, :].unsqueeze(3).broadcast_to((P, G, 3, MUL))
                dve.wait_ge(*s1["up"](g + 1))
                dve.wait_ge(*s1d["w_in"][u](16 * (use + 1)))
                reuse(dve, seg[1]["agg"], g)
                dve.tensor_tensor(by_four(md, 0, 2), by_four(wv, 0, 2), by_four(up, 0, 1).broadcast_to((P, G, 2, MUL)),
                                  ALU.mult).then_inc(s1["m0b"].sem, 1)
                dve.wait_ge(*s1["rh"](g + 1))
                dve.tensor_tensor(vr[u][:, :, :, :], by_four(up, MUL, 3), unit, ALU.mult).then_inc(s1["vr"].sem, 1)
                dve.wait_ge(*s1["m0b"](g + 1))
                dve.tensor_tensor(by_four(md, 2 * MUL, 3), by_four(md, MUL, 1).broadcast_to((P, G, 3, MUL)), unit,
                                  ALU.mult).then_inc(s1["m1"].sem, 1)
                dve.wait_ge(*s1["vr"](g + 1))
                dve.tensor_tensor(rq[u][:, :, :], vr[u][:, :, 0, :], vr[u][:, :, 1, :], ALU.add).then_inc(s1["vr01"].sem, 1)
                dve.tensor_tensor(by_four(md, 5 * MUL, 3), by_four(wv, 2 * MUL, 1).broadcast_to((P, G, 3, MUL)),
                                  by_four(up, MUL, 3), ALU.mult)
                dve.wait_ge(*s1["vr01"](g + 1))
                dve.tensor_tensor(rq[u][:, :, :], rq[u][:, :, :], vr[u][:, :, 2, :], ALU.add).then_inc(s1["vr012"].sem, 1)
                dve.wait_ge(*s1["vr012"](g + 1))
                dve.wait_ge(*s1["m1"](g + 1))
                dve.tensor_tensor(md[:, :, MUL:2 * MUL], wv[:, :, 3 * MUL:4 * MUL], rq[u][:, :, :], ALU.mult).then_inc(s1["m2"].sem, 1)

            def s1_y(g, u, use):
                dve.wait_ge(*s1["h_mm"](g + 1))
                dve.wait_ge(*s1d["x_in"][u](16 * (use + 1)))
                reuse(dve, s1["x"], g)
                dve.tensor_tensor(bA2[u][:, :, :], ps[u][0][:, :, :], bC[u][:, :, :], ALU.add).then_inc(s1["y"].sem, 1)

            def s1_step(at):
                at(1, select(1))
                at(1, s1_messages)
                at(2, s1_y)
                at(2, statistics(0, bA2, s1, 1, s1["y"]))
                at(3, shift(0, s1, 1))
                at(2, aggregate(0, s1, 1))
                at(2, rows_to_write(1))
                at(1, carry(1, [2, 3], s1["h_mm"]))

            pipeline(dve, s1_step, EDGE_GROUPS, 3)
            slots_done(dve, 1)

            def s2_xb(g, u, use):
                dve.wait_ge(*s2d["x_in"][u](16 * (use + 1)))
                reuse(dve, s2["y"], g)
                dve.tensor_tensor(bD[u][:, :, :], bC[u][:, :, :], over_tiles(half_beta2), ALU.add).then_inc(s2["xb"].sem, 1)
                dve.tensor_copy(cinv[u][:, :], count_inv[:, tiles_of(g)]).then_inc(s2["cinv"].sem, 1)

            def s2_f(g, u, use):
                dve.wait_ge(*s2["l_mm"](g + 1))
                dve.wait_ge(*s2["rb"](g + 1))
                dve.wait_ge(*s2["cinv"](g + 1))
                for j in range(G):
                    last = dve.scalar_tensor_tensor(ps[u][2][:, j, :], ps[u][2][:, j, :], cinv[u][:, j:j + 1], bE[u][:, j, :],
                                                    ALU.mult, ALU.add)
                last.then_inc(s2["f"].sem, 1)

            def s2_step(at):
                at(2, s2_xb)
                at(2, s2_f)
                at(3, shift(1, s2, 2))
                at(1, select(2))
                at(2, moments(0, bank(2), s2, 1, s2["gelu"]))
                at(2, scaled_by(rows["gamma2"], 2, s2))
                at(1, carry(2, [1], s2["l_mm"]))
                at(2, residual(s2, 2))
                at(2, moments(1, bA2, s2, 2, s2["y"]))
                at(2, rows_to_write(2))

            pipeline(dve, s2_step, EDGE_GROUPS, 3)
            slots_done(dve, 2)

            def s3_y(g, u, use):
                dve.wait_ge(*s3["rs1"](g + 1))
                dve.wait_ge(*s3["fg"](g + 1))
                reuse(dve, seg[3]["agg"], g)
                scale_add(0, u, bE[u], ps[u][2], lambda j: rows["ln_b3"][:, :]).then_inc(s3["y"].sem, 1)

            def s3_rh(g, u, use):
                dve.wait_ge(*s3["r_tanh"](g + 1))
                dve.wait_ge(*s3["hn"](g + 1))
                dve.scalar_tensor_tensor(flat(bG[u]), flat(gr[u]), 1.0, flat(ps[u][0]), ALU.add, ALU.mult).then_inc(s3["rh"].sem, 1)

            def s3_ya(g, u, use):
                dve.wait_ge(*s3["z_tanh"](g + 1))
                dve.scalar_tensor_tensor(flat(bD[u]), flat(ps[u][2]), 3.0, flat(xt3[u]), ALU.add, ALU.mult).then_inc(s3["ya"].sem, 1)

            def s3_ni(g, u, use):
                dve.wait_ge(*s3["rh"](g + 1))
                dve.wait_ge(*s3["in_mm"](g + 1))
                dve.scalar_tensor_tensor(flat(ps[u][3]), flat(bG[u]), 0.5, flat(ps[u][3]), ALU.mult, ALU.add).then_inc(s3["ni"].sem, 1)

            def s3_yb(g, u, use):
                dve.wait_ge(*s3["n"](g + 1))
                dve.scalar_tensor_tensor(flat(ps[u][2]), flat(ps[u][2]), -1.0, flat(gn[u]), ALU.add, ALU.mult).then_inc(s3["yb"].sem, 1)

            def s3_yt(g, u, use):
                dve.wait_ge(*s3["ya"](g + 1))
                dve.wait_ge(*s3["yb"](g + 1))
                reuse(dve, s3["tr4"], g)
                dve.tensor_tensor(flat(bE2[u]), flat(bD[u]), flat(ps[u][2]), ALU.subtract).then_inc(s3["yt"].sem, 1)

            def s3_step(at):
                at(2, select(3, gated=True))
                at(4, moments(1, bank(3), s3, 2, s3["tr4"]))
                at(2, moments(0, bank(2), s3, 1, s3["h_mm"]))
                at(2, scaled_by(rows["ln_g3"], 2, s3))
                at(4, shift(1, s3, 2))
                at(3, s3_rh)
                at(2, s3_y)
                at(3, s3_ya)
                at(3, s3_ni)
                at(2, carry(3, [3], s3["a2_mm"]))
                at(3, s3_yb)
                at(3, s3_yt)
                at(3, rows_to_write(3))

            pipeline(dve, s3_step, EDGE_GROUPS, 4)
            slots_done(dve, 3)


def kernel(**inputs):
    import numpy as np
    import concourse.bacc as bacc
    from concourse.bass_utils import run_bass_kernel_spmd

    v = {k: np.asarray(a) for k, a in inputs.items()}

    def row(a):
        return np.ascontiguousarray(a.reshape(1, -1))

    def t(a):
        return np.ascontiguousarray(a.T)

    def padded(a, n, fill=0):
        out = np.full((n,) + a.shape[1:], fill, a.dtype)
        out[:a.shape[0]] = a
        return out

    tiles = EDGE_GROUPS * G
    src = padded(v["src"], EDGES_PAD)
    dst = padded(v["dst"], EDGES_PAD, LAST_ROW)
    after = np.concatenate([dst[1:], np.full(1, -1, dst.dtype)])

    def columns(a):
        return a.reshape(EDGE_GROUPS, G, P).transpose(0, 2, 1)

    wup = np.zeros((D, D), np.float32)
    wup[:MUL, :MUL] = v["L1_gnn_W_up0"]
    wo = np.zeros((2 * D, D), np.float32)
    wo[0:2 * MUL, :MUL] = v["L1_gnn_W_out0"]
    for c in range(3):
        wup[MUL + c::3, MUL + MUL * c:MUL + MUL * (c + 1)] = v["L1_gnn_W_up1"]
        wo[MUL * (2 + c):MUL * (3 + c), MUL + c::3] = v["L1_gnn_W_out1"][:MUL]
        wo[MUL * (5 + c):MUL * (6 + c), MUL + c::3] = v["L1_gnn_W_out1"][MUL:]
    attr = padded(v["edge_attr_64"], EDGES_PAD).T
    w1 = v["L3_gnn_W1"]
    arrays = {
        "x": padded(v["x"], NODES_PAD),
        "edge_idx": np.ascontiguousarray(np.concatenate([columns(src), columns(dst)], axis=2)),
        "edge_cols": np.ascontiguousarray(np.concatenate([columns(dst), columns(after)], axis=2)),
        "dst_line": row(np.concatenate([np.full(1, -1, dst.dtype), dst])),
        "edge_vec": np.ascontiguousarray(padded(v["edge_attr_3"], EDGES_PAD).reshape(tiles, P, 3).transpose(1, 0, 2)).reshape(P, tiles * 3),
        "edge_r": row(padded(v["edge_weight"], EDGES_PAD)),
        "attr": padded(v["edge_attr_64"], EDGES_PAD),
        "attr_t": np.concatenate([attr, np.ones((1, EDGES_PAD), np.float32)]),
        "b0": row(v["L0_gnn_b"]), "gamma0": row(v["L0_gnn_gamma"]), "beta0": row(v["L0_gnn_beta"]), "w0": v["L0_gnn_W"], "b0_col": v["L0_gnn_b"].reshape(-1, 1),
        "wup": wup, "wo": wo, "m0": v["L1_gnn_mlp_w0"], "m1": v["L1_gnn_mlp_w1"],
        "m2": np.concatenate([v["L1_gnn_mlp_w2"], row(v["L1_gnn_mlp_b2"])]),
        "mb0": v["L1_gnn_mlp_b0"].reshape(-1, 1), "mb1": v["L1_gnn_mlp_b1"].reshape(-1, 1),
        "wl": v["L2_gnn_W_l"], "bl": row(v["L2_gnn_b_l"]), "wr": v["L2_gnn_W_r"], "bl_col": v["L2_gnn_b_l"].reshape(-1, 1),
        "gamma2": row(v["L2_gnn_gamma"]), "beta2": row(v["L2_gnn_beta"]),
        "w1ab": w1[:2 * D], "w1c": np.concatenate([w1[2 * D:], row(v["L3_gnn_b1"])]),
        "ln_g3": row(v["L3_gnn_ln_g"]), "ln_b3": row(v["L3_gnn_ln_b"]), "w2": v["L3_gnn_W2"], "b2row": row(v["L3_gnn_b2"]),
        "gate_w": row(v["L3_gnn_gate_w"]), "gate_b": v["L3_gnn_gate_b"].reshape(1, 1),
        "wih": t(v["L3_gnn_W_ih"]), "whh": t(v["L3_gnn_W_hh"]),
        "bih": t(v["L3_gnn_b_ih"].reshape(3, D)), "bhh": t(v["L3_gnn_b_hh"].reshape(3, D)),
    }
    nc = bacc.Bacc("TRN2", target_bir_lowering=False, num_devices=1)
    feeds, aps = {}, {}
    for name, a in arrays.items():
        a = np.ascontiguousarray(a)
        feeds[f"in_{name}"] = a
        aps[name] = nc.dram_tensor(f"in_{name}", a.shape, mybir.dt.from_np(a.dtype), kind="ExternalInput").ap()
    out = nc.dram_tensor("out_0", (NODES_PAD, D), F32, kind="ExternalOutput").ap()
    build(nc, aps, out)
    r = run_bass_kernel_spmd(nc, [feeds], core_ids=[0])
    return r.results[0]["out_0"][:N_NODES]
```
